# Optimizing a Trainium2 kernel written in Bass

```python
import numpy as np
import jax
import jax.numpy as jnp

def _softmax(x, axis=-1):
    return jax.nn.softmax(x, axis=axis)

def _gelu(x):
    return jax.nn.gelu(x, approximate=True)

def _silu(x):
    return jax.nn.silu(x)

def _sigmoid(x):
    return jax.nn.sigmoid(x)

def _layernorm(x, axis=-1, eps=1e-05):
    m = jnp.mean(x, axis=axis, keepdims=True)
    v = jnp.var(x, axis=axis, keepdims=True)
    return (x - m) / jnp.sqrt(v + eps)

def _scatter_add(tgt, idx, src, axis=0):
    return tgt.at[idx].add(src)

def _segment_sum(src, seg, n):
    return jax.ops.segment_sum(src, seg, n)
kernel_name = 'mk_gnn_preln_d4_gnn_r8_f17e12'

def setup_inputs(seed: int=0):
    np.random.seed(seed)
    _w = jnp.asarray

    def _rec_inputs():
        import jax
        import jax.numpy as jnp
        _gk = jax.random.key(seed)
        x = -0.001003 + 1 * jax.random.normal(jax.random.fold_in(_gk, 1), (256, 768), jnp.float32)
        _s = jax.random.randint(jax.random.fold_in(_gk, 2), (2048,), 0, 256, jnp.int32)
        _d = jax.random.randint(jax.random.fold_in(_gk, 3), (2048,), 0, 256, jnp.int32)
        _loop = jnp.arange(256, dtype=jnp.int32)
        src = jnp.concatenate([_s, _d, _loop])
        dst = jnp.concatenate([_d, _s, _loop])
        _o = jnp.argsort(dst, stable=True)
        src = src[_o]
        dst = dst[_o]
        edge_type_3 = jax.random.randint(jax.random.fold_in(_gk, 12), (4352,), 0, 3, jnp.int32)
        edge_type_4 = jax.random.randint(jax.random.fold_in(_gk, 13), (4352,), 0, 4, jnp.int32)
        return (x, src, dst, edge_type_3, edge_type_4)
    x, src, dst, edge_type_3, edge_type_4 = _rec_inputs()

    def _L0_gnn_setup():
        import jax, jax.numpy as jnp
        import numpy as np
        NUM_RELATIONS = 3

        def _rgcn(x, W_rel, W_root, bias, src, dst, etype):
            n = x.shape[0]
            xr = jnp.einsum('ni,rio->rno', x, W_rel)
            msg = xr[etype, src]
            out = x @ W_root + bias
            for r in range(NUM_RELATIONS):
                m = etype == r
                s = jax.ops.segment_sum(jnp.where(m[:, None], msg, 0.0), dst, num_segments=n)
                c = jax.ops.segment_sum(m.astype(x.dtype), dst, num_segments=n)
                out = out + s / jnp.maximum(c, 1.0)[:, None]
            return out

        def _gate(h, q, Wg, bg, Wq, bq):
            B, L, F = q.shape
            N = h.shape[0] // B
            h3 = h.reshape(B, N, F)
            hg = jnp.einsum('bnf,gf->bng', h3, Wg[:, :F])
            qg = jnp.einsum('blf,gf->blg', q, Wg[:, F:]) + bg
            attn = jax.nn.sigmoid(hg[:, :, None, :] + qg[:, None, :, :])
            qi = jnp.einsum('bnlf,blf->bnf', attn, q)
            alpha = jax.nn.sigmoid(jnp.einsum('bnf,gf->bng', h3, Wq[:, :F]) + jnp.einsum('bnf,gf->bng', qi, Wq[:, F:]) + bq)
            hn = alpha * jnp.tanh(qi) + (1.0 - alpha) * h3
            return hn.reshape(B * N, F)
        key = jax.random.key(seed)
        ks = jax.random.split(key, 16)
        F = 768
        BN, E, B, L = (256, 8192, 8, 64)
        s = 0.02
        return {'x': jax.random.normal(ks[0], (BN, F), jnp.float32), 'edge_index': jax.random.randint(ks[1], (2, E), 0, BN), 'edge_type': jax.random.randint(ks[2], (E,), 0, NUM_RELATIONS), 'query_embs': jax.random.normal(ks[3], (B, L, F), jnp.float32), 'W_rel1': jax.random.normal(ks[4], (NUM_RELATIONS, F, F), jnp.float32) * s, 'W_root1': jax.random.normal(ks[5], (F, F), jnp.float32) * s, 'b1': jnp.zeros((F,), jnp.float32), 'W_rel2': jax.random.normal(ks[6], (NUM_RELATIONS, F, F), jnp.float32) * s, 'W_root2': jax.random.normal(ks[7], (F, F), jnp.float32) * s, 'b2': jnp.zeros((F,), jnp.float32), 'Wg': jax.random.normal(ks[8], (F, 2 * F), jnp.float32) * s, 'bg': jnp.zeros((F,), jnp.float32), 'Wq': jax.random.normal(ks[9], (F, 2 * F), jnp.float32) * s, 'bq': jnp.zeros((F,), jnp.float32)}
    _L0_gnn_all = _L0_gnn_setup()
    _L0_gnn_in = {k: v for k, v in _L0_gnn_all.items() if k in ('query_embs', 'W_rel1', 'W_root1', 'b1', 'W_rel2', 'W_root2', 'b2', 'Wg', 'bg', 'Wq', 'bq')}
    del _L0_gnn_all

    def _L1_gnn_setup():
        import jax, jax.numpy as jnp
        import numpy as np
        N_NODES = 2500
        N_EDGES = 12500
        D = 768
        NUM_REL = 4

        def _rgcn_conv(x, weight, root, bias, src, dst, etype):
            n = x.shape[0]
            out = x @ root + bias
            for r in range(NUM_REL):
                sel = etype == r
                self_f = sel.astype(x.dtype)
                deg = jnp.zeros((n,), x.dtype).at[dst].add(self_f)
                norm = jnp.where(sel, 1.0 / jnp.maximum(deg[dst], 1.0), 0.0)
                h_r = x @ weight[r]
                msgs = h_r[src] * norm[:, None]
                out = out + jax.ops.segment_sum(msgs, dst, num_segments=n)
            return out
        key = jax.random.key(seed)
        ks = jax.random.split(key, 12)
        entity = jax.random.normal(ks[0], (N_NODES, D), dtype=jnp.float32)
        edge_index = jax.random.randint(ks[1], (2, N_EDGES), 0, N_NODES, dtype=jnp.int64)
        edge_type = jax.random.randint(ks[2], (N_EDGES,), 0, NUM_REL, dtype=jnp.int64)
        s = 0.02
        params = {}
        for i, layer in enumerate(['1', '2', '3']):
            params[f'W{layer}'] = jax.random.normal(ks[3 + 3 * i], (NUM_REL, D, D), dtype=jnp.float32) * s
            params[f'root{layer}'] = jax.random.normal(ks[4 + 3 * i], (D, D), dtype=jnp.float32) * s
            params[f'b{layer}'] = jnp.zeros((D,), dtype=jnp.float32)
        return {'entity': entity, 'edge_index': edge_index, 'edge_type': edge_type, **params}
    _L1_gnn_all = _L1_gnn_setup()
    _L1_gnn_in = {k: v for k, v in _L1_gnn_all.items() if k in ('W1', 'root1', 'b1', 'W2', 'root2', 'b2', 'W3', 'root3', 'b3')}
    del _L1_gnn_all

    def _L2_gnn_setup():
        import jax, jax.numpy as jnp
        import numpy as np
        N = 6250
        E = 200000
        IN_DIM = 768
        HID = 256
        OUT_DIM = 768
        HEADS = 4
        NEG_SLOPE = 0.2

        def gat_conv(x, src, dst, W, a_src, a_dst, bias, heads):
            n = x.shape[0]
            h = (x @ W).reshape(n, heads, -1)
            alpha_s = (h * a_src[None]).sum(-1)
            alpha_d = (h * a_dst[None]).sum(-1)
            e = jax.nn.leaky_relu(alpha_s[src] + alpha_d[dst], NEG_SLOPE)
            m = jax.ops.segment_max(e, dst, num_segments=n)
            e = jnp.exp(e - m[dst])
            denom = jax.ops.segment_sum(e, dst, num_segments=n)
            alpha = e / (denom[dst] + 1e-16)
            out = jax.ops.segment_sum(h[src] * alpha[:, :, None], dst, num_segments=n)
            return out.reshape(n, -1) + bias
        key = jax.random.key(seed)
        ks = jax.random.split(key, 12)
        C1 = HID // HEADS
        x = jax.random.normal(ks[0], (N, IN_DIM), dtype=jnp.float32)
        edge_index = jax.random.randint(ks[1], (2, E), 0, N, dtype=jnp.int64)
        sc = lambda f: 1.0 / np.sqrt(f)
        W1 = jax.random.normal(ks[2], (IN_DIM, HEADS * C1), jnp.float32) * sc(IN_DIM)
        a_src1 = jax.random.normal(ks[3], (HEADS, C1), jnp.float32) * sc(C1)
        a_dst1 = jax.random.normal(ks[4], (HEADS, C1), jnp.float32) * sc(C1)
        b1 = jnp.zeros((HEADS * C1,), jnp.float32)
        W2 = jax.random.normal(ks[5], (HID, HID), jnp.float32) * sc(HID)
        a_src2 = jax.random.normal(ks[6], (1, HID), jnp.float32) * sc(HID)
        a_dst2 = jax.random.normal(ks[7], (1, HID), jnp.float32) * sc(HID)
        b2 = jnp.zeros((HID,), jnp.float32)
        Wm1 = jax.random.normal(ks[8], (HID, HID), jnp.float32) * sc(HID)
        bm1 = jnp.zeros((HID,), jnp.float32)
        Wm2 = jax.random.normal(ks[9], (HID, OUT_DIM), jnp.float32) * sc(HID)
        bm2 = jnp.zeros((OUT_DIM,), jnp.float32)
        return {'x': x, 'edge_index': edge_index, 'W1': W1, 'a_src1': a_src1, 'a_dst1': a_dst1, 'b1': b1, 'W2': W2, 'a_src2': a_src2, 'a_dst2': a_dst2, 'b2': b2, 'Wm1': Wm1, 'bm1': bm1, 'Wm2': Wm2, 'bm2': bm2}
    _L2_gnn_all = _L2_gnn_setup()
    _L2_gnn_in = {k: v for k, v in _L2_gnn_all.items() if k in ('W1', 'a_src1', 'a_dst1', 'b1', 'W2', 'a_src2', 'a_dst2', 'b2', 'Wm1', 'bm1', 'Wm2', 'bm2')}
    del _L2_gnn_all

    def _L3_gnn_setup():
        import jax, jax.numpy as jnp
        import numpy as np
        N = 2500
        E_RAND = 40000
        NEG_SLOPE = 0.2

        def gat_layer(x, W, a_src, a_dst, bias, src, dst, heads, out_c, concat):
            n = x.shape[0]
            h = (x @ W).reshape(n, heads, out_c)
            al_s = jnp.einsum('nhc,hc->nh', h, a_src)
            al_d = jnp.einsum('nhc,hc->nh', h, a_dst)
            e = jax.nn.leaky_relu(al_s[src] + al_d[dst], NEG_SLOPE)
            m = jax.ops.segment_max(e, dst, num_segments=n)
            ex = jnp.exp(e - m[dst])
            z = jax.ops.segment_sum(ex, dst, num_segments=n)
            alpha = ex / (z[dst] + 1e-16)
            msg = h[src] * alpha[:, :, None]
            out = jax.ops.segment_sum(msg, dst, num_segments=n)
            out = out.reshape(n, heads * out_c) if concat else out.mean(axis=1)
            return out + bias
        key = jax.random.key(seed)
        ks = jax.random.split(key, 10)
        x = jax.random.normal(ks[0], (N, 768), dtype=jnp.float32)
        src = jax.random.randint(ks[1], (E_RAND,), 0, N)
        dst = jax.random.randint(ks[2], (E_RAND,), 0, N)
        loop = jnp.arange(N)
        edge_index = jnp.stack([jnp.concatenate([src, loop]), jnp.concatenate([dst, loop])])
        s = 1.0 / np.sqrt(768.0)
        W1 = jax.random.normal(ks[3], (768, 768), dtype=jnp.float32) * s
        a_src1 = jax.random.normal(ks[4], (8, 96), dtype=jnp.float32) * 0.1
        a_dst1 = jax.random.normal(ks[5], (8, 96), dtype=jnp.float32) * 0.1
        b1 = jnp.zeros((768,), dtype=jnp.float32)
        W2 = jax.random.normal(ks[6], (768, 768), dtype=jnp.float32) * s
        a_src2 = jax.random.normal(ks[7], (1, 768), dtype=jnp.float32) * 0.1
        a_dst2 = jax.random.normal(ks[8], (1, 768), dtype=jnp.float32) * 0.1
        b2 = jnp.zeros((768,), dtype=jnp.float32)
        return {'x': x, 'edge_index': edge_index, 'W1': W1, 'a_src1': a_src1, 'a_dst1': a_dst1, 'b1': b1, 'W2': W2, 'a_src2': a_src2, 'a_dst2': a_dst2, 'b2': b2}
    _L3_gnn_all = _L3_gnn_setup()
    _L3_gnn_in = {k: v for k, v in _L3_gnn_all.items() if k in ('W1', 'a_src1', 'a_dst1', 'b1', 'W2', 'a_src2', 'a_dst2', 'b2')}
    del _L3_gnn_all
    return {'x': x, 'src': src, 'dst': dst, 'edge_type_3': edge_type_3, 'edge_type_4': edge_type_4, 'L0_gnn_query_embs': _L0_gnn_in['query_embs'], 'L0_gnn_W_rel1': _L0_gnn_in['W_rel1'], 'L0_gnn_W_root1': _L0_gnn_in['W_root1'], 'L0_gnn_b1': _L0_gnn_in['b1'], 'L0_gnn_W_rel2': _L0_gnn_in['W_rel2'], 'L0_gnn_W_root2': _L0_gnn_in['W_root2'], 'L0_gnn_b2': _L0_gnn_in['b2'], 'L0_gnn_Wg': _L0_gnn_in['Wg'], 'L0_gnn_bg': _L0_gnn_in['bg'], 'L0_gnn_Wq': _L0_gnn_in['Wq'], 'L0_gnn_bq': _L0_gnn_in['bq'], 'L1_gnn_W1': _L1_gnn_in['W1'], 'L1_gnn_root1': _L1_gnn_in['root1'], 'L1_gnn_b1': _L1_gnn_in['b1'], 'L1_gnn_W2': _L1_gnn_in['W2'], 'L1_gnn_root2': _L1_gnn_in['root2'], 'L1_gnn_b2': _L1_gnn_in['b2'], 'L1_gnn_W3': _L1_gnn_in['W3'], 'L1_gnn_root3': _L1_gnn_in['root3'], 'L1_gnn_b3': _L1_gnn_in['b3'], 'L2_gnn_W1': _L2_gnn_in['W1'], 'L2_gnn_a_src1': _L2_gnn_in['a_src1'], 'L2_gnn_a_dst1': _L2_gnn_in['a_dst1'], 'L2_gnn_b1': _L2_gnn_in['b1'], 'L2_gnn_W2': _L2_gnn_in['W2'], 'L2_gnn_a_src2': _L2_gnn_in['a_src2'], 'L2_gnn_a_dst2': _L2_gnn_in['a_dst2'], 'L2_gnn_b2': _L2_gnn_in['b2'], 'L2_gnn_Wm1': _L2_gnn_in['Wm1'], 'L2_gnn_bm1': _L2_gnn_in['bm1'], 'L2_gnn_Wm2': _L2_gnn_in['Wm2'], 'L2_gnn_bm2': _L2_gnn_in['bm2'], 'L3_gnn_W1': _L3_gnn_in['W1'], 'L3_gnn_a_src1': _L3_gnn_in['a_src1'], 'L3_gnn_a_dst1': _L3_gnn_in['a_dst1'], 'L3_gnn_b1': _L3_gnn_in['b1'], 'L3_gnn_W2': _L3_gnn_in['W2'], 'L3_gnn_a_src2': _L3_gnn_in['a_src2'], 'L3_gnn_a_dst2': _L3_gnn_in['a_dst2'], 'L3_gnn_b2': _L3_gnn_in['b2']}

def reference(x, src, dst, edge_type_3, edge_type_4, L0_gnn_query_embs, L0_gnn_W_rel1, L0_gnn_W_root1, L0_gnn_b1, L0_gnn_W_rel2, L0_gnn_W_root2, L0_gnn_b2, L0_gnn_Wg, L0_gnn_bg, L0_gnn_Wq, L0_gnn_bq, L1_gnn_W1, L1_gnn_root1, L1_gnn_b1, L1_gnn_W2, L1_gnn_root2, L1_gnn_b2, L1_gnn_W3, L1_gnn_root3, L1_gnn_b3, L2_gnn_W1, L2_gnn_a_src1, L2_gnn_a_dst1, L2_gnn_b1, L2_gnn_W2, L2_gnn_a_src2, L2_gnn_a_dst2, L2_gnn_b2, L2_gnn_Wm1, L2_gnn_bm1, L2_gnn_Wm2, L2_gnn_bm2, L3_gnn_W1, L3_gnn_a_src1, L3_gnn_a_dst1, L3_gnn_b1, L3_gnn_W2, L3_gnn_a_src2, L3_gnn_a_dst2, L3_gnn_b2):
    import jax
    import jax.numpy as jnp

    def _L0_gnn_ref(x, edge_index, edge_type, query_embs, W_rel1, W_root1, b1, W_rel2, W_root2, b2, Wg, bg, Wq, bq):
        import jax, jax.numpy as jnp
        import numpy as np
        NUM_RELATIONS = 3

        def _rgcn(x, W_rel, W_root, bias, src, dst, etype):
            n = x.shape[0]
            xr = jnp.einsum('ni,rio->rno', x, W_rel)
            msg = xr[etype, src]
            out = x @ W_root + bias
            for r in range(NUM_RELATIONS):
                m = etype == r
                s = jax.ops.segment_sum(jnp.where(m[:, None], msg, 0.0), dst, num_segments=n)
                c = jax.ops.segment_sum(m.astype(x.dtype), dst, num_segments=n)
                out = out + s / jnp.maximum(c, 1.0)[:, None]
            return out

        def _gate(h, q, Wg, bg, Wq, bq):
            B, L, F = q.shape
            N = h.shape[0] // B
            h3 = h.reshape(B, N, F)
            hg = jnp.einsum('bnf,gf->bng', h3, Wg[:, :F])
            qg = jnp.einsum('blf,gf->blg', q, Wg[:, F:]) + bg
            attn = jax.nn.sigmoid(hg[:, :, None, :] + qg[:, None, :, :])
            qi = jnp.einsum('bnlf,blf->bnf', attn, q)
            alpha = jax.nn.sigmoid(jnp.einsum('bnf,gf->bng', h3, Wq[:, :F]) + jnp.einsum('bnf,gf->bng', qi, Wq[:, F:]) + bq)
            hn = alpha * jnp.tanh(qi) + (1.0 - alpha) * h3
            return hn.reshape(B * N, F)
        src, dst = (edge_index[0], edge_index[1])
        h = jax.nn.relu(_rgcn(x, W_rel1, W_root1, b1, src, dst, edge_type))
        h = _gate(h, query_embs, Wg, bg, Wq, bq)
        h = jax.nn.relu(_rgcn(h, W_rel2, W_root2, b2, src, dst, edge_type))
        h = _gate(h, query_embs, Wg, bg, Wq, bq)
        return h

    def _L1_gnn_ref(entity, edge_index, edge_type, W1, root1, b1, W2, root2, b2, W3, root3, b3):
        import jax, jax.numpy as jnp
        import numpy as np
        N_NODES = 2500
        N_EDGES = 12500
        D = 768
        NUM_REL = 4

        def _rgcn_conv(x, weight, root, bias, src, dst, etype):
            n = x.shape[0]
            out = x @ root + bias
            for r in range(NUM_REL):
                sel = etype == r
                self_f = sel.astype(x.dtype)
                deg = jnp.zeros((n,), x.dtype).at[dst].add(self_f)
                norm = jnp.where(sel, 1.0 / jnp.maximum(deg[dst], 1.0), 0.0)
                h_r = x @ weight[r]
                msgs = h_r[src] * norm[:, None]
                out = out + jax.ops.segment_sum(msgs, dst, num_segments=n)
            return out
        src, dst = (edge_index[0], edge_index[1])
        x = jax.nn.relu(_rgcn_conv(entity, W1, root1, b1, src, dst, edge_type))
        x = jax.nn.relu(_rgcn_conv(x, W2, root2, b2, src, dst, edge_type))
        x = _rgcn_conv(x, W3, root3, b3, src, dst, edge_type)
        return x

    def _L2_gnn_ref(x, edge_index, W1, a_src1, a_dst1, b1, W2, a_src2, a_dst2, b2, Wm1, bm1, Wm2, bm2):
        import jax, jax.numpy as jnp
        import numpy as np
        N = 6250
        E = 200000
        IN_DIM = 768
        HID = 256
        OUT_DIM = 768
        HEADS = 4
        NEG_SLOPE = 0.2

        def gat_conv(x, src, dst, W, a_src, a_dst, bias, heads):
            n = x.shape[0]
            h = (x @ W).reshape(n, heads, -1)
            alpha_s = (h * a_src[None]).sum(-1)
            alpha_d = (h * a_dst[None]).sum(-1)
            e = jax.nn.leaky_relu(alpha_s[src] + alpha_d[dst], NEG_SLOPE)
            m = jax.ops.segment_max(e, dst, num_segments=n)
            e = jnp.exp(e - m[dst])
            denom = jax.ops.segment_sum(e, dst, num_segments=n)
            alpha = e / (denom[dst] + 1e-16)
            out = jax.ops.segment_sum(h[src] * alpha[:, :, None], dst, num_segments=n)
            return out.reshape(n, -1) + bias
        n = x.shape[0]
        loops = jnp.arange(n, dtype=edge_index.dtype)
        src = jnp.concatenate([edge_index[0], loops])
        dst = jnp.concatenate([edge_index[1], loops])
        h = gat_conv(x, src, dst, W1, a_src1, a_dst1, b1, HEADS)
        h = jax.nn.relu(h)
        h = gat_conv(h, src, dst, W2, a_src2, a_dst2, b2, 1)
        h = jax.nn.relu(h)
        h = jax.nn.relu(h @ Wm1 + bm1)
        return h @ Wm2 + bm2

    def _L3_gnn_ref(x, edge_index, W1, a_src1, a_dst1, b1, W2, a_src2, a_dst2, b2):
        import jax, jax.numpy as jnp
        import numpy as np
        N = 2500
        E_RAND = 40000
        NEG_SLOPE = 0.2

        def gat_layer(x, W, a_src, a_dst, bias, src, dst, heads, out_c, concat):
            n = x.shape[0]
            h = (x @ W).reshape(n, heads, out_c)
            al_s = jnp.einsum('nhc,hc->nh', h, a_src)
            al_d = jnp.einsum('nhc,hc->nh', h, a_dst)
            e = jax.nn.leaky_relu(al_s[src] + al_d[dst], NEG_SLOPE)
            m = jax.ops.segment_max(e, dst, num_segments=n)
            ex = jnp.exp(e - m[dst])
            z = jax.ops.segment_sum(ex, dst, num_segments=n)
            alpha = ex / (z[dst] + 1e-16)
            msg = h[src] * alpha[:, :, None]
            out = jax.ops.segment_sum(msg, dst, num_segments=n)
            out = out.reshape(n, heads * out_c) if concat else out.mean(axis=1)
            return out + bias
        src, dst = (edge_index[0], edge_index[1])
        h = gat_layer(x, W1, a_src1, a_dst1, b1, src, dst, heads=8, out_c=96, concat=True)
        h = jax.nn.elu(h)
        out = gat_layer(h, W2, a_src2, a_dst2, b2, src, dst, heads=1, out_c=768, concat=False)
        return out
    edge_index = jnp.stack([src, dst])
    h = jnp.maximum(_layernorm(x, axis=-1), 0.0)
    x = x + _L0_gnn_ref(h, edge_index, edge_type_3, L0_gnn_query_embs, L0_gnn_W_rel1, L0_gnn_W_root1, L0_gnn_b1, L0_gnn_W_rel2, L0_gnn_W_root2, L0_gnn_b2, L0_gnn_Wg, L0_gnn_bg, L0_gnn_Wq, L0_gnn_bq)
    h = jnp.maximum(_layernorm(x, axis=-1), 0.0)
    x = x + _L1_gnn_ref(h, edge_index, edge_type_4, L1_gnn_W1, L1_gnn_root1, L1_gnn_b1, L1_gnn_W2, L1_gnn_root2, L1_gnn_b2, L1_gnn_W3, L1_gnn_root3, L1_gnn_b3)
    h = jnp.maximum(_layernorm(x, axis=-1), 0.0)
    x = x + _L2_gnn_ref(h, edge_index, L2_gnn_W1, L2_gnn_a_src1, L2_gnn_a_dst1, L2_gnn_b1, L2_gnn_W2, L2_gnn_a_src2, L2_gnn_a_dst2, L2_gnn_b2, L2_gnn_Wm1, L2_gnn_bm1, L2_gnn_Wm2, L2_gnn_bm2)
    h = jnp.maximum(_layernorm(x, axis=-1), 0.0)
    x = x + _L3_gnn_ref(h, edge_index, L3_gnn_W1, L3_gnn_a_src1, L3_gnn_a_dst1, L3_gnn_b1, L3_gnn_W2, L3_gnn_a_src2, L3_gnn_a_dst2, L3_gnn_b2)
    return x

_drawn_inputs = setup_inputs


def setup_inputs(seed=0):
    import zlib

    import numpy as np

    out = dict(_drawn_inputs(seed))
    spreads = {'L0_gnn_b1': (0.0, 0.607),
     'L0_gnn_b2': (0.0, 0.1),
     'L0_gnn_bg': (0.0, 0.503),
     'L0_gnn_bq': (0.0, 0.631),
     'L1_gnn_b1': (0.0, 0.1),
     'L1_gnn_b2': (0.0, 0.1),
     'L1_gnn_b3': (0.0, 0.1),
     'L2_gnn_b1': (0.0, 0.337),
     'L2_gnn_b2': (0.0, 0.1),
     'L2_gnn_bm1': (0.0, 0.1),
     'L2_gnn_bm2': (0.0, 0.1),
     'L3_gnn_b1': (0.0, 0.1),
     'L3_gnn_b2': (0.0, 0.1)}
    factors = {'L2_gnn_a_src1': 8.0,
     'L2_gnn_a_dst1': 8.0,
     'L2_gnn_a_src2': 8.0,
     'L2_gnn_a_dst2': 8.0,
     'L3_gnn_a_dst1': 8.0,
     'L3_gnn_a_src2': 8.0,
     'L3_gnn_a_dst2': 8.0}
    for name, (base, spread) in spreads.items():
        noise = np.random.default_rng([zlib.crc32(name.encode()), seed]).standard_normal(out[name].shape)
        drawn = base * np.exp(spread * noise) if base else spread * noise
        out[name] = jnp.asarray(drawn.astype(out[name].dtype))
    for name, factor in factors.items():
        out[name] = (out[name] * factor).astype(out[name].dtype)
    return out
```

```python
from contextlib import ExitStack

import concourse.bass as bass
from concourse import mybir

P = 128
N = 256
NT = N // P
F = 768
KC = F // P
FH = F // 2
E = 4352
EC = E // P
EC0 = 18
B, L = 8, 64
NB = N // B
LH = L // 2
R3, R4 = 3, 4
SHIFT = 12
ZT = 4
STEPS = KC * B
NU = 33
NEG = -1.0e30
EPS = 1e-5
SLOPE = 0.2

F32, F32R, BF16 = mybir.dt.float32, mybir.dt.float32r, mybir.dt.bfloat16
I32, I16 = mybir.dt.int32, mybir.dt.int16
ALU, ACT, AX = mybir.AluOpType, mybir.ActivationFunctionType, mybir.AxisListType

C_ID, C_IOTA, C_ONES, C_SEL, C_SELB = 0, P, P + N, 2 * P + N, 2 * P + N + 2 * 512
C_ALL = C_SELB + 4 * P
BIAS_ROWS = 4
GAT = [(4, 64, 0, 256, 0), (1, 256, 512, 768, 256), (8, 96, 1024, 1792, 768), (1, 768, 2560, 3328, 1536)]
GB_M1, GB_M2 = 512, 2304
PROJ = [(6, 256, 0, 30), (2, 256, 1536, 30), (2, 256, 2048, 30), (2, 768, 2560, 30), (6, 768, 0, 31), (6, 768, 0, 32)]
PTILE = [0, 3, 4, 5, 6, 9, 12]


class Chain:

    def __init__(self, eng, sem):
        self.eng, self.sem, self.n = eng, sem, 0

    def step(self, ins):
        self.n += 1
        ins.then_inc(self.sem, 1)
        self.eng.wait_ge(self.sem, self.n)


def build(nc, x, ei, qT, consts, brows, gbias, gavec, W, out):
    ctx = ExitStack()
    with ctx:
        at = [nc.sbuf_base]

        def place(size):
            o = (at[0] + 31) // 32 * 32
            at[0] = o + size
            return o

        def sb(name, shape, dt, off=None):
            size = 1
            for s in shape[1:]:
                size *= s
            size *= {F32: 4, F32R: 4, I32: 4, BF16: 2, I16: 2}[dt]
            o = place(size) if off is None else off
            return nc.alloc_sbuf_tensor_at(name, shape, dt, offset=o)

        def sem(name):
            return ctx.enter_context(nc.semaphore(name))

        ps = ctx.enter_context(nc.psum_tensor("ps", [P, 8, 512], F32))

        Wr = sb("w_raw", [P, 3, 2 * F], F32)
        Wh = sb("w_hi", [P, 3, 2 * F], F32R)
        Wl = sb("w_lo", [P, 3, 2 * F], F32R)
        y_off = place(12288)
        YTh = sb("yt_hi", [P, 2, KC, N], F32R, y_off)
        YTl = sb("yt_lo", [P, 2, KC, N], F32R)
        H = sb("h", [P, NT, F], F32)
        t_off = place(6144)
        qiT = sb("qi_t", [P, KC, N], F32, t_off)
        A3 = sb("a3", [P, NT, R3, N], F32R)
        A4i = sb("a4_i", [P, NT, R4, N], I16)
        rinv3 = sb("rinv3", [P, R3, N], F32)
        ident = sb("ident", [P, P], F32)
        ones = sb("ones", [P, P], F32R)
        onesf = sb("ones_f", [8, P], F32)
        SEL = sb("sel", [P, 2, 512], F32R)
        selb = sb("selb", [P, 4, P], F32R)
        Bias = sb("bias", [P, 2 * F], F32R)
        q_off = place(12288)
        qTf = sb("q_t", [P, KC, B * L], F32, q_off)
        z_off = place(49152)
        Z = sb("z_rows", [P, 2 * B, F], F32R, z_off)
        g_off = place(24576)
        small = sb("small", [P, 128], F32)
        mhalf = sb("mhalf", [P, NT], F32)
        const_in = sb("const_in", [P, C_ALL], F32, z_off)
        bias_in = sb("bias_in", [BIAS_ROWS, 2 * F], F32, z_off + 4 * C_ALL)
        edge_i = sb("edge_i", [P, 4, EC], I32, t_off)
        edge_f = sb("edge_f", [P, 5, EC], F32, t_off + 16 * EC)
        oh_off = (t_off + 36 * EC + 31) // 32 * 32
        iota = sb("iota", [P, N], BF16, oh_off)
        OH = sb("onehot_src", [P, 2, N], BF16, oh_off + 512)
        V = sb("onehot_dst", [P, 2, 3 * N], BF16, oh_off + 1536)
        dec_lo = sb("dec_lo", [P, 3 * N], I32, g_off)
        dec_hi = sb("dec_hi", [P, 3 * N], I32, g_off + 3072)
        acc = sb("acc", [P, NT, 6, N], I16, g_off + 6144)
        Hh = sb("h_hi", [P, NT, F], F32R, g_off)
        Hl = sb("h_lo", [P, NT, F], F32R, g_off + 6144)
        PR = sb("prod", [P, 2, 2048], F32, g_off)
        S = sb("sums", [P, 2, 1024], F32, g_off + 16384)
        alpha = sb("alpha", [P, NT, F], F32, g_off + 12288)
        tq = sb("tanh_q", [P, NT, F], F32, g_off + 18432)
        X = sb("x", [P, NT, F], F32, z_off)
        A4 = sb("a4", [P, NT, R4, N], F32R, z_off + 6144)
        rinv4 = sb("rinv4", [P, R4, N], F32, z_off + 6144 + 8192)
        av = sb("a_vec", [P, 4096], F32, z_off + 6144)
        cnt = sb("count", [P, 2, NT, N], F32, z_off + 22528)
        neg = sb("masked", [P, 2, NT, N], F32, z_off + 26624)
        hau = sb("h_aug", [P, 1568], F32, z_off + 30720)
        ald_sb = sb("ald_t", [8, N], F32, z_off + 36992)
        gb = sb("g_bias", [P, 3072], F32, q_off)
        zb = sb("attn", [P, 2, 2048], F32, g_off)
        gtmp = sb("gat_tmp", [P, 2048], F32, g_off + 16384)
        blkS = sb("blk_s", [8, 2048], F32, g_off)
        blkM = sb("blk_m", [8, 2048], F32, g_off + 8192)
        blkD = sb("blk_d", [8, 2048], F32, g_off + 16384)
        gout = sb("g_out", [P, NT, F], F32, y_off + 6144)
        elu_t = sb("elu_t", [P, NT, F], F32, g_off)

        s_const, s_edge, s_x, s_q, s_bias = (sem(n) for n in ("s_const", "s_edge", "s_x", "s_q", "s_bias"))
        s_raw = [sem(f"s_raw{j}") for j in range(3)]
        s_whi, s_wlo, s_used = sem("s_whi"), sem("s_wlo"), sem("s_used")
        s_cst = sem("s_cst")
        s_chain = sem("s_chain")
        s_achain = sem("s_achain")
        s_pchain = sem("s_pchain")
        s_var, s_rstd, s_norm = sem("s_var"), sem("s_rstd"), sem("s_norm")
        s_H, s_hhi, s_h = sem("s_H"), sem("s_hhi"), sem("s_h")
        s_yt, s_scale, s_ythi, s_ytlo = sem("s_yt"), sem("s_scale"), sem("s_ythi"), sem("s_ytlo")
        s_qhi, s_qlo = sem("s_qhi"), sem("s_qlo")
        s_out = sem("s_out")
        s_qghi, s_qglo = sem("s_qghi"), sem("s_qglo")
        s_oh, s_adj, s_acount, s_deg, s_rinv = sem("s_oh"), sem("s_adj"), sem("s_acount"), sem("s_deg"), sem("s_rinv")
        s_dec = sem("s_dec")
        s_hghi, s_hglo = sem("s_hghi"), sem("s_hglo")
        s_gate1, s_gate2 = sem("s_gate1"), sem("s_gate2")
        s_z, s_sig, s_mul, s_add, s_red = sem("s_z"), sem("s_sig"), sem("s_mul"), sem("s_add"), sem("s_red")
        s_qihi, s_qilo, s_tr, s_tanh, s_alpha = (sem(n) for n in ("s_qihi", "s_qilo", "s_tr", "s_tanh", "s_alpha"))
        s_x2, s_res, s_gv = sem("s_x2"), sem("s_res"), sem("s_gv")
        s_cntT, s_cnt = sem("s_cntT"), sem("s_cnt")
        p_H, p_t, p_hi, p_lo, p_out, p_ev = (sem(n) for n in ("p_H", "p_t", "p_hi", "p_lo", "p_out", "p_ev"))
        g_h, g_al, g_alT, g_blkS, g_ms, g_m, g_mT, g_blk, g_bc, g_zz, g_lk, g_sub, g_rl, g_ex, g_p, g_o, g_el, g_ex2 = (
            sem(n) for n in ("g_h", "g_al", "g_alT", "g_blkS", "g_ms", "g_m", "g_mT", "g_blk", "g_bc", "g_zz",
                             "g_lk", "g_sub", "g_rl", "g_ex", "g_p", "g_o", "g_el", "g_ex2"))
        s_fin, s_store = sem("s_fin"), sem("s_store")

        block = ctx.enter_context(nc.Block())

        def nodes(ap):
            return ap.rearrange("(t p) f -> p t f", p=P)

        def two_banks(nt):
            return ps[:, 2 * nt:2 * nt + 2, 0:FH]

        def halves(ap):
            return ap.rearrange("p (h f) -> p h f", h=2)

        def tile3(j):
            return ps[:, 4 + j, :].rearrange("p (k n) -> p k n", k=2)

        def wait_out(eng, group, t, U):
            if t == 0:
                eng.wait_ge(s_out, group + 1)
            else:
                eng.wait_ge(s_used, 3 * U + 3)

        @block.sync
        def _(sp):
            def load_slab(U, j):
                sp.dma_start(Wr[:, j, :], W[U, :, j, :] if isinstance(U, int)
                             else W[bass.DynSlice(U, 1), :, j, :].rearrange("o p f -> p (o f)")).then_inc(s_raw[j], 16)

            sp.dma_start(const_in[:], consts).then_inc(s_const, 16)
            sp.dma_start(bias_in[:], brows).then_inc(s_bias, 16)
            for j in range(3):
                load_slab(0, j)
            with sp.Fori(1, NU) as U:
                for j in range(3):
                    sp.wait_ge(s_wlo, 3 * U + (j - 2))
                    load_slab(U, j)
            sp.wait_ge(s_fin, 2)
            sp.dma_start(nodes(out), X[:]).then_inc(s_store, 16)
            sp.wait_ge(s_store, 16)

        @block.gpsimd
        def _(pool):
            ch = Chain(pool, s_pchain)

            def w_lo(U):
                for j in range(3):
                    w_lo_slab(U, j)

            def w_lo_slab(U, j):
                pool.wait_ge(s_whi, 3 * U + (j + 1))
                pool.tensor_tensor(Wl[:, j, :], Wr[:, j, :], Wh[:, j, :], ALU.subtract).then_inc(s_wlo, 1)

            def rstd(n):
                pool.wait_ge(s_var, n + 1)
                pool.tensor_tensor(small[:, 48:50], small[:, 44:46], mhalf[:], ALU.pow).then_inc(s_rstd, 1)

            ch.step(pool.memset(mhalf[:], -0.5))
            w_lo(0)
            rstd(0)
            w_lo(1)
            with pool.Fori(0, 2) as i:
                for v in range(1, 6):
                    w_lo(7 * i + (1 + v))
                for f in range(KC):
                    for b in range(B):
                        st = f * B + b
                        if f in (1, 2, 3) and b == 1:
                            w_lo_slab(7 * i + 7, f - 1)
                        if f in (3, 5) and b == 2:
                            w_lo_slab(7 * i + 8, (f - 3) // 2)
                        pool.wait_ge(s_mul, 4 * STEPS * i + 4 * (st + 1))
                        if st >= 2:
                            pool.wait_ge(s_red, STEPS * i + (st - 1))
                        pool.tensor_tensor(S[:, st % 2, :], PR[:, st % 2, 0:1024], PR[:, st % 2, 1024:2048],
                                           ALU.add).then_inc(s_add, 1)
                w_lo_slab(7 * i + 8, 2)
            rstd(1)
            with pool.Fori(0, 3) as i:
                for v in range(5):
                    w_lo(5 * i + (16 + v))
            rstd(2)
            w_lo(31)
            rstd(3)
            w_lo(32)

        @block.scalar
        def _(act):
            ch = Chain(act, s_achain)

            def copy(o, i):
                return act.activation(o, i, ACT.Copy)

            def w_hi_slab(U, j, first=False):
                act.wait_ge(s_raw[j], 16 * U + 16)
                if not first:
                    act.wait_ge(s_used, 3 * U + (j - 2))
                copy(Wh[:, j, :], Wr[:, j, :]).then_inc(s_whi, 1)

            def w_hi(U, first=False):
                for j in range(3):
                    w_hi_slab(U, j, first)

            def yt_hi(T, slot, scaled=None):
                for j in range(3):
                    if scaled is None:
                        act.wait_ge(s_yt, T + (j + 1))
                    else:
                        act.wait_ge(s_scale, scaled + (j + 1))
                    copy(YTh[:, slot, 2 * j:2 * j + 2, :], tile3(j)).then_inc(s_ythi, 1)

            def relu_norm(n, h_sem):
                act.wait_ge(s_norm, 2 * n + 2)
                for t in range(NT):
                    act.activation(H[:, t, :], H[:, t, :], ACT.Relu).then_inc(h_sem, 1)

            def h_hi(n):
                act.wait_ge(s_H, n)
                for t in range(NT):
                    copy(Hh[:, t, :], H[:, t, :]).then_inc(s_hhi, 1)

            act.dma_start(edge_i[:], ei).then_inc(s_edge, 16)
            act.dma_start(H[:], nodes(x)).then_inc(s_x, 16)
            act.dma_start(qTf[:], qT).then_inc(s_q, 16)

            act.wait_ge(s_q, 16)
            for t in range(2):
                copy(YTh[:, t, :, :], qTf[:, :, t * N:(t + 1) * N]).then_inc(s_qhi, 1)
            w_hi(0, first=True)
            relu_norm(0, s_H)

            for t in range(2):
                for u in range(NT):
                    if t == 0:
                        act.wait_ge(s_out, u + 1)
                    else:
                        wait_out(act, 2, u, 0)
                    for g in range(4):
                        copy(halves(Z[64:96, 8 * t + 4 * u + g, :]), ps[32 * g:32 * g + 32, 2 * u:2 * u + 2, 0:FH]
                             ).then_inc(s_qghi, 1)
            w_hi(1)
            act.wait_ge(s_acount, 1)
            h_hi(2)

            with act.Fori(0, 2) as i:
                yt_hi(15 * i, 0)
                for v in range(4):
                    if v < 3:
                        yt_hi(None, (v + 1) % 2, 9 * i + 3 * v)
                    w_hi(7 * i + (2 + v))
                for t in range(NT):
                    wait_out(act, 3 * i + 3, t, 7 * i + 4)
                    act.activation(halves(H[:, t, :]), two_banks(t), ACT.Relu).then_inc(s_H, 1)
                yt_hi(15 * i + 12, 0)
                w_hi(7 * i + 6)

                def hg_hi(b):
                    if b % 4 == 0:
                        wait_out(act, 3 * i + 4, b // 4, 7 * i + 5)
                    for lh in range(2):
                        ins = copy(halves(Z[0:32, 2 * b + lh, :]),
                                   ps[32 * (b % 4):32 * (b % 4) + 32, 2 * (b // 4):2 * (b // 4) + 2, 0:FH])
                    ins.then_inc(s_hghi, 1)

                hg_hi(0)
                for f in range(KC):
                    for b in range(B):
                        st = f * B + b
                        if f == 0 and b < B // 2:
                            for b2 in range(2 * b + 1, min(2 * b + 3, B)):
                                hg_hi(b2)
                        for t in range(ZT):
                            act.wait_ge(s_z, 4 * STEPS * i + (4 * st + t + 1))
                            act.activation(ps[:, 4 + t, :], ps[:, 4 + t, :], ACT.Sigmoid).then_inc(s_sig, 1)
                        if f in (1, 2, 3) and b == 0:
                            w_hi_slab(7 * i + 7, f - 1)
                        if f in (3, 5) and b == 1:
                            w_hi_slab(7 * i + 8, (f - 3) // 2)
                        if f > 0 and b == 1:
                            act.wait_ge(s_red, STEPS * i + B * f)
                            copy(YTh[:, 1, f - 1, :], qiT[:, f - 1, :]).then_inc(s_qihi, 1)
                act.wait_ge(s_red, STEPS * i + STEPS)
                copy(YTh[:, 1, KC - 1, :], qiT[:, KC - 1, :]).then_inc(s_qihi, 1)
                act.wait_ge(s_tr, i + 1)
                tflat = ps[:, 4:7, :].rearrange("p b n -> p (b n)")
                for t in range(NT):
                    act.activation(tq[:, t, :], tflat[:, t * F:(t + 1) * F], ACT.Tanh).then_inc(s_tanh, 1)
                for t in range(NT):
                    wait_out(act, 3 * i + 5, t, 7 * i + 7)
                    act.activation(halves(alpha[:, t, :]), two_banks(t), ACT.Sigmoid).then_inc(s_alpha, 1)
                w_hi_slab(7 * i + 8, 2)
                h_hi(4 * i + 6)

            act.wait_ge(s_h, 6)
            act.dma_start(X[:], nodes(x)).then_inc(s_x2, 16)
            relu_norm(1, s_H)
            h_hi(12)
            with act.Fori(0, 2) as i:
                yt_hi(15 * i + 30, 0)
                for v in range(5):
                    if v < 4:
                        yt_hi(None, (v + 1) % 2, 12 * i + (18 + 3 * v))
                    w_hi(5 * i + (16 + v))
                for t in range(NT):
                    wait_out(act, i + 9, t, 5 * i + 19)
                    act.activation(halves(H[:, t, :]), two_banks(t), ACT.Relu).then_inc(s_H, 1)
                h_hi(2 * i + 14)
            yt_hi(60, 0)
            for v in range(5):
                if v < 4:
                    yt_hi(None, (v + 1) % 2, 42 + 3 * v)
                w_hi(26 + v)
            act.wait_ge(s_res, 2)
            act.dma_start(av[:], gavec.partition_broadcast(P)).then_inc(s_gv, 16)
            act.dma_start(gb[:], gbias.partition_broadcast(P)).then_inc(s_gv, 16)
            relu_norm(2, p_H)

            def proj_hi(q):
                for j in range(PTILE[q + 1] - PTILE[q]):
                    act.wait_ge(p_t, PTILE[q] + j + 1)
                    copy(YTh[:, 0, 2 * j:2 * j + 2, :], tile3(j)).then_inc(p_hi, 1)

            def gat(g, q):
                hn, c, _, _, _ = GAT[g]
                hv = hau[:, 0:NT * hn * (c + 1)].rearrange("p (t h c) -> p t h c", t=NT, h=hn)
                for t in range(NT):
                    act.wait_ge(p_out, 2 * q + t + 1)
                    if hn * c == F:
                        src = two_banks(t)
                        if hn == 1:
                            dst = halves(hv[:, t, 0, 0:c])
                            copy(dst, src).then_inc(g_h, 1)
                        else:
                            for u in range(2):
                                ins = copy(hv[:, t, 4 * u:4 * u + 4, 0:c],
                                           ps[:, 2 * t + u, 0:FH].rearrange("p (h c) -> p h c", c=c))
                            ins.then_inc(g_h, 1)
                    else:
                        copy(hv[:, t, :, 0:c], ps[:, 2 * t, 0:hn * c].rearrange("p (h c) -> p h c", c=c)).then_inc(g_h, 1)
                w = hn * N
                for t in range(NT):
                    act.wait_ge(g_sub, 2 * g + t + 1)
                    act.activation(zb[:, t, 0:w], zb[:, t, 0:w], ACT.Relu, scale=-1.0).then_inc(g_rl, 1)
                    act.wait_ge(g_rl, 2 * g + t + 1)
                    act.activation(zb[:, t, 0:w], zb[:, t, 0:w], ACT.Exp, scale=-1.0).then_inc(g_ex, 1)

            proj_hi(0)
            gat(0, 0)
            proj_hi(1)
            gat(1, 1)
            proj_hi(2)
            proj_hi(3)
            act.wait_ge(p_out, 8)
            w_hi(31, first=True)
            relu_norm(3, p_H)
            proj_hi(4)
            gat(2, 4)
            w_hi(32, first=True)
            act.wait_ge(g_el, 2)
            act.activation(elu_t[:], elu_t[:], ACT.Exp).then_inc(g_ex2, 1)
            proj_hi(5)
            gat(3, 5)

        @block.tensor
        def _(pe):
            def parts(slot, k, t, Wk, cols=((0, 0, FH), (1, FH, FH))):
                out_ = []
                for Y, Wx in ((YTh, Wh), (YTh, Wl), (YTl, Wh)):
                    for bank, c0, w in cols:
                        out_.append((ps[:, 2 * t + bank, 0:w], Y[:, slot, k, t * P:(t + 1) * P], Wk(Wx, c0, w)))
                return out_

            def slab_chunk(k):
                return lambda Wx, c0, w: Wx[:, k // 2, (k % 2) * F + c0:(k % 2) * F + c0 + w]

            def bias_mm(row, slot):
                for t in range(NT):
                    for h in range(2):
                        if isinstance(slot, int):
                            rhs = Bias[:, slot * F + h * FH:slot * F + (h + 1) * FH]
                        else:
                            rhs = Bias[:, bass.DynSlice(slot * F + h * FH, FH)]
                        pe.matmul(ps[:, 2 * t + h, 0:FH], selb[:, row, :], rhs, start=True, stop=False)

            def product(U, slot, ready, bias, release=True):
                if bias is not None:
                    bias_mm(*bias)
                for j in range(3):
                    pe.wait_ge(s_wlo, 3 * U + (j + 1))
                    if ready is not None:
                        pe.wait_ge(s_ytlo, ready + (j + 1))
                    for kk in range(2):
                        k = 2 * j + kk
                        for t in range(NT):
                            for n, (o, a, b_) in enumerate(parts(slot, k, t, slab_chunk(k))):
                                mm = pe.matmul(o, a, b_, start=False,
                                               stop=(last_unit[0] and k == KC - 1 and n >= 4))
                            if last_unit[0] and k == KC - 1 and t == 0:
                                mm.then_inc(s_out, 1)
                    if release:
                        mm.then_inc(s_used, 1)
                    elif j == 2:
                        mm.then_inc(s_out, 1)

            last_unit = [False]

            def transposed(src, sem_, chunks=KC):
                for j in range(chunks // 2):
                    for kk in range(2):
                        for t in range(NT):
                            k = 2 * j + kk
                            ins = pe.transpose(ps[:, 4 + j, kk * N + t * P:kk * N + (t + 1) * P],
                                               src[:, t, k * P:(k + 1) * P], ident[:])
                    ins.then_inc(sem_, 1)

            def aggregate(A, r, prev):
                for j in range(3):
                    pe.wait_ge(s_ytlo, prev + (j + 1))
                    for kk in range(2):
                        k = 2 * j + kk
                        n = 0
                        for t in range(NT):
                            for Hx in (Hh, Hl):
                                ins = pe.matmul(ps[:, 4 + j, kk * N:(kk + 1) * N], Hx[:, t, k * P:(k + 1) * P],
                                                A[:, t, r, :], start=(n == 0), stop=(n == 3))
                                n += 1
                    ins.then_inc(s_yt, 1)

            def count_half(h):
                c0, c1 = (0, EC0) if h == 0 else (EC0, EC)

                def chunk(slot, first, last, ready):
                    pe.wait_ge(s_oh, ready)
                    for t in range(NT):
                        for u in range(2):
                            ins = pe.matmul(ps[:, 4 + 2 * t + u, 0:FH], OH[:, slot, t * P:(t + 1) * P],
                                            V[:, slot, u * FH:(u + 1) * FH], start=first, stop=last)
                    ins.then_inc(s_adj, 1)

                if h == 1:
                    pe.wait_ge(s_dec, 1)
                for u in range(2):
                    chunk(u, u == 0, False, c0 + u + 1)
                with pe.Fori(c0 // 2 + 1, c1 // 2 - 1) as i:
                    for u in range(2):
                        chunk(u, False, False, 2 * i + (u + 1))
                for u in range(2):
                    chunk(u, False, u == 1, c1 - 2 + u + 1)

            pe.wait_ge(s_cst, 1)
            last_unit[0] = True
            for t in range(2):
                pe.wait_ge(s_qlo, t + 1)
                if t == 1:
                    pe.wait_ge(s_qglo, 8)
                product(0, t, None, (3, 1), release=(t == 1))
                count_half(t)
            last_unit[0] = False
            for r, bank, c in ((0, 4, 0), (1, 4, N), (2, 5, 0)):
                pe.wait_ge(s_acount, 1)
                for t in range(NT):
                    ins = pe.matmul(ps[:, bank, c:c + N], ones[:], A3[:, t, r, :], start=(t == 0), stop=(t == 1))
            ins.then_inc(s_deg, 1)
            pe.wait_ge(s_rinv, 1)
            pe.wait_ge(s_qglo, 16)

            with pe.Fori(0, 2) as i:
                T = 15 * i
                U = 7 * i + 1
                pe.wait_ge(s_H, 4 * i + 2)
                transposed(H, s_yt)
                pe.wait_ge(s_h, 2 * i + 2)
                aggregate(A3, 0, T)
                for v in range(4):
                    last_unit[0] = v == 3
                    product(U + v, v % 2, T + 3 * v, (0, i) if v == 0 else None)
                    if v < 2:
                        aggregate(A3, v + 1, T + 3 * (v + 1))
                pe.wait_ge(s_H, 4 * i + 4)
                transposed(H, s_yt)
                for j in range(3):
                    pe.wait_ge(s_wlo, 3 * (U + 4) + (j + 1))
                    pe.wait_ge(s_ytlo, T + (12 + j + 1))
                    for kk in range(2):
                        k = 2 * j + kk
                        for t in range(NT):
                            for n, (o, a, b_) in enumerate(parts(0, k, t, slab_chunk(k))):
                                mm = pe.matmul(o, a, b_, start=(k == 0 and n < 2), stop=(k == KC - 1 and n >= 4))
                            if k == KC - 1 and t == 0:
                                mm.then_inc(s_out, 1)
                    mm.then_inc(s_used, 1)
                for f in range(KC):
                    hq = [m for kk in range(2) for t in range(NT) for m in parts(0, 2 * f + kk, t, slab_chunk(2 * f + kk))] \
                        if f < 3 else []
                    qq = [m for t in range(NT) for m in parts(1, f - 1, t, slab_chunk(f - 1))] if f > 0 else []
                    for b in range(B):
                        st = f * B + b
                        if f == 0:
                            pe.wait_ge(s_hglo, 8 * i + (b + 1))
                        for t in range(ZT):
                            k = 4 * st + t
                            if k >= 4:
                                pe.wait_ge(s_mul, 4 * STEPS * i + (k - 3))
                            pe.matmul(ps[:, 4 + t, :], Z[:, 2 * b + t // 2, f * P:(f + 1) * P], SEL[:, t % 2, :],
                                      start=True, stop=True).then_inc(s_z, 1)
                        if f < 3 and (f > 0 or b >= 4):
                            if b == (4 if f == 0 else 0):
                                pe.wait_ge(s_wlo, 3 * (U + 5) + (f + 1))
                            if (f, b) == (0, 4):
                                pe.wait_ge(s_hglo, 8 * i + 8)
                                bias_mm(1, i)
                            for o, a, b_ in hq[3 * b:3 * b + 3] if f > 0 else hq[6 * (b - 4):6 * (b - 4) + 6]:
                                mm = pe.matmul(o, a, b_, start=False, stop=False)
                            if b == B - 1:
                                mm.then_inc(s_used, 1)
                        if f > 0 and b >= 4:
                            if b == 4:
                                pe.wait_ge(s_wlo, 3 * (U + 6) + ((f - 1) // 2 + 1))
                                pe.wait_ge(s_qilo, 6 * i + f)
                            for o, a, b_ in qq[3 * (b - 4):3 * (b - 4) + 3]:
                                mm = pe.matmul(o, a, b_, start=False, stop=False)
                            if b == B - 1 and f in (2, 4):
                                mm.then_inc(s_used, 1)
                pe.wait_ge(s_mul, 4 * STEPS * i + 4 * STEPS)
                pe.wait_ge(s_red, STEPS * i + STEPS)
                tflat = ps[:, 4:7, :].rearrange("p b n -> p (b n)")
                for t in range(NT):
                    for f in range(KC):
                        ins = pe.transpose(tflat[:, t * F + f * P:t * F + (f + 1) * P],
                                           qiT[:, f, t * P:(t + 1) * P], ident[:])
                ins.then_inc(s_tr, 1)
                pe.wait_ge(s_wlo, 3 * (U + 6) + 3)
                pe.wait_ge(s_qilo, 6 * i + 6)
                for t in range(NT):
                    for n, (o, a, b_) in enumerate(parts(1, KC - 1, t, slab_chunk(KC - 1))):
                        mm = pe.matmul(o, a, b_, start=False, stop=(n >= 4))
                    mm.then_inc(s_out if t == 0 else s_used, 1)

            pe.wait_ge(s_acount, 2)
            for r in range(R4):
                for t in range(NT):
                    ins = pe.matmul(ps[:, 4 + r // 2, (r % 2) * N:(r % 2 + 1) * N], ones[:], A4[:, t, r, :],
                                    start=(t == 0), stop=(t == 1))
            ins.then_inc(s_deg, 1)
            pe.wait_ge(s_rinv, 2)

            def layer1(i, last):
                T = 15 * i + 30
                U = 5 * i + 15
                pe.wait_ge(s_H, 2 * i + 12)
                transposed(H, s_yt)
                pe.wait_ge(s_h, 2 * i + 8)
                aggregate(A4, 0, T)
                for v in range(5):
                    last_unit[0] = v == 4
                    product(U + v, v % 2, T + 3 * v, ((3, 0) if last else (2, i)) if v == 0 else None)
                    if v < 3:
                        aggregate(A4, v + 1, T + 3 * (v + 1))
                last_unit[0] = False

            with pe.Fori(0, 2) as i:
                layer1(i, False)
            layer1(2, True)

            pe.wait_ge(s_cnt, 1)
            for t in range(NT):
                for u in range(NT):
                    ins = pe.transpose(ps[:, 4, t * N + u * P:t * N + (u + 1) * P],
                                       cnt[:, 1, u, t * P:(t + 1) * P], ident[:])
            ins.then_inc(s_cntT, 1)
            pe.wait_ge(s_cnt, 2)

            def project(q):
                chunks, w, off, unit = PROJ[q]
                pe.wait_ge(p_H, 2 * q + 2)
                if q > 0:
                    pe.wait_ge(p_lo, PTILE[q])
                transposed(H, p_t, chunks)
                cols = ((0, 0, w),) if w <= 512 else ((0, 0, FH), (1, FH, FH))
                pe.wait_ge(s_wlo, 3 * unit + 3)
                for k in range(chunks):
                    if k % 2 == 0:
                        pe.wait_ge(p_lo, PTILE[q] + k // 2 + 1)
                    for t in range(NT):
                        ms = parts(0, k, t, lambda Wx, c0, n: Wx[:].rearrange("p j f -> p (j f)")[:, off + k * w + c0:off + k * w + c0 + n], cols)
                        for n, (o, a, b_) in enumerate(ms):
                            mm = pe.matmul(o, a, b_, start=(k == 0 and n < len(cols)), 
                                           stop=(k == chunks - 1 and n >= 2 * len(cols)))
                        if k == chunks - 1:
                            mm.then_inc(p_out, 1)

            def gat(g):
                hn, c, _, _, _ = GAT[g]
                pe.wait_ge(g_al, g + 1)
                for k, c0 in ((0, 0), (1, hn)):
                    for t in range(NT):
                        ins = pe.transpose(ps[0:hn, 4, k * N + t * P:k * N + (t + 1) * P],
                                           small[:, 64 + t * 16 + c0:64 + t * 16 + c0 + hn], ident[:])
                ins.then_inc(g_alT, 1)
                w = hn * N
                pieces = [(o, min(512, w - o)) for o in range(0, w, 512)]
                pe.wait_ge(g_blkS, g + 1)
                for o, n in pieces:
                    ins = pe.matmul(ps[:, 4 + o // 512, 0:n], onesf[0:hn, :], blkS[0:hn, o:o + n], start=True, stop=True)
                ins.then_inc(g_ms, 1)
                pe.wait_ge(g_m, g + 1)
                for t in range(NT):
                    ins = pe.transpose(ps[0:hn, 4, t * P:(t + 1) * P], small[:, 96 + t * 8:96 + t * 8 + hn], ident[:])
                ins.then_inc(g_mT, 1)
                pe.wait_ge(g_blk, g + 1)
                pe.wait_ge(g_h, 2 * g + 2)
                for o, n in pieces:
                    pe.matmul(ps[:, o // 512, 0:n], onesf[0:hn, :], blkM[0:hn, o:o + n], start=True, stop=True)
                for o, n in pieces:
                    ins = pe.matmul(ps[:, 4 + o // 512, 0:n], onesf[0:hn, :], blkD[0:hn, o:o + n], start=True, stop=True)
                ins.then_inc(g_bc, 1)
                pe.wait_ge(g_p, 2 * g + 2)
                hv = hau[:, 0:NT * hn * (c + 1)].rearrange("p (t h c) -> p t h c", t=NT, h=hn)
                for d in range(NT):
                    if c == F:
                        todo = [(ps[:, 2 * d + u, 0:FH + u], 0, u * FH, (u + 1) * FH + u) for u in range(2)]
                    else:
                        per = max(1, hn // 2)
                        todo = [(ps[:, 2 * d + h // per, (h % per) * (c + 1):(h % per + 1) * (c + 1)], h, 0, c + 1)
                                for h in range(hn)]
                    for o, h, c0, c1 in todo:
                        for t in range(NT):
                            ins = pe.matmul(o, zb[:, t, h * N + d * P:h * N + (d + 1) * P], hv[:, t, h, c0:c1],
                                            start=(t == 0), stop=(t == 1))
                    ins.then_inc(g_o, 1)

            project(0)
            gat(0)
            project(1)
            gat(1)
            project(2)
            project(3)
            project(4)
            gat(2)
            project(5)
            gat(3)

        @block.vector
        def _(dve):
            ch = Chain(dve, s_chain)
            TT = dve.tensor_tensor

            def norm(src, n):
                for t in range(NT):
                    for h in range(2):
                        ins = dve.bn_stats(small[:, 12 * t + 6 * h:12 * t + 6 * h + 6], src[:, t, h * FH:(h + 1) * FH])
                ch.step(ins)
                for t in range(NT):
                    ins = dve.bn_aggr(small[:, 24 + 2 * t:26 + 2 * t],
                                      small[:, 12 * t:12 * t + 12])
                ch.step(ins)
                mv = small[:, 24:28].rearrange("p (t s) -> p t s", t=NT)
                dve.tensor_scalar(small[:, 44:46], mv[:, :, 1], EPS, None, ALU.add).then_inc(s_var, 1)
                dve.wait_ge(s_rstd, n + 1)
                for t in range(NT):
                    dve.tensor_scalar(H[:, t, :], src[:, t, :], small[:, 24 + 2 * t:25 + 2 * t], small[:, 48 + t:49 + t],
                                      ALU.subtract, ALU.mult).then_inc(s_norm, 1)

            def h_lo(n):
                for t in range(NT):
                    dve.wait_ge(s_hhi, n + (t + 1))
                    TT(Hl[:, t, :], H[:, t, :], Hh[:, t, :], ALU.subtract).then_inc(s_h, 1)

            def yt_lo_tile(T, slot, j):
                dve.wait_ge(s_ythi, T + (j + 1))
                TT(YTl[:, slot, 2 * j:2 * j + 2, :], tile3(j), YTh[:, slot, 2 * j:2 * j + 2, :],
                   ALU.subtract).then_inc(s_ytlo, 1)

            def yt_root(T):
                for j in range(3):
                    yt_lo_tile(T, 0, j)

            def yt_relation(T, slot, rinv, r):
                for j in range(4):
                    if j < 3:
                        dve.wait_ge(s_yt, T + (j + 1))
                        TT(tile3(j), tile3(j), rinv[:, r, :].unsqueeze(1).broadcast_to([P, 2, N]),
                           ALU.mult).then_inc(s_scale, 1)
                    if j > 0:
                        yt_lo_tile(T, slot, j - 1)

            dve.wait_ge(s_const, 16)
            dve.tensor_copy(ident[:], const_in[:, C_ID:C_ID + P])
            dve.tensor_copy(iota[:], const_in[:, C_IOTA:C_IOTA + N])
            dve.tensor_copy(ones[:], const_in[:, C_ONES:C_ONES + P])
            dve.tensor_copy(onesf[:], const_in[0:8, C_ONES:C_ONES + P])
            dve.tensor_copy(SEL[:].rearrange("p a b -> p (a b)"), const_in[:, C_SEL:C_SEL + 1024])
            dve.tensor_copy(selb[:].rearrange("p a b -> p (a b)"), const_in[:, C_SELB:C_SELB + 4 * P])
            dve.wait_ge(s_bias, 16)
            ch.step(dve.tensor_scalar(Bias[:], const_in[:, 0:2 * F], 0.0, None, ALU.mult))
            ch.step(dve.tensor_copy(Bias[0:BIAS_ROWS, :], bias_in[:]))
            TT(Bias[32:32 + BIAS_ROWS, :], bias_in[:], Bias[0:BIAS_ROWS, :], ALU.subtract).then_inc(s_cst, 1)

            dve.wait_ge(s_edge, 16)
            ef = lambda k: edge_f[:, k, :]
            dve.tensor_copy(ef(0), edge_i[:, 0, :])
            ch.step(dve.tensor_copy(ef(1), edge_i[:, 1, :]))
            step2 = float(1 << SHIFT)
            tmp = small[:, 64:64 + EC]
            for k, col, t0 in ((2, 2, 0), (3, 3, 0), (4, 3, 2)):
                ch.step(dve.tensor_scalar(tmp, edge_i[:, col, :], float(t0 + 1), step2, ALU.is_equal, ALU.mult))
                ch.step(dve.scalar_tensor_tensor(out=ef(k), in0=edge_i[:, col, :], scalar=float(t0), in1=tmp,
                                                 op0=ALU.is_equal, op1=ALU.add))
            for t in range(2):
                dve.wait_ge(s_qhi, t + 1)
                TT(YTl[:, t, :, :], qTf[:, :, t * N:(t + 1) * N], YTh[:, t, :, :], ALU.subtract).then_inc(s_qlo, 1)
            dve.wait_ge(s_x, 16)
            norm(H, 0)

            def onehots(c, slot, wait):
                if wait is not None:
                    dve.wait_ge(s_adj, wait)
                col = lambda k: (edge_f[:, k, c:c + 1] if isinstance(c, int) else edge_f[:, k, bass.DynSlice(c, 1)])
                dve.tensor_scalar(OH[:, slot, :], iota[:], col(0), None, ALU.is_equal)
                for k in range(3):
                    ins = dve.tensor_scalar(V[:, slot, k * N:(k + 1) * N], iota[:], col(1), col(2 + k),
                                            ALU.is_equal, ALU.mult)
                ins.then_inc(s_oh, 1)

            def decode(h):
                dve.wait_ge(s_adj, EC0 if h == 0 else EC)
                for t in range(NT):
                    ch.step(dve.tensor_copy(halves(dec_lo[:]), ps[:, 4 + 2 * t:6 + 2 * t, 0:FH]))
                    ch.step(dve.tensor_scalar(dec_hi[:], dec_lo[:], SHIFT, None, ALU.logical_shift_right))
                    ch.step(dve.tensor_scalar(dec_lo[:], dec_lo[:], (1 << SHIFT) - 1, None, ALU.bitwise_and))
                    lo3 = dec_lo[:].rearrange("p (k n) -> p k n", k=3)
                    hi3 = dec_hi[:].rearrange("p (k n) -> p k n", k=3)
                    if h == 0:
                        dve.tensor_copy(acc[:, t, 0:3, :], lo3)
                        ins = dve.tensor_copy(acc[:, t, 3:6, :], hi3)
                        if t == 0:
                            ch.step(ins)
                        else:
                            ins.then_inc(s_dec, 1)
                            dve.wait_ge(s_dec, 1)
                    else:
                        TT(acc[:, t, 0:3, :], acc[:, t, 0:3, :], lo3, ALU.add)
                        ch.step(TT(acc[:, t, 3:6, :], acc[:, t, 3:6, :], hi3, ALU.add))

            for c in range(2):
                onehots(c, c, None)
            with dve.Fori(1, EC0 // 2) as i:
                for u in range(2):
                    onehots(2 * i + u, u, 2 * i + (u - 1))
            decode(0)

            def qg_lo(t):
                for k in range(8 * t, 8 * t + 8):
                    u, g = k % 8 // 4, k % 4
                    dve.wait_ge(s_qghi, k + 1)
                    TT(halves(Z[96:128, k, :]), ps[32 * g:32 * g + 32, 2 * u:2 * u + 2, 0:FH], halves(Z[64:96, k, :]),
                       ALU.subtract).then_inc(s_qglo, 1)

            qg_lo(0)
            with dve.Fori(EC0 // 2, EC // 2) as i:
                for u in range(2):
                    onehots(2 * i + u, u, 2 * i + (u - 1))
            decode(1)
            for r, pl in ((0, 0), (1, 3)):
                dve.tensor_copy(A3[:, :, r, :], acc[:, :, pl, :])
            for r, pl in ((0, 1), (1, 4), (2, 2), (3, 5)):
                dve.tensor_copy(A4i[:, :, r, :], acc[:, :, pl, :])
            td = dec_lo[:, 0:512].bitcast(F32).rearrange("p (t n) -> p t n", t=NT)
            ch.step(TT(td, acc[:, :, 1, :], acc[:, :, 4, :], ALU.add))
            for pl, op in ((2, ALU.add), (5, ALU.add), (0, ALU.subtract)):
                ch.step(TT(td, td, acc[:, :, pl, :], op))
            TT(A3[:, :, 2, :], td, acc[:, :, 3, :], ALU.subtract).then_inc(s_acount, 1)
            dve.wait_ge(s_deg, 1)
            ch.step(dve.tensor_scalar(rinv3[:, 0:2, :], ps[:, 4, :].rearrange("p (r n) -> p r n", r=2), 1.0, None, ALU.max))
            ch.step(dve.tensor_scalar(rinv3[:, 2, :], ps[:, 5, 0:N], 1.0, None, ALU.max))
            dve.reciprocal(rinv3[:], rinv3[:]).then_inc(s_rinv, 1)
            dve.wait_ge(s_rinv, 1)
            qg_lo(1)
            h_lo(0)

            with dve.Fori(0, 2) as i:
                T = 15 * i
                yt_root(T)
                for v in range(1, 4):
                    yt_relation(T + 3 * v, v % 2, rinv3, v - 1)
                yt_root(T + 12)

                def hg_lo(b):
                    dve.wait_ge(s_hghi, 8 * i + (b + 1))
                    for lh in range(2):
                        ins = TT(halves(Z[32:64, 2 * b + lh, :]),
                                 ps[32 * (b % 4):32 * (b % 4) + 32, 2 * (b // 4):2 * (b // 4) + 2, 0:FH],
                                 halves(Z[0:32, 2 * b + lh, :]), ALU.subtract)
                    ins.then_inc(s_hglo, 1)

                hg_lo(0)

                def reduce(st):
                    f, b = st // B, st % B
                    dve.wait_ge(s_add, STEPS * i + (st + 1))
                    dve.tensor_reduce(qiT[:, f, b * NB:(b + 1) * NB], S[:, st % 2, :].rearrange("p (n l) -> p n l", l=LH),
                                      AX.X, ALU.add).then_inc(s_red, 1)

                def qi_lo(f):
                    dve.wait_ge(s_qihi, 6 * i + (f + 1))
                    TT(YTl[:, 1, f, :], qiT[:, f, :], YTh[:, 1, f, :], ALU.subtract).then_inc(s_qilo, 1)

                for st in range(STEPS):
                    f, b = st // B, st % B
                    if st < B // 2:
                        for b2 in range(2 * st + 1, min(2 * st + 3, B)):
                            hg_lo(b2)
                    if st >= 2:
                        dve.wait_ge(s_add, STEPS * i + (st - 1))
                    for t in range(ZT):
                        dve.wait_ge(s_sig, 4 * STEPS * i + (4 * st + t + 1))
                        l0 = b * L + (t // 2) * LH
                        TT(PR[:, st % 2, t * 512:(t + 1) * 512].rearrange("p (n l) -> p n l", l=LH),
                           ps[:, 4 + t, :].rearrange("p (n l) -> p n l", l=LH),
                           qTf[:, f, l0:l0 + LH].unsqueeze(1).broadcast_to([P, NB // 2, LH]), ALU.mult).then_inc(s_mul, 1)
                    if st >= 1:
                        reduce(st - 1)
                    if f > 0 and b == 2:
                        qi_lo(f - 1)
                reduce(STEPS - 1)
                qi_lo(KC - 1)
                for t in range(NT):
                    dve.wait_ge(s_tanh, 2 * i + (t + 1))
                    TT(tq[:, t, :], tq[:, t, :], H[:, t, :], ALU.subtract).then_inc(s_gate1, 1)
                for t in range(NT):
                    dve.wait_ge(s_gate1, 2 * i + (t + 1))
                    dve.wait_ge(s_alpha, 2 * i + (t + 1))
                    TT(tq[:, t, :], tq[:, t, :], alpha[:, t, :], ALU.mult).then_inc(s_gate2, 1)
                for t in range(NT):
                    dve.wait_ge(s_gate2, 2 * i + (t + 1))
                    TT(H[:, t, :], H[:, t, :], tq[:, t, :], ALU.add).then_inc(s_H, 1)
                h_lo(2 * i + 2)

            dve.wait_ge(s_x2, 16)
            ch.step(TT(X[:], X[:], H[:], ALU.add))
            norm(X, 1)
            dve.tensor_copy(A4[:], A4i[:]).then_inc(s_acount, 1)
            dve.wait_ge(s_deg, 2)
            ch.step(dve.tensor_scalar(rinv4[:].rearrange("p (b r) n -> p b (r n)", b=2), ps[:, 4:6, :], 1.0, None, ALU.max))
            dve.reciprocal(rinv4[:], rinv4[:]).then_inc(s_rinv, 1)
            dve.wait_ge(s_rinv, 2)
            h_lo(6)

            def layer1(i):
                T = 15 * i + 30
                yt_root(T)
                for v in range(1, 5):
                    yt_relation(T + 3 * v, v % 2, rinv4, v - 1)

            with dve.Fori(0, 2) as i:
                layer1(i)
                h_lo(2 * i + 8)
            layer1(2)
            for t in range(NT):
                wait_out(dve, 11, t, 29)
                TT(halves(X[:, t, :]), halves(X[:, t, :]), two_banks(t), ALU.add).then_inc(s_res, 1)
            dve.wait_ge(s_res, 2)
            norm(X, 2)
            dve.wait_ge(s_rinv, 2)
            ch.step(TT(cnt[:, 1, :, :], A4i[:, :, 0, :], A4i[:, :, 1, :], ALU.add))
            ch.step(TT(cnt[:, 1, :, :], cnt[:, 1, :, :], A4i[:, :, 2, :], ALU.add))
            ch.step(TT(cnt[:, 1, :, :], cnt[:, 1, :, :], A4i[:, :, 3, :], ALU.add))
            ch.step(dve.tensor_copy(cnt[:, 0, :, :], cnt[:, 1, :, :]))
            for t in range(NT):
                ins = TT(cnt[:, 0, t, t * P:(t + 1) * P], cnt[:, 0, t, t * P:(t + 1) * P], ident[:], ALU.add)
            ins.then_inc(s_cnt, 1)
            dve.wait_ge(s_cntT, 1)
            cT = ps[:, 4, :].rearrange("p (t n) -> p t n", t=NT)
            ch.step(dve.tensor_copy(neg[:, 0, :, :], cT))
            for t in range(NT):
                ins = TT(neg[:, 0, t, t * P:(t + 1) * P], neg[:, 0, t, t * P:(t + 1) * P], ident[:], ALU.add)
            ch.step(ins)
            dve.tensor_scalar(neg[:, 1, :, :], cT, 0.0, NEG, ALU.is_equal, ALU.mult)
            dve.tensor_scalar(neg[:, 0, :, :], neg[:, 0, :, :], 0.0, NEG, ALU.is_equal, ALU.mult).then_inc(s_cnt, 1)
            dve.wait_ge(s_cnt, 2)
            dve.wait_ge(s_gv, 32)

            def proj_lo(q):
                for j in range(PTILE[q + 1] - PTILE[q]):
                    dve.wait_ge(p_hi, PTILE[q] + j + 1)
                    TT(YTl[:, 0, 2 * j:2 * j + 2, :], tile3(j), YTh[:, 0, 2 * j:2 * j + 2, :],
                       ALU.subtract).then_inc(p_lo, 1)

            def gat(g, self_loop):
                hn, c, o_s, o_d, o_b = GAT[g]
                hc, w = hn * c, hn * N
                hv = hau[:, 0:NT * hn * (c + 1)].rearrange("p (t h c) -> p t h c", t=NT, h=hn)
                dve.wait_ge(g_h, 2 * g + 2)
                ch.step(dve.memset(hv[:, :, :, c:c + 1], 1.0))
                for t in range(NT):
                    for k, o in ((0, o_s), (1, o_d)):
                        tv = gtmp[:, 0:hc].rearrange("p (h c) -> p h c", h=hn)
                        ch.step(TT(tv, hv[:, t, :, 0:c], av[:, o:o + hc].rearrange("p (h c) -> p h c", h=hn), ALU.mult))
                        ins = dve.tensor_reduce(small[:, 64 + 16 * t + k * hn:64 + 16 * t + k * hn + hn], tv,
                                                AX.X, ALU.add)
                        if (t, k) == (NT - 1, 1):
                            ins.then_inc(g_al, 1)
                            dve.wait_ge(g_al, g + 1)
                        else:
                            ch.step(ins)
                dve.wait_ge(g_alT, g + 1)
                mask = ident[0:hn, 0:hn].unsqueeze(2).broadcast_to([hn, hn, N])

                def blocks(dst, rows):
                    return TT(dst[0:hn, 0:w].rearrange("p (h n) -> p h n", h=hn),
                              rows.unsqueeze(1).broadcast_to([hn, hn, N]), mask, ALU.mult)

                ch.step(dve.tensor_copy(ald_sb[0:hn, :], ps[0:hn, 4, N:2 * N]))
                blocks(blkS, ps[0:hn, 4, 0:N]).then_inc(g_blkS, 1)
                dve.wait_ge(g_ms, g + 1)
                nb_ = (w + 511) // 512
                for t in range(NT):
                    srcs = ps[:, 4:4 + nb_, 0:min(512, w)]
                    if hn > 1:
                        a = srcs.rearrange("p b (h n) -> p (b h) n", n=N)
                    else:
                        a = srcs
                    tv = gtmp[:, 0:w].rearrange("p (h n) -> p h n", h=hn)
                    ch.step(TT(tv, a, neg[:, self_loop, t, :].unsqueeze(1).broadcast_to([P, hn, N]), ALU.add))
                    ch.step(dve.tensor_reduce(small[:, 96 + 8 * t:96 + 8 * t + hn], tv, AX.X, ALU.max))
                mx = small[:, 96:112].rearrange("p (t h) -> p t h", t=NT)[:, :, 0:hn]
                ald = small[:, 64:96].rearrange("p (t h) -> p t h", t=NT)[:, :, hn:2 * hn]
                ch.step(TT(mx, mx, ald, ALU.add))
                dve.scalar_tensor_tensor(out=mx, in0=mx, scalar=SLOPE, in1=mx, op0=ALU.mult, op1=ALU.max).then_inc(g_m, 1)
                dve.wait_ge(g_mT, g + 1)
                blocks(blkD, ald_sb[0:hn, :])
                blocks(blkM, ps[0:hn, 4, 0:N]).then_inc(g_blk, 1)
                dve.wait_ge(g_bc, g + 1)
                for t in range(NT):
                    zt = zb[:, t, 0:w]
                    z3 = zt.rearrange("p (h n) -> p h n", h=hn)
                    pd = ps[:, 4:4 + nb_, 0:min(512, w)]
                    pm = ps[:, 0:nb_, 0:min(512, w)]
                    if hn > 1:
                        pd = pd.rearrange("p b (h n) -> p (b h) n", n=N)
                    als = small[:, 64 + 16 * t:64 + 16 * t + hn].unsqueeze(2).broadcast_to([P, hn, N])
                    ch.step(TT(z3, pd, als, ALU.add))
                    ch.step(dve.scalar_tensor_tensor(out=zt, in0=zt, scalar=SLOPE, in1=zt, op0=ALU.mult, op1=ALU.max))
                    TT(zt.rearrange("p (b n) -> p b n", b=nb_), zt.rearrange("p (b n) -> p b n", b=nb_), pm,
                       ALU.subtract).then_inc(g_sub, 1)
                for t in range(NT):
                    z3 = zb[:, t, 0:w].rearrange("p (h n) -> p h n", h=hn)
                    dve.wait_ge(g_ex, 2 * g + t + 1)
                    TT(z3, z3, cnt[:, self_loop, t, :].unsqueeze(1).broadcast_to([P, hn, N]), ALU.mult).then_inc(g_p, 1)
                for t in range(NT):
                    dve.wait_ge(g_o, 2 * g + t + 1)
                    rd = small[:, 52:52 + hn]
                    if c == F:
                        ch.step(dve.tensor_scalar(rd, ps[:, 2 * t + 1, FH:FH + 1], 1e-16, None, ALU.add))
                        ch.step(dve.reciprocal(rd, rd))
                        ch.step(dve.tensor_scalar(halves(gout[:, t, :]), two_banks(t), rd, None, ALU.mult))
                    else:
                        per = max(1, hn // 2)
                        nbk = 1 if hn == 1 else 2
                        for u in range(nbk):
                            pv = ps[:, 2 * t + u, 0:per * (c + 1)].rearrange("p (h c) -> p h c", h=per)
                            r_ = small[:, 52 + u * per:52 + (u + 1) * per]
                            ch.step(dve.tensor_scalar(r_, pv[:, :, c], 1e-16, None, ALU.add))
                            ch.step(dve.reciprocal(r_, r_))
                            ch.step(TT(gout[:, t, u * per * c:(u + 1) * per * c].rearrange("p (h c) -> p h c", h=per),
                                       pv[:, :, 0:c], r_.unsqueeze(2).broadcast_to([P, per, c]), ALU.mult))
                    ch.step(TT(gout[:, t, 0:hc], gout[:, t, 0:hc], gb[:, o_b:o_b + hc], ALU.add))

            def relu_to_h(hc):
                for t in range(NT):
                    dve.tensor_scalar(H[:, t, 0:hc], gout[:, t, 0:hc], 0.0, None, ALU.max).then_inc(p_H, 1)

            proj_lo(0)
            gat(0, 0)
            relu_to_h(256)
            proj_lo(1)
            gat(1, 0)
            relu_to_h(256)
            proj_lo(2)
            for t in range(NT):
                dve.wait_ge(p_out, 4 + t + 1)
                ch.step(TT(gout[:, t, 0:256], ps[:, 2 * t, 0:256], gb[:, GB_M1:GB_M1 + 256], ALU.add))
            relu_to_h(256)
            proj_lo(3)
            for t in range(NT):
                dve.wait_ge(p_out, 6 + t + 1)
                ch.step(TT(halves(gout[:, t, :]), two_banks(t), halves(gb[:, GB_M2:GB_M2 + F]), ALU.add))
            ch.step(TT(X[:], X[:], gout[:], ALU.add))
            norm(X, 3)
            proj_lo(4)
            gat(2, 1)
            dve.tensor_scalar(elu_t[:], gout[:], 0.0, None, ALU.min).then_inc(g_el, 2)
            ch.step(dve.tensor_scalar(H[:], gout[:], 0.0, None, ALU.max))
            dve.wait_ge(g_ex2, 1)
            for t in range(NT):
                dve.scalar_tensor_tensor(out=H[:, t, :], in0=elu_t[:, t, :], scalar=-1.0, in1=H[:, t, :],
                                         op0=ALU.add, op1=ALU.add).then_inc(p_H, 1)
            proj_lo(5)
            gat(3, 1)
            for t in range(NT):
                TT(X[:, t, :], X[:, t, :], gout[:, t, :], ALU.add).then_inc(s_fin, 1)


def kernel(**inputs):
    import numpy as np
    import concourse.bacc as bacc
    from concourse.bass_utils import run_bass_kernel_spmd

    a = {k: np.asarray(v) for k, v in inputs.items()}

    def unit(w):
        return w.reshape(KC, P, F).transpose(1, 0, 2).reshape(P, 3, 2 * F)

    wg, wq = a["L0_gnn_Wg"], a["L0_gnn_Wq"]
    units = [unit(wg[:, F:].T)]
    for n in "12":
        units.append(unit(a["L0_gnn_W_root" + n]))
        units += [unit(w) for w in a["L0_gnn_W_rel" + n]]
        units += [unit(wg[:, :F].T), unit(wq[:, :F].T), unit(wq[:, F:].T)]
    for n in "123":
        units.append(unit(a["L1_gnn_root" + n]))
        units += [unit(w) for w in a["L1_gnn_W" + n]]
    small_w = [a["L2_gnn_" + n] for n in ("W1", "W2", "Wm1", "Wm2")]
    small_w = [w.reshape(-1, P, w.shape[1]).transpose(1, 0, 2).reshape(P, -1) for w in small_w]
    used = sum(w.shape[1] for w in small_w)
    small_w.append(np.zeros((P, KC * F - used), np.float32))
    units.append(np.concatenate(small_w, axis=1).reshape(P, 3, 2 * F))
    units += [unit(a["L3_gnn_W1"]), unit(a["L3_gnn_W2"])]

    consts = np.zeros((P, C_ALL), np.float32)
    row = np.arange(P)
    consts[:, C_ID:C_ID + P] = np.eye(P)
    consts[:, C_IOTA:C_IOTA + N] = np.arange(N)
    consts[:, C_ONES:C_ONES + P] = 1.0
    n_of = np.arange(2 * 512) // LH
    l_of = np.arange(2 * 512) % LH
    consts[:64, C_SEL:C_SEL + 1024] = row[:64, None] % 32 == n_of[None]
    consts[64:, C_SEL:C_SEL + 1024] = row[64:, None] % 32 == l_of[None]
    for k in range(4):
        consts[[k, 32 + k], C_SELB + k * P:C_SELB + (k + 1) * P] = 1.0

    arrays = {
        "x": a["x"],
        "edges": np.stack([a["src"], a["dst"], a["edge_type_3"], a["edge_type_4"]]).reshape(4, EC, P).transpose(2, 0, 1),
        "queries": a["L0_gnn_query_embs"].reshape(B * L, F).T.reshape(KC, P, B * L).transpose(1, 0, 2),
        "consts": consts,
        "biases": np.stack([np.concatenate([a[m], a[n]]) for m, n in (
            ("L0_gnn_b1", "L0_gnn_b2"), ("L0_gnn_bq", "L0_gnn_bq"), ("L1_gnn_b1", "L1_gnn_b2"), ("L1_gnn_b3", "L0_gnn_bg"))]),
        "gat_biases": np.concatenate([a[n] for n in ("L2_gnn_b1", "L2_gnn_b2", "L2_gnn_bm1", "L3_gnn_b1", "L3_gnn_b2",
                                                     "L2_gnn_bm2")]),
        "gat_vectors": np.concatenate([a[n].reshape(-1) for n in (
            "L2_gnn_a_src1", "L2_gnn_a_dst1", "L2_gnn_a_src2", "L2_gnn_a_dst2",
            "L3_gnn_a_src1", "L3_gnn_a_dst1", "L3_gnn_a_src2", "L3_gnn_a_dst2")]),
        "weights": np.stack(units),
    }
    nc = bacc.Bacc("TRN2", target_bir_lowering=False, num_devices=1)
    arrays = {n: np.ascontiguousarray(v) for n, v in arrays.items()}
    args = [nc.dram_tensor(n, v.shape, mybir.dt.from_np(v.dtype), kind="ExternalInput").ap() for n, v in arrays.items()]
    result = nc.dram_tensor("result", (N, F), F32, kind="ExternalOutput").ap()
    build(nc, *args, result)
    r = run_bass_kernel_spmd(nc, [arrays], core_ids=[0])
    return r.results[0]["result"]
```

```python
from contextlib import ExitStack

import concourse.bass as bass
from concourse import mybir

P = 128
N = 256
NT = N // P
F = 768
KC = F // P
FH = F // 2
E = 4352
EC = E // P
B, L = 8, 64
NB = N // B
LH = L // 2
R3, R4 = 3, 4
PACK = 4608.0
MID = 2048.0
ROUND = 1.5 * 2.0 ** 23
ZU = 2
FOLDED = [s % 5 in (1, 3) for s in range(KC * B)]
STEPS = KC * B
NU = 33
NEG = -1.0e30
EPS = 1e-5
SLOPE = 0.2

F32, F32R, BF16 = mybir.dt.float32, mybir.dt.float32r, mybir.dt.bfloat16
I32, I16 = mybir.dt.int32, mybir.dt.int16
ALU, ACT, AX = mybir.AluOpType, mybir.ActivationFunctionType, mybir.AxisListType

C_IOTA, C_P, C_P64, C_P32 = 0, N, N + 1, N + 2
C_ALL = N + 3
SLOTS = 8
PSLOTS = 3
SELK = 8
BIAS_ROWS = 4
GAT = [(4, 64, 0, 256, 0), (1, 256, 512, 768, 256), (8, 96, 1024, 1792, 768), (1, 768, 2560, 3328, 1536)]
GB_M1, GB_M2 = 512, 2304
PROJ = [(6, 256, 0, 30), (2, 256, 1536, 30), (2, 256, 2048, 30), (2, 768, 2560, 30), (6, 768, 0, 31), (6, 768, 0, 32)]
PTILE = [0, 3, 4, 5, 6, 9, 12]


class Chain:

    def __init__(self, eng, sem):
        self.eng, self.sem, self.n = eng, sem, 0

    def step(self, ins):
        self.n += 1
        ins.then_inc(self.sem, 1)
        self.eng.wait_ge(self.sem, self.n)


def build(nc, x, ei, qT, consts, brows, gbias, gavec, W, out):
    ctx = ExitStack()
    with ctx:
        at = [nc.sbuf_base]

        def place(size):
            o = (at[0] + 31) // 32 * 32
            at[0] = o + size
            return o

        def sb(name, shape, dt, off=None):
            size = 1
            for s in shape[1:]:
                size *= s
            size *= {F32: 4, F32R: 4, I32: 4, BF16: 2, I16: 2}[dt]
            o = place(size) if off is None else off
            return nc.alloc_sbuf_tensor_at(name, shape, dt, offset=o)

        def sem(name):
            return ctx.enter_context(nc.semaphore(name))

        ps = ctx.enter_context(nc.psum_tensor("ps", [P, 8, 512], F32))

        Wr = sb("w_raw", [P, 3, 2 * F], F32)
        Wh = sb("w_hi", [P, 3, 2 * F], F32R)
        Wl = sb("w_lo", [P, 3, 2 * F], F32R)
        y_off = place(12288)
        YTh = sb("yt_hi", [P, 2, KC, N], F32R, y_off)
        YTl = sb("yt_lo", [P, 2, KC, N], F32R)
        H = sb("h", [P, NT, F], F32)
        t_off = place(6144)
        qiT = sb("qi_t", [P, KC, N], F32, t_off)
        A3 = sb("a3", [P, NT, R3, N], F32R)
        A4i = sb("a4_i", [P, NT, R4, N], I16)
        deg3 = sb("deg3", [P, R3, N], I16)
        deg4 = sb("deg4", [P, R4, N], I16)
        rinv = sb("rinv", [P, N], F32, t_off)
        X = sb("x", [P, NT, F], F32)
        ident = sb("ident", [P, P], F32)
        ones = sb("ones", [P, P], F32R)
        identb = sb("ident_b", [P, P], BF16)
        SELn = sb("sel_node", [P, 2, 1024], F32R)
        SELl = sb("sel_query", [P, 2, 512], F32R)
        selb = sb("sel_row", [P, SELK, P], F32R)
        Bias = sb("bias", [P, 2 * F], F32R)
        q_off = place(12288)
        qTf = sb("q_t", [P, KC, B * L], F32, q_off)
        z_off = place(36864)
        HG = sb("hg", [P, B // 2, F], F32R, z_off)
        QG = sb("qg", [P, B, F], F32R, z_off + 4 * F * B // 2)
        g_off = place(24576)
        small = sb("small", [P, 128], F32)
        mhalf = sb("mhalf", [P, NT], F32)
        bias_in = sb("bias_in", [BIAS_ROWS, 2 * F], F32, z_off + 12288)
        edge_i = sb("edge_i", [P, 4, EC], I32, t_off)
        edge_f = sb("edge_f", [P, 5, EC], F32, t_off + 16 * EC)
        oh_off = (t_off + 36 * EC + 31) // 32 * 32
        iota = sb("iota", [P, N], BF16, oh_off)
        const_in = sb("const_in", [P, C_ALL], F32, oh_off + 1536)
        OH = sb("onehot_src", [P, SLOTS, N], BF16, g_off)
        V = sb("onehot_dst", [P, SLOTS, 3 * N], BF16, g_off + 2 * SLOTS * N)
        A4t = sb("a4_setup", [P, NT, R4, N], F32R, g_off + 8 * SLOTS * N)
        off_l = sb("offset_l", [P, P], BF16, oh_off + 512)
        off_r = sb("offset_r", [P, FH], BF16, oh_off + 768)
        other = sb("other_count", [P, NT, 3 * N], F32, z_off)
        rest = sb("rest_count", [P, NT, N], F32, z_off + 6144)
        Hh = sb("h_hi", [P, NT, F], F32R, g_off)
        Hl = sb("h_lo", [P, NT, F], F32R, g_off + 6144)
        PR = sb("prod", [P, PSLOTS, 2048], F32, g_off)
        alpha = sb("alpha", [P, NT, F], F32, g_off + 12288)
        tq = sb("tanh_q", [P, NT, F], F32, g_off + 18432)
        A4 = sb("a4", [P, NT, R4, N], F32R, z_off)
        hau = sb("h_aug", [P, 1568], F32, z_off)
        MR = sb("max_rows", [64, N], F32R, z_off + 6400)
        av = sb("a_vec", [P, 4096], F32, z_off + 8192)
        cnt = sb("count", [P, 2, NT, N], F32, z_off + 24576)
        noedge_d = sb("no_edge_dst", [P, 2, NT, N], BF16, z_off + 28672)
        noedge_s = sb("no_edge_src", [P, 2, NT, N], BF16, z_off + 30720)
        looped = sb("looped", [P, NT, N], F32, z_off + 32768)
        AR = sb("logit_rows", [64, 2, N], F32R, z_off + 34816)
        gb = sb("g_bias", [P, 3072], F32, q_off)
        zb = sb("attn", [P, 2, 2048], F32, g_off)
        gtmp = sb("gat_tmp", [P, 2048], F32, g_off + 16384)
        gout = sb("g_out", [P, NT, F], F32, y_off + 6144)
        elu_t = sb("elu_t", [P, NT, F], F32, g_off)

        s_const, s_edge, s_x, s_q, s_bias = (sem(n) for n in ("s_const", "s_edge", "s_x", "s_q", "s_bias"))
        s_raw = [sem(f"s_raw{j}") for j in range(3)]
        s_whi, s_wlo, s_used = sem("s_whi"), sem("s_wlo"), sem("s_used")
        s_cst = sem("s_cst")
        s_chain = sem("s_chain")
        s_achain = sem("s_achain")
        s_pchain = sem("s_pchain")
        s_var, s_rstd, s_norm = sem("s_var"), sem("s_rstd"), sem("s_norm")
        s_H, s_hhi, s_h = sem("s_H"), sem("s_hhi"), sem("s_h")
        s_yt, s_scale, s_ythi, s_ytlo = sem("s_yt"), sem("s_scale"), sem("s_ythi"), sem("s_ytlo")
        s_qhi, s_qlo = sem("s_qhi"), sem("s_qlo")
        s_out = sem("s_out")
        s_fold, s_brow, s_off, s_rv, s_a4t, s_a4 = (
            sem(n) for n in ("s_fold", "s_brow", "s_off", "s_rv", "s_a4t", "s_a4"))
        s_qghi, s_qglo = sem("s_qghi"), sem("s_qglo")
        s_oh, s_adj, s_acount, s_deg, s_rinv = sem("s_oh"), sem("s_adj"), sem("s_acount"), sem("s_deg"), sem("s_rinv")
        s_hghi, s_hglo = sem("s_hghi"), sem("s_hglo")
        s_gate1, s_gate2 = sem("s_gate1"), sem("s_gate2")
        s_z, s_sig, s_mul, s_add, s_red = sem("s_z"), sem("s_sig"), sem("s_mul"), sem("s_add"), sem("s_red")
        s_qihi, s_qilo, s_tr, s_tanh, s_alpha = (sem(n) for n in ("s_qihi", "s_qilo", "s_tr", "s_tanh", "s_alpha"))
        s_x2, s_res, s_gv = sem("s_x2"), sem("s_res"), sem("s_gv")
        s_cntT, s_cnt = sem("s_cntT"), sem("s_cnt")
        p_H, p_t, p_hi, p_lo, p_out, p_ev = (sem(n) for n in ("p_H", "p_t", "p_hi", "p_lo", "p_out", "p_ev"))
        g_h, g_ald, g_al, g_alT, g_ar, g_ms, g_m, g_mT, g_mr, g_zz, g_mm, g_sl, g_zr, g_sub, g_ex, g_p0, g_p1, g_o, g_el, g_ex2 = (
            sem(n) for n in ("g_h", "g_ald", "g_al", "g_alT", "g_ar", "g_ms", "g_m", "g_mT", "g_mr", "g_zz", "g_mm",
                             "g_sl", "g_zr", "g_sub", "g_ex", "g_p0", "g_p1", "g_o", "g_el", "g_ex2"))
        s_fin, s_store = sem("s_fin"), sem("s_store")

        block = ctx.enter_context(nc.Block())

        def nodes(ap):
            return ap.rearrange("(t p) f -> p t f", p=P)

        def two_banks(nt):
            return ps[:, 2 * nt:2 * nt + 2, 0:FH]

        def halves(ap):
            return ap.rearrange("p (h f) -> p h f", h=2)

        def tile3(j):
            return ps[:, 4 + j, :].rearrange("p (k n) -> p k n", k=2)

        def head_views(g):
            hn, c = GAT[g][:2]
            w = hn * N
            hv = hau[:, 0:NT * hn * (c + 1)].rearrange("p (t h c) -> p t h c", t=NT, h=hn)
            return hn, c, w, (w + 511) // 512, hv

        def logit_banks(g, t):
            wide = GAT[g][0] * N > 1024
            return (4, 0) if wide else (4 + 2 * t, 2 * t)

        def wait_out(eng, group, t, U):
            if t == 0:
                eng.wait_ge(s_out, group + 1)
            else:
                eng.wait_ge(s_used, 3 * U + 3)

        @block.sync
        def _(sp):
            def load_slab(U, j):
                sp.dma_start(Wr[:, j, :], W[U, :, j, :] if isinstance(U, int)
                             else W[bass.DynSlice(U, 1), :, j, :].rearrange("o p f -> p (o f)")).then_inc(s_raw[j], 16)

            sp.dma_start(const_in[:], consts).then_inc(s_const, 16)
            sp.dma_start(bias_in[:], brows).then_inc(s_bias, 16)
            for j in range(3):
                load_slab(0, j)
            with sp.Fori(1, NU) as U:
                for j in range(3):
                    sp.wait_ge(s_wlo, 3 * U + (j - 2))
                    load_slab(U, j)
            for t in range(NT):
                sp.wait_ge(s_fin, t + 1)
                sp.dma_start(nodes(out)[:, t, :], X[:, t, :]).then_inc(s_store, 16)
            sp.wait_ge(s_store, 16 * NT)

        @block.gpsimd
        def _(pool):
            ch = Chain(pool, s_pchain)

            def w_lo(U):
                for j in range(3):
                    w_lo_slab(U, j)

            def w_lo_slab(U, j):
                pool.wait_ge(s_whi, 3 * U + (j + 1))
                pool.tensor_tensor(Wl[:, j, :], Wr[:, j, :], Wh[:, j, :], ALU.subtract).then_inc(s_wlo, 1)

            def rstd(n):
                pool.wait_ge(s_var, n + 1)
                pool.tensor_tensor(small[:, 48:50], small[:, 44:46], mhalf[:], ALU.pow).then_inc(s_rstd, 1)

            pool.memset(off_l[:], MID / P)
            pool.memset(off_r[:], -PACK)
            pool.memset(mhalf[:], -0.5).then_inc(s_off, 1)
            pool.wait_ge(s_const, 16)

            def equal(out_, count, rest_, col):
                return pool.tensor_scalar(out_, count.broadcast_to(rest_), const_in[:, col:col + 1], None, ALU.is_equal)

            num = const_in[:, C_IOTA:C_IOTA + P]
            pool.tensor_scalar(ones[:], num, 0.0, 1.0, ALU.mult, ALU.add)
            pool.tensor_scalar(Bias[:], num[:, 0:1].broadcast_to([P, 2 * F]), 0.0, None, ALU.mult)
            equal(selb[:], num[:, 0:SELK].unsqueeze(2), [P, SELK, P], C_P32)
            pool.tensor_scalar(ident[:], num, const_in[:, C_P:C_P + 1], None, ALU.is_equal).then_inc(s_cst, 1)
            w_lo(0)
            rstd(0)
            for b in range(2):
                equal(SELn[:, b, :].rearrange("p (n l) -> p n l", l=LH), num[:, b * NB:(b + 1) * NB].unsqueeze(2),
                      [P, NB, LH], C_P64)
            for h in range(2):
                ins = equal(SELl[:, h, :].rearrange("p (n l) -> p n l", l=LH),
                            num[:, h * LH:(h + 1) * LH].unsqueeze(1), [P, NB // 2, LH], C_P64)
            ins.then_inc(s_cst, 1)
            w_lo(1)
            with pool.Fori(0, 2) as i:
                for v in range(1, 6):
                    w_lo(7 * i + (1 + v))
                for f in range(KC):
                    for b in range(B):
                        st = f * B + b
                        if f in (1, 2, 3) and b == 2:
                            w_lo_slab(7 * i + 7, f - 1)
                        if f in (3, 5) and b == 5:
                            w_lo_slab(7 * i + 8, (f - 3) // 2)
                        if st == STEPS - 1:
                            continue
                        pool.wait_ge(s_mul, ZU * (STEPS * i + (st + 1)))
                        sums = PR[:, st % PSLOTS, 0:1024]
                        ins = pool.tensor_tensor(sums, sums, PR[:, st % PSLOTS, 1024:2048], ALU.add)
                        if FOLDED[st]:
                            ins.then_inc(s_fold, 1)
                            pool.wait_ge(s_fold, sum(FOLDED) * i + sum(FOLDED[:st + 1]))
                            s3 = sums.rearrange("p (n l) -> p n l", l=LH)
                            ins = pool.tensor_tensor(s3[:, :, 0:LH // 2], s3[:, :, 0:LH // 2], s3[:, :, LH // 2:LH], ALU.add)
                        ins.then_inc(s_add, 1)
                w_lo_slab(7 * i + 8, 2)
            rstd(1)
            with pool.Fori(0, 3) as i:
                for v in range(5):
                    w_lo(5 * i + (16 + v))
            rstd(2)

            def attention(g):
                hn, c, w, _, hv = head_views(g)
                o_d, loop = GAT[g][3], g // 2
                pool.wait_ge(g_h, 2 * g + 2)
                if g > 0:
                    pool.wait_ge(g_o, 2 * g)
                pool.tensor_tensor(zb[:, 0, 0:NT * hn * c].rearrange("p (t h c) -> p t h c", t=NT, h=hn), hv[:, :, :, 0:c],
                                   av[:, o_d:o_d + hn * c].rearrange("p (h c) -> p h c", h=hn).unsqueeze(1).broadcast_to(
                                       [P, NT, hn, c]), ALU.mult).then_inc(g_ald, 1)
                pool.wait_ge(g_ex, 2 * g + 1)
                z3 = zb[:, 0, 0:w].rearrange("p (h n) -> p h n", h=hn)
                pool.tensor_tensor(z3, z3, cnt[:, loop, 0, :].unsqueeze(1).broadcast_to([P, hn, N]),
                                   ALU.mult).then_inc(g_p0, 1)

            pool.wait_ge(s_gv, 32)
            attention(0)
            attention(1)
            w_lo_slab(31, 0)
            rstd(3)
            w_lo_slab(31, 1)
            w_lo_slab(31, 2)
            attention(2)
            w_lo(32)
            attention(3)

        @block.scalar
        def _(act):
            ch = Chain(act, s_achain)

            def copy(o, i):
                return act.activation(o, i, ACT.Copy)

            def w_hi_slab(U, j, first=False):
                act.wait_ge(s_raw[j], 16 * U + 16)
                if not first:
                    act.wait_ge(s_used, 3 * U + (j - 2))
                copy(Wh[:, j, :], Wr[:, j, :]).then_inc(s_whi, 1)

            def w_hi_piece(U, j, n):
                if n == 0:
                    act.wait_ge(s_raw[j], 16 * U + 16)
                    act.wait_ge(s_used, 3 * U + (j - 2))
                c = slice(n * F, (n + 1) * F)
                ins = copy(Wh[:, j, c], Wr[:, j, c])
                if n == 1:
                    ins.then_inc(s_whi, 1)

            def w_hi(U, first=False):
                for j in range(3):
                    w_hi_slab(U, j, first)

            def yt_hi(T, slot, scaled=None):
                for j in range(3):
                    if scaled is None:
                        act.wait_ge(s_yt, T + (j + 1))
                    else:
                        act.wait_ge(s_scale, scaled + (j + 1))
                    copy(YTh[:, slot, 2 * j:2 * j + 2, :], tile3(j)).then_inc(s_ythi, 1)

            def relu_norm(n, h_sem):
                act.wait_ge(s_norm, 2 * n + 2)
                for t in range(NT):
                    act.activation(H[:, t, :], H[:, t, :], ACT.Relu).then_inc(h_sem, 1)

            def h_hi(n):
                act.wait_ge(s_H, n)
                for t in range(NT):
                    copy(Hh[:, t, :], H[:, t, :]).then_inc(s_hhi, 1)

            act.dma_start(edge_i[:], ei).then_inc(s_edge, 16)
            act.dma_start(qTf[:], qT).then_inc(s_q, 16)
            act.dma_start(X[:], nodes(x)).then_inc(s_x, 16)

            act.wait_ge(s_q, 16)
            for t in range(2):
                copy(YTh[:, t, :, :], qTf[:, :, t * N:(t + 1) * N]).then_inc(s_qhi, 1)
            w_hi(0, first=True)
            relu_norm(0, s_H)

            for t in range(2):
                for u in range(NT):
                    if t == 0:
                        act.wait_ge(s_out, u + 1)
                    else:
                        wait_out(act, 2, u, 0)
                    for g in range(2):
                        copy(halves(QG[0:64, 4 * t + 2 * u + g, :]), ps[64 * g:64 * g + 64, 2 * u:2 * u + 2, 0:FH]
                             ).then_inc(s_qghi, 1)
                if t == 0:
                    act.wait_ge(s_acount, 1)
                    copy(A4t[:], A4i[:]).then_inc(s_a4t, 1)
                    w_hi_slab(1, 0)
            for j in (1, 2):
                w_hi_slab(1, j)

            with act.Fori(0, 2) as i:
                yt_hi(15 * i, 0)
                h_hi(4 * i + 2)
                for v in range(4):
                    if v < 3:
                        yt_hi(None, (v + 1) % 2, 9 * i + 3 * v)
                    w_hi(7 * i + (2 + v))
                for t in range(NT):
                    wait_out(act, 3 * i + 3, t, 7 * i + 4)
                    act.activation(halves(H[:, t, :]), two_banks(t), ACT.Relu).then_inc(s_H, 1)
                yt_hi(15 * i + 12, 0)
                w_hi(7 * i + 6)

                def hg_hi(pair):
                    if pair % 2 == 0:
                        wait_out(act, 3 * i + 4, pair // 2, 7 * i + 5)
                    r = 64 * (pair % 2)
                    copy(halves(HG[0:64, pair, :]), ps[r:r + 64, 2 * (pair // 2):2 * (pair // 2) + 2, 0:FH]
                         ).then_inc(s_hghi, 1)

                hg_hi(0)
                hg_hi(1)
                for f in range(KC):
                    for b in range(B):
                        st = f * B + b
                        if st in (1, 3):
                            hg_hi(2 + st // 2)
                        for k in range(2 * ZU):
                            act.wait_ge(s_z, 2 * ZU * STEPS * i + (2 * ZU * st + k + 1))
                            act.activation(ps[:, 4 + k, :], ps[:, 4 + k, :], ACT.Sigmoid).then_inc(s_sig, 1)
                        if f in (1, 2, 3) and b < 2:
                            w_hi_piece(7 * i + 7, f - 1, b)
                        if f in (3, 5) and b in (3, 4):
                            w_hi_piece(7 * i + 8, (f - 3) // 2, b - 3)
                        if f > 0 and b == 2:
                            act.wait_ge(s_red, STEPS * i + B * f)
                            copy(YTh[:, 1, f - 1, :], qiT[:, f - 1, :]).then_inc(s_qihi, 1)
                act.wait_ge(s_red, STEPS * i + STEPS)
                copy(YTh[:, 1, KC - 1, :], qiT[:, KC - 1, :]).then_inc(s_qihi, 1)
                act.wait_ge(s_tr, i + 1)
                tflat = ps[:, 4:7, :].rearrange("p b n -> p (b n)")
                for t in range(NT):
                    act.activation(tq[:, t, :], tflat[:, t * F:(t + 1) * F], ACT.Tanh).then_inc(s_tanh, 1)
                for t in range(NT):
                    wait_out(act, 3 * i + 5, t, 7 * i + 7)
                    act.activation(halves(alpha[:, t, :]), two_banks(t), ACT.Sigmoid).then_inc(s_alpha, 1)
                w_hi_slab(7 * i + 8, 2)

            act.wait_ge(s_gate2, 4)
            act.dma_start(av[:], gavec.partition_broadcast(P)).then_inc(s_gv, 16)
            act.dma_start(gb[:], gbias.partition_broadcast(P)).then_inc(s_gv, 16)
            copy(A4[:], A4i[:]).then_inc(s_a4, 1)
            relu_norm(1, s_H)
            with act.Fori(0, 2) as i:
                yt_hi(15 * i + 30, 0)
                h_hi(2 * i + 12)
                for v in range(5):
                    if v < 4:
                        yt_hi(None, (v + 1) % 2, 12 * i + (18 + 3 * v))
                    w_hi(5 * i + (16 + v))
                for t in range(NT):
                    wait_out(act, i + 9, t, 5 * i + 19)
                    act.activation(halves(H[:, t, :]), two_banks(t), ACT.Relu).then_inc(s_H, 1)
            yt_hi(60, 0)
            h_hi(16)
            for v in range(5):
                if v < 4:
                    yt_hi(None, (v + 1) % 2, 42 + 3 * v)
                w_hi(26 + v)
            relu_norm(2, p_H)

            def proj_hi(q):
                for j in range(PTILE[q + 1] - PTILE[q]):
                    act.wait_ge(p_t, PTILE[q] + j + 1)
                    copy(YTh[:, 0, 2 * j:2 * j + 2, :], tile3(j)).then_inc(p_hi, 1)

            def gat(g, q):
                hn, c, _, _, _ = GAT[g]
                hv = hau[:, 0:NT * hn * (c + 1)].rearrange("p (t h c) -> p t h c", t=NT, h=hn)
                for t in range(NT):
                    act.wait_ge(p_out, 2 * q + t + 1)
                    if hn * c == F:
                        src = two_banks(t)
                        if hn == 1:
                            dst = halves(hv[:, t, 0, 0:c])
                            copy(dst, src).then_inc(g_h, 1)
                        else:
                            for u in range(2):
                                ins = copy(hv[:, t, 4 * u:4 * u + 4, 0:c],
                                           ps[:, 2 * t + u, 0:FH].rearrange("p (h c) -> p h c", c=c))
                            ins.then_inc(g_h, 1)
                    else:
                        copy(hv[:, t, :, 0:c], ps[:, 2 * t, 0:hn * c].rearrange("p (h c) -> p h c", c=c)).then_inc(g_h, 1)
                w, nb = hn * N, (hn * N + 511) // 512
                for t in range(NT):
                    zbank = logit_banks(g, t)[0]
                    act.wait_ge(g_zz, 2 * g + t + 1)
                    act.activation(zb[:, t, 0:w].rearrange("p (b n) -> p b n", b=nb), ps[:, zbank:zbank + nb, 0:min(512, w)],
                                   ACT.Copy, scale=SLOPE).then_inc(g_sl, 1)
                for t in range(NT):
                    act.wait_ge(g_sub, 2 * g + t + 1)
                    act.activation(zb[:, t, 0:w], zb[:, t, 0:w], ACT.Exp).then_inc(g_ex, 1)

            proj_hi(0)
            gat(0, 0)
            proj_hi(1)
            gat(1, 1)
            proj_hi(2)
            proj_hi(3)
            act.wait_ge(p_out, 8)
            w_hi(31, first=True)
            relu_norm(3, p_H)
            proj_hi(4)
            gat(2, 4)
            w_hi(32, first=True)
            act.wait_ge(g_el, 2)
            act.activation(elu_t[:], elu_t[:], ACT.Exp).then_inc(g_ex2, 1)
            proj_hi(5)
            gat(3, 5)

        @block.tensor
        def _(pe):
            def parts(slot, k, t, Wk, cols=((0, 0, FH), (1, FH, FH))):
                out_ = []
                for Y, Wx in ((YTh, Wh), (YTh, Wl), (YTl, Wh)):
                    for bank, c0, w in cols:
                        out_.append((ps[:, 2 * t + bank, 0:w], Y[:, slot, k, t * P:(t + 1) * P], Wk(Wx, c0, w)))
                return out_

            def slab_chunk(k):
                return lambda Wx, c0, w: Wx[:, k // 2, (k % 2) * F + c0:(k % 2) * F + c0 + w]

            def bias_mm(row, slot):
                for t in range(NT):
                    for h in range(2):
                        if isinstance(slot, int):
                            rhs = Bias[:, slot * F + h * FH:slot * F + (h + 1) * FH]
                        else:
                            rhs = Bias[:, bass.DynSlice(slot * F + h * FH, FH)]
                        pe.matmul(ps[:, 2 * t + h, 0:FH], selb[:, row, :], rhs, start=True, stop=False)

            def product(U, slot, ready, bias, release=True, fresh=False, between=None):
                if bias is not None:
                    bias_mm(*bias)
                def chunks(j, t, end):
                    for k in (2 * j, 2 * j + 1):
                        for n, (o, a, b_) in enumerate(parts(slot, k, t, slab_chunk(k))):
                            mm = pe.matmul(o, a, b_, start=(fresh and k == 0 and n < 2),
                                           stop=(end and k == KC - 1 and n >= 4))
                    return mm

                for j in range(3):
                    if between is not None and j == 2:
                        between()
                    pe.wait_ge(s_wlo, 3 * U + (j + 1))
                    if ready is not None:
                        pe.wait_ge(s_ytlo, ready + (j + 1))
                    for t in range(NT):
                        mm = chunks(j, t, last_unit[0])
                        if last_unit[0] and j == 2 and (t == 0 or not release):
                            mm.then_inc(s_out, 1)
                    if release:
                        mm.then_inc(s_used, 1)

            last_unit = [False]

            def transposed(src, sem_, src_ready, count, chunks=KC):
                for t in range(NT):
                    pe.wait_ge(src_ready, count - (1 - t))
                    for j in range(chunks // 2):
                        for kk in range(2):
                            k = 2 * j + kk
                            ins = pe.transpose(ps[:, 4 + j, kk * N + t * P:kk * N + (t + 1) * P],
                                               src[:, t, k * P:(k + 1) * P], ident[:])
                        if t == NT - 1:
                            ins.then_inc(sem_, 1)

            def aggregate(A, r, prev):
                for j in range(3):
                    pe.wait_ge(s_ytlo, prev + (j + 1))
                    for kk in range(2):
                        k = 2 * j + kk
                        n = 0
                        for t in range(NT):
                            for Hx in (Hh, Hl):
                                ins = pe.matmul(ps[:, 4 + j, kk * N:(kk + 1) * N], Hx[:, t, k * P:(k + 1) * P],
                                                A[:, t, r, :], start=(n == 0), stop=(n == 3))
                                n += 1
                    ins.then_inc(s_yt, 1)

            def count_chunk(slot, last, ready):
                pe.wait_ge(s_oh, ready)
                for t in range(NT):
                    for u in range(2):
                        ins = pe.matmul(ps[:, 4 + 2 * t + u, 0:FH], OH[:, slot, t * P:(t + 1) * P],
                                        V[:, slot, u * FH:(u + 1) * FH], start=False, stop=last)
                ins.then_inc(s_adj, 1)

            pe.wait_ge(s_off, 1)
            for k in range(4):
                pe.matmul(ps[:, 4 + k, 0:FH], off_l[:], off_r[:], start=True, stop=False)

            def count_group(i):
                for u in range(SLOTS):
                    count_chunk(u, False, SLOTS * i + (u + 1))

            with pe.Fori(0, 2) as i:
                count_group(i)
            last_unit[0] = True
            pe.wait_ge(s_brow, 1)
            pe.wait_ge(s_qlo, 1)
            product(0, 0, None, (3, 1), release=False)
            with pe.Fori(2, EC // SLOTS) as i:
                count_group(i)
            for c in range(EC // SLOTS * SLOTS, EC):
                count_chunk(c % SLOTS, c == EC - 1, c + 1)
            pe.wait_ge(s_qlo, 2)
            pe.wait_ge(s_qglo, 4)
            product(0, 1, None, (3, 1))
            last_unit[0] = False
            pe.wait_ge(s_acount, 1)
            for r, bank, c in ((0, 4, 0), (1, 4, N), (2, 5, 0)):
                for t in range(NT):
                    ins = pe.matmul(ps[:, bank, c:c + N], ones[:], A3[:, t, r, :], start=(t == 0), stop=(t == 1))
            pe.wait_ge(s_a4t, 1)
            for r in range(R4):
                for t in range(NT):
                    ins = pe.matmul(ps[:, 6 + r // 2, (r % 2) * N:(r % 2 + 1) * N], ones[:], A4t[:, t, r, :],
                                    start=(t == 0), stop=(t == 1))
            ins.then_inc(s_deg, 1)
            pe.wait_ge(s_rinv, 1)
            pe.wait_ge(s_cst, 2)

            with pe.Fori(0, 2) as i:
                T = 15 * i
                U = 7 * i + 1
                transposed(H, s_yt, s_H, 4 * i + 2)

                def first_sums():
                    pe.wait_ge(s_h, 2 * i + 2)
                    aggregate(A3, 0, T)

                pe.wait_ge(s_qglo, 8)
                for v in range(4):
                    last_unit[0] = v == 3
                    product(U + v, v % 2, T + 3 * v, (0, i) if v == 0 else None, between=first_sums if v == 0 else None)
                    if v < 2:
                        aggregate(A3, v + 1, T + 3 * (v + 1))
                transposed(H, s_yt, s_H, 4 * i + 4)
                last_unit[0] = True
                product(U + 4, 0, T + 12, None, fresh=True)
                last_unit[0] = False

                def gate_arguments(f, b, u):
                    k = ZU * (f * B + b) + u
                    if k >= ZU:
                        pe.wait_ge(s_mul, ZU * STEPS * i + (k - 1))
                    for h in range(2):
                        pe.matmul(ps[:, 4 + 2 * u + h, :], HG[:, b // 2, f * P:(f + 1) * P],
                                  SELn[:, b % 2, h * 512:(h + 1) * 512], start=True, stop=False)
                        pe.matmul(ps[:, 4 + 2 * u + h, :], QG[:, b, f * P:(f + 1) * P], SELl[:, u, :],
                                  start=False, stop=True).then_inc(s_z, 1)

                for f in range(KC):
                    hq = [m for kk in range(2) for t in range(NT) for m in parts(0, 2 * f + kk, t, slab_chunk(2 * f + kk))] \
                        if f < 3 else []
                    qq = [m for t in range(NT) for m in parts(1, f - 1, t, slab_chunk(f - 1))] if f > 0 else []
                    for b in range(B):
                        st = f * B + b
                        if f == 0:
                            pe.wait_ge(s_hglo, 4 * i + (b // 2 + 1))
                        gate_arguments(f, b, 0)
                        if f < 3 and (f > 0 or b >= 4):
                            if b == (4 if f == 0 else 0):
                                pe.wait_ge(s_wlo, 3 * (U + 5) + (f + 1))
                            if (f, b) == (0, 4):
                                pe.wait_ge(s_hglo, 4 * i + 4)
                                bias_mm(1, i)
                            for o, a, b_ in hq[3 * b:3 * b + 3] if f > 0 else hq[6 * (b - 4):6 * (b - 4) + 6]:
                                mm = pe.matmul(o, a, b_, start=False, stop=False)
                            if b == B - 1:
                                mm.then_inc(s_used, 1)
                        if f > 0 and b >= 4:
                            if b == 4:
                                pe.wait_ge(s_wlo, 3 * (U + 6) + ((f - 1) // 2 + 1))
                                pe.wait_ge(s_qilo, 6 * i + f)
                            for o, a, b_ in qq[3 * (b - 4):3 * (b - 4) + 3]:
                                mm = pe.matmul(o, a, b_, start=False, stop=False)
                            if b == B - 1 and f in (2, 4):
                                mm.then_inc(s_used, 1)
                        gate_arguments(f, b, 1)
                pe.wait_ge(s_mul, ZU * STEPS * i + ZU * STEPS)
                pe.wait_ge(s_red, STEPS * i + STEPS)
                tflat = ps[:, 4:7, :].rearrange("p b n -> p (b n)")
                for t in range(NT):
                    for f in range(KC):
                        ins = pe.transpose(tflat[:, t * F + f * P:t * F + (f + 1) * P],
                                           qiT[:, f, t * P:(t + 1) * P], ident[:])
                ins.then_inc(s_tr, 1)
                pe.wait_ge(s_wlo, 3 * (U + 6) + 3)
                pe.wait_ge(s_qilo, 6 * i + 6)
                for t in range(NT):
                    for n, (o, a, b_) in enumerate(parts(1, KC - 1, t, slab_chunk(KC - 1))):
                        mm = pe.matmul(o, a, b_, start=False, stop=(n >= 4))
                    mm.then_inc(s_out if t == 0 else s_used, 1)

            def layer1(i, last):
                T = 15 * i + 30
                U = 5 * i + 15
                transposed(H, s_yt, s_H, 2 * i + 12)
                def first_sums():
                    if not last:
                        pe.wait_ge(s_a4, 1)
                    pe.wait_ge(s_h, 2 * i + 6)
                    aggregate(A4, 0, T)

                for v in range(5):
                    last_unit[0] = v == 4
                    product(U + v, v % 2, T + 3 * v, ((3, 0) if last else (2, i)) if v == 0 else None,
                            between=first_sums if v == 0 else None)
                    if v < 3:
                        aggregate(A4, v + 1, T + 3 * (v + 1))
                    if last and v == 1:
                        pe.wait_ge(s_cnt, 1)
                        for t in range(NT):
                            for u in range(NT):
                                ins = pe.transpose(ps[:, 7, t * N + u * P:t * N + (u + 1) * P],
                                                   cnt[:, 1, u, t * P:(t + 1) * P], ident[:])
                        ins.then_inc(s_cntT, 1)
                last_unit[0] = False

            with pe.Fori(0, 2) as i:
                layer1(i, False)
            layer1(2, True)

            def project(q):
                chunks, w, off, unit = PROJ[q]
                if q > 0:
                    pe.wait_ge(p_lo, PTILE[q])
                transposed(H, p_t, p_H, 2 * q + 2, chunks)
                cols = ((0, 0, w),) if w <= 512 else ((0, 0, FH), (1, FH, FH))
                pe.wait_ge(s_wlo, 3 * unit + 3)
                for k in range(chunks):
                    if k % 2 == 0:
                        pe.wait_ge(p_lo, PTILE[q] + k // 2 + 1)
                    for t in range(NT):
                        ms = parts(0, k, t, lambda Wx, c0, n: Wx[:].rearrange("p j f -> p (j f)")[:, off + k * w + c0:off + k * w + c0 + n], cols)
                        for n, (o, a, b_) in enumerate(ms):
                            mm = pe.matmul(o, a, b_, start=(k == 0 and n < len(cols)), 
                                           stop=(k == chunks - 1 and n >= 2 * len(cols)))
                        if k == chunks - 1:
                            mm.then_inc(p_out, 1)

            def gat(g):
                hn, c, w, _, hv = head_views(g)
                loop = g // 2
                heads = range(hn)

                def bank_of(base, h):
                    return ps[:, base + h // 2, (h % 2) * N:(h % 2 + 1) * N]

                pe.wait_ge(g_al, g + 1)
                for k in range(2):
                    for t in range(NT):
                        ins = pe.transpose(ps[0:hn, 4, k * N + t * P:k * N + (t + 1) * P],
                                           small[:, 64 + 16 * k + hn * t:64 + 16 * k + hn * (t + 1)], ident[:])
                ins.then_inc(g_alT, 1)
                pe.wait_ge(g_ar, g + 1)
                pe.wait_ge(g_h, 2 * g + 2)
                for t in range(NT):
                    for h in heads:
                        o = bank_of(4 * (1 - t), h)
                        pe.matmul(o, selb[0:64, h, :], AR[:, 0, :], start=True, stop=False)
                        ins = pe.matmul(o, identb[:], noedge_d[:, loop, t, :], start=False, stop=True)
                    ins.then_inc(g_ms, 1)
                pe.wait_ge(g_m, g + 1)
                for t in range(NT):
                    ins = pe.transpose(ps[0:hn, 4, t * P:(t + 1) * P], small[:, 96 + hn * t:96 + hn * (t + 1)], ident[:])
                ins.then_inc(g_mT, 1)
                pe.wait_ge(g_mr, g + 1)
                for t in range(NT):
                    zbank, mbank = logit_banks(g, t)
                    if t > 0 and w > 1024:
                        pe.wait_ge(g_zr, 2 * g + t)
                    for h0 in range(0, hn, 2):
                        n = min(2, hn - h0)
                        pe.matmul(ps[:, zbank + h0 // 2, 0:n * N].rearrange("p (h n) -> p h n", h=n),
                                  AR[:, 0, t * P:(t + 1) * P], selb[0:64, h0:h0 + n, 0:1].broadcast_to([64, n, N]),
                                  start=True, stop=False)
                        for h in range(h0, h0 + n):
                            ins = pe.matmul(bank_of(zbank, h), selb[0:64, h, :], AR[:, 1, :], start=False, stop=(h == h0 + n - 1))
                    ins.then_inc(g_zz, 1)
                    if t > 0 and w > 1024:
                        pe.wait_ge(g_sub, 2 * g + t)
                    for h in heads:
                        o = bank_of(mbank, h)
                        pe.matmul(o, selb[0:64, h, :], MR[:], start=True, stop=False)
                        ins = pe.matmul(o, identb[:], noedge_s[:, loop, t, :], start=False, stop=True)
                    ins.then_inc(g_mm, 1)
                pe.wait_ge(g_p0, g + 1)
                pe.wait_ge(g_p1, g + 1)
                for d in range(NT):
                    if c == F:
                        todo = [(ps[:, 2 * d + u, 0:FH + u], 0, u * FH, (u + 1) * FH + u) for u in range(2)]
                    else:
                        per = max(1, hn // 2)
                        todo = [(ps[:, 2 * d + h // per, (h % per) * (c + 1):(h % per + 1) * (c + 1)], h, 0, c + 1)
                                for h in heads]
                    for o, h, c0, c1 in todo:
                        for t in range(NT):
                            ins = pe.matmul(o, zb[:, t, h * N + d * P:h * N + (d + 1) * P], hv[:, t, h, c0:c1],
                                            start=(t == 0), stop=(t == 1))
                    ins.then_inc(g_o, 1)

            project(0)
            gat(0)
            project(1)
            gat(1)
            project(2)
            project(3)
            project(4)
            gat(2)
            project(5)
            gat(3)

        @block.vector
        def _(dve):
            ch = Chain(dve, s_chain)
            TT = dve.tensor_tensor

            def norm_stats(src):
                for t in range(NT):
                    for h in range(2):
                        ins = dve.bn_stats(small[:, 12 * t + 6 * h:12 * t + 6 * h + 6], src[:, t, h * FH:(h + 1) * FH])
                ch.step(ins)
                for t in range(NT):
                    ins = dve.bn_aggr(small[:, 24 + 2 * t:26 + 2 * t],
                                      small[:, 12 * t:12 * t + 12])
                ch.step(ins)
                mv = small[:, 24:28].rearrange("p (t s) -> p t s", t=NT)
                dve.tensor_scalar(small[:, 44:46], mv[:, :, 1], EPS, None, ALU.add).then_inc(s_var, 1)

            def norm_apply(src, n):
                dve.wait_ge(s_rstd, n + 1)
                for t in range(NT):
                    dve.tensor_scalar(H[:, t, :], src[:, t, :], small[:, 24 + 2 * t:25 + 2 * t], small[:, 48 + t:49 + t],
                                      ALU.subtract, ALU.mult).then_inc(s_norm, 1)

            def h_lo(n):
                for t in range(NT):
                    dve.wait_ge(s_hhi, n + (t + 1))
                    TT(Hl[:, t, :], H[:, t, :], Hh[:, t, :], ALU.subtract).then_inc(s_h, 1)

            def yt_lo_tile(T, slot, j):
                dve.wait_ge(s_ythi, T + (j + 1))
                TT(YTl[:, slot, 2 * j:2 * j + 2, :], tile3(j), YTh[:, slot, 2 * j:2 * j + 2, :],
                   ALU.subtract).then_inc(s_ytlo, 1)

            def yt_root(T):
                for j in range(3):
                    yt_lo_tile(T, 0, j)

            def yt_relation(T, slot, deg, r, nth):
                dve.reciprocal(rinv[:], deg[:, r, :]).then_inc(s_rv, 1)
                dve.wait_ge(s_rv, nth)
                for j in range(4):
                    if j < 3:
                        dve.wait_ge(s_yt, T + (j + 1))
                        TT(tile3(j), tile3(j), rinv[:].unsqueeze(1).broadcast_to([P, 2, N]),
                           ALU.mult).then_inc(s_scale, 1)
                    if j > 0:
                        yt_lo_tile(T, slot, j - 1)

            dve.wait_ge(s_const, 16)
            dve.tensor_copy(iota[:], const_in[:, C_IOTA:C_IOTA + N])
            dve.wait_ge(s_edge, 16)
            ef = lambda k: edge_f[:, k, :]
            dve.tensor_copy(ef(0), edge_i[:, 0, :])
            ch.step(dve.tensor_copy(ef(1), edge_i[:, 1, :]))
            tmp = small[:, 64:64 + EC]
            for k, col, t0 in ((2, 2, 0), (3, 3, 0), (4, 3, 2)):
                ch.step(dve.tensor_scalar(tmp, edge_i[:, col, :], float(t0 + 1), PACK, ALU.is_equal, ALU.mult))
                ch.step(dve.scalar_tensor_tensor(out=ef(k), in0=edge_i[:, col, :], scalar=float(t0), in1=tmp,
                                                 op0=ALU.is_equal, op1=ALU.add))

            def onehots(c, slot, wait):
                if wait is not None:
                    dve.wait_ge(s_adj, wait)
                col = lambda k: (edge_f[:, k, c:c + 1] if isinstance(c, int) else edge_f[:, k, bass.DynSlice(c, 1)])
                dve.tensor_scalar(OH[:, slot, :], iota[:], col(0), None, ALU.is_equal)
                for k in range(3):
                    ins = dve.tensor_scalar(V[:, slot, k * N:(k + 1) * N], iota[:], col(1), col(2 + k),
                                            ALU.is_equal, ALU.mult)
                ins.then_inc(s_oh, 1)

            for u in range(SLOTS):
                onehots(u, u, None)
            dve.wait_ge(s_bias, 16)
            dve.wait_ge(s_cst, 1)
            ch.step(dve.tensor_copy(Bias[0:BIAS_ROWS, :], bias_in[:]))
            TT(Bias[32:32 + BIAS_ROWS, :], bias_in[:], Bias[0:BIAS_ROWS, :], ALU.subtract).then_inc(s_brow, 1)
            for t in range(2):
                dve.wait_ge(s_qhi, t + 1)
                TT(YTl[:, t, :, :], qTf[:, :, t * N:(t + 1) * N], YTh[:, t, :, :], ALU.subtract).then_inc(s_qlo, 1)
            dve.wait_ge(s_x, 16)
            norm_stats(X)
            with dve.Fori(1, EC // SLOTS) as i:
                for u in range(SLOTS):
                    onehots(SLOTS * i + u, u, SLOTS * (i - 1) + (u + 1))
            norm_apply(X, 0)

            def qg_lo(t):
                for k in range(4 * t, 4 * t + 4):
                    u, g = k % 4 // 2, k % 2
                    dve.wait_ge(s_qghi, k + 1)
                    TT(halves(QG[64:128, k, :]), ps[64 * g:64 * g + 64, 2 * u:2 * u + 2, 0:FH], halves(QG[0:64, k, :]),
                       ALU.subtract).then_inc(s_qglo, 1)

            for c in range(EC // SLOTS * SLOTS, EC):
                onehots(c, c % SLOTS, c - SLOTS + 1)
            qg_lo(0)

            dve.wait_ge(s_adj, EC)
            for t in range(NT):
                dve.tensor_scalar(halves(other[:, t, :]), ps[:, 4 + 2 * t:6 + 2 * t, 0:FH], 1.0 / PACK, -E / PACK / 2,
                                  ALU.mult, ALU.add).then_inc(s_chain, 1)
            ch.n += NT
            dve.wait_ge(s_chain, ch.n)
            ch.step(dve.tensor_scalar(other[:], other[:], ROUND, -ROUND, ALU.add, ALU.add))
            dve.tensor_scalar(A3[:, :, 1, :], other[:, :, 0:N], MID, None, ALU.add)
            for k in range(2):
                dve.tensor_scalar(A4i[:, :, 2 * k + 1, :], other[:, :, (k + 1) * N:(k + 2) * N], MID, None, ALU.add)
            for t in range(NT):
                for k in range(3):
                    lo = k * N
                    while lo < (k + 1) * N:
                        hi = min((k + 1) * N, (lo // FH + 1) * FH)
                        dst = A3[:, t, 0, lo - k * N:hi - k * N] if k == 0 else A4i[:, t, 2 * (k - 1), lo - k * N:hi - k * N]
                        ins = dve.scalar_tensor_tensor(out=dst, in0=other[:, t, lo:hi], scalar=-PACK,
                                                       in1=ps[:, 4 + 2 * t + lo // FH, lo % FH:lo % FH + hi - lo],
                                                       op0=ALU.mult, op1=ALU.add)
                        lo = hi
            ch.step(ins)
            ch.step(TT(rest[:], A4i[:, :, 0, :], A4i[:, :, 1, :], ALU.add))
            for a_, op in ((A4i[:, :, 2, :], ALU.add), (A4i[:, :, 3, :], ALU.add), (A3[:, :, 0, :], ALU.subtract)):
                ch.step(TT(rest[:], rest[:], a_, op))
            TT(A3[:, :, 2, :], rest[:], A3[:, :, 1, :], ALU.subtract).then_inc(s_acount, 1)

            dve.wait_ge(s_deg, 1)
            ch.step(dve.tensor_scalar(deg3[:, 0:2, :], ps[:, 4, :].rearrange("p (r n) -> p r n", r=2), 1.0, None, ALU.max))
            ch.step(dve.tensor_scalar(deg3[:, 2, :], ps[:, 5, 0:N], 1.0, None, ALU.max))
            dve.tensor_scalar(deg4[:].rearrange("p (b r) n -> p b (r n)", b=2), ps[:, 6:8, :], 1.0, None,
                              ALU.max).then_inc(s_rinv, 1)
            dve.wait_ge(s_rinv, 1)
            qg_lo(1)

            with dve.Fori(0, 2) as i:
                T = 15 * i
                yt_root(T)
                h_lo(2 * i)
                for v in range(1, 4):
                    yt_relation(T + 3 * v, v % 2, deg3, v - 1, R3 * i + v)
                yt_root(T + 12)

                def hg_lo(pair):
                    dve.wait_ge(s_hghi, 4 * i + (pair + 1))
                    r = 64 * (pair % 2)
                    TT(halves(HG[64:128, pair, :]), ps[r:r + 64, 2 * (pair // 2):2 * (pair // 2) + 2, 0:FH],
                       halves(HG[0:64, pair, :]), ALU.subtract).then_inc(s_hglo, 1)

                hg_lo(0)
                hg_lo(1)

                def reduce(st):
                    f, b = st // B, st % B
                    dve.wait_ge(s_add, (STEPS - 1) * i + (st + 1))
                    dve.tensor_reduce(qiT[:, f, b * NB:(b + 1) * NB], PR[:, st % PSLOTS, 0:1024].rearrange(
                        "p (n l) -> p n l", l=LH)[:, :, 0:LH // 2 if FOLDED[st] else LH],
                                      AX.X, ALU.add).then_inc(s_red, 1)

                def qi_lo(f):
                    dve.wait_ge(s_qihi, 6 * i + (f + 1))
                    TT(YTl[:, 1, f, :], qiT[:, f, :], YTh[:, 1, f, :], ALU.subtract).then_inc(s_qilo, 1)

                for st in range(STEPS):
                    f, b = st // B, st % B
                    if st in (1, 3):
                        hg_lo(2 + st // 2)
                    if st >= PSLOTS:
                        dve.wait_ge(s_red, STEPS * i + (st - PSLOTS + 1))
                    for u in range(ZU):
                        if u == 1 and st >= 2:
                            reduce(st - 2)
                        dve.wait_ge(s_sig, 2 * (ZU * STEPS * i + (ZU * st + u + 1)))
                        l0 = b * L + u * LH
                        TT(PR[:, st % PSLOTS, u * 1024:(u + 1) * 1024].rearrange("p (n l) -> p n l", l=LH),
                           ps[:, 4 + 2 * u:6 + 2 * u, :].rearrange("p b (n l) -> p (b n) l", l=LH),
                           qTf[:, f, l0:l0 + LH].unsqueeze(1).broadcast_to([P, NB, LH]), ALU.mult).then_inc(s_mul, 1)
                    if f > 0 and b == 3:
                        qi_lo(f - 1)
                reduce(STEPS - 2)
                dve.wait_ge(s_mul, ZU * STEPS * (i + 1))
                dve.tensor_reduce(qiT[:, KC - 1, (B - 1) * NB:B * NB], PR[:, (STEPS - 1) % PSLOTS, :].rearrange(
                    "p (u n l) -> p n u l", u=ZU, l=LH), AX.XY, ALU.add).then_inc(s_red, 1)
                qi_lo(KC - 1)
                for t in range(NT):
                    dve.wait_ge(s_tanh, 2 * i + (t + 1))
                    TT(tq[:, t, :], tq[:, t, :], H[:, t, :], ALU.subtract).then_inc(s_gate1, 1)
                for t in range(NT):
                    dve.wait_ge(s_gate1, 2 * i + (t + 1))
                    dve.wait_ge(s_alpha, 2 * i + (t + 1))
                    TT(tq[:, t, :], tq[:, t, :], alpha[:, t, :], ALU.mult).then_inc(s_gate2, 1)
                for t in range(NT):
                    dve.wait_ge(s_gate2, 2 * i + (t + 1))
                    TT(H[:, t, :], H[:, t, :], tq[:, t, :], ALU.add).then_inc(s_H, 1)

            dve.wait_ge(s_H, 10)
            ch.step(TT(X[:], X[:], H[:], ALU.add))
            norm_stats(X)
            norm_apply(X, 1)

            def layer1(i):
                T = 15 * i + 30
                yt_root(T)
                h_lo(2 * i + 4)
                for v in range(1, 5):
                    if isinstance(i, int) and v == 2:
                        counts_of_all()
                    if isinstance(i, int) and v == 4:
                        attention_counts()
                    yt_relation(T + 3 * v, v % 2, deg4, v - 1, 2 * R3 + (R4 * i + v))

            def counts_of_all():
                ch.step(TT(cnt[:, 1, :, :], A4i[:, :, 0, :], A4i[:, :, 1, :], ALU.add))
                ch.step(TT(cnt[:, 1, :, :], cnt[:, 1, :, :], A4i[:, :, 2, :], ALU.add))
                ch.step(TT(cnt[:, 1, :, :], cnt[:, 1, :, :], A4i[:, :, 3, :], ALU.add))
                ch.step(dve.tensor_copy(cnt[:, 0, :, :], cnt[:, 1, :, :]))
                for t in range(NT):
                    ins = TT(cnt[:, 0, t, t * P:(t + 1) * P], cnt[:, 0, t, t * P:(t + 1) * P], ident[:], ALU.add)
                ins.then_inc(s_cnt, 1)
                dve.wait_ge(s_cnt, 1)

            def attention_counts():
                dve.wait_ge(s_cntT, 1)
                cT = ps[:, 7, :].rearrange("p (t n) -> p t n", t=NT)
                dve.tensor_scalar(noedge_d[:, 1, :, :], cT, 0.0, NEG, ALU.is_equal, ALU.mult)
                dve.tensor_scalar(noedge_s[:, 1, :, :], cnt[:, 1, :, :], 0.0, -NEG, ALU.is_equal, ALU.mult)
                dve.tensor_scalar(noedge_s[:, 0, :, :], cnt[:, 0, :, :], 0.0, -NEG, ALU.is_equal, ALU.mult)
                dve.tensor_copy(identb[:], ident[:])
                dve.tensor_scalar(AR[:], ident[0:64, 0:1].unsqueeze(2).broadcast_to([64, 2, N]), 0.0, None, ALU.mult)
                ch.step(dve.tensor_copy(looped[:], cT))
                for t in range(NT):
                    ins = TT(looped[:, t, t * P:(t + 1) * P], looped[:, t, t * P:(t + 1) * P], ident[:], ALU.add)
                ch.step(ins)
                ch.step(dve.tensor_scalar(noedge_d[:, 0, :, :], looped[:], 0.0, NEG, ALU.is_equal, ALU.mult))

            with dve.Fori(0, 2) as i:
                layer1(i)
            layer1(2)
            for t in range(NT):
                wait_out(dve, 11, t, 29)
                TT(halves(X[:, t, :]), halves(X[:, t, :]), two_banks(t), ALU.add).then_inc(s_res, 1)
            dve.wait_ge(s_res, 2)
            norm_stats(X)
            norm_apply(X, 2)
            dve.wait_ge(s_gv, 32)

            def proj_lo(q):
                for j in range(PTILE[q + 1] - PTILE[q]):
                    dve.wait_ge(p_hi, PTILE[q] + j + 1)
                    TT(YTl[:, 0, 2 * j:2 * j + 2, :], tile3(j), YTh[:, 0, 2 * j:2 * j + 2, :],
                       ALU.subtract).then_inc(p_lo, 1)

            def rows_hi_lo(rows, src, hn, done):
                ch.step(dve.tensor_copy(rows[0:hn], src))
                TT(rows[32:32 + hn], src, rows[0:hn], ALU.subtract).then_inc(done, 1)

            def gat(g, last=False):
                hn, c, w, nb, hv = head_views(g)
                o_s, o_b = GAT[g][2], GAT[g][4]
                hc = hn * c
                ch.step(dve.memset(hv[:, :, :, c:c + 1], 1.0))
                dve.wait_ge(g_h, 2 * g + 2)
                tv = gtmp[:, 0:NT * hc].rearrange("p (t h c) -> p t h c", t=NT, h=hn)
                ch.step(TT(tv, hv[:, :, :, 0:c], av[:, o_s:o_s + hc].rearrange("p (h c) -> p h c", h=hn).unsqueeze(
                    1).broadcast_to([P, NT, hn, c]), ALU.mult))
                dve.tensor_reduce(small[:, 64:64 + NT * hn], gtmp[:, 0:NT * hc].rearrange("p (h c) -> p h c", c=c),
                                  AX.X, ALU.add)
                dve.wait_ge(g_ald, g + 1)
                dve.tensor_reduce(small[:, 80:80 + NT * hn], zb[:, 0, 0:NT * hc].rearrange("p (h c) -> p h c", c=c),
                                  AX.X, ALU.add).then_inc(g_al, 1)
                dve.wait_ge(g_alT, g + 1)
                rows_hi_lo(AR, ps[0:hn, 4, :].rearrange("p (k n) -> p k n", k=2), hn, g_ar)
                for t in range(NT):
                    dve.wait_ge(g_ms, 2 * g + t + 1)
                    srcs = ps[:, 4 * (1 - t):4 * (1 - t) + nb, 0:min(512, w)]
                    if hn > 1:
                        srcs = srcs.rearrange("p b (h n) -> p (b h) n", n=N)
                    ins = dve.tensor_reduce(small[:, 96 + hn * t:96 + hn * (t + 1)], srcs, AX.X, ALU.max)
                ch.step(ins)
                mx, ald = small[:, 96:96 + NT * hn], small[:, 80:80 + NT * hn]
                ch.step(TT(mx, mx, ald, ALU.add))
                dve.scalar_tensor_tensor(out=mx, in0=mx, scalar=SLOPE, in1=mx, op0=ALU.mult, op1=ALU.max).then_inc(g_m, 1)
                dve.wait_ge(g_mT, g + 1)
                rows_hi_lo(MR, ps[0:hn, 4, 0:N], hn, g_mr)
                for t in range(NT):
                    zbank, mbank = logit_banks(g, t)
                    zt = zb[:, t, 0:w].rearrange("p (b n) -> p b n", b=nb)
                    z_, m_ = (ps[:, b:b + nb, 0:min(512, w)] for b in (zbank, mbank))
                    dve.wait_ge(g_zz, 2 * g + t + 1)
                    dve.wait_ge(g_sl, 2 * g + t + 1)
                    TT(zt, zt, z_, ALU.max).then_inc(g_zr, 1)
                    dve.wait_ge(g_zr, 2 * g + t + 1)
                    dve.wait_ge(g_mm, 2 * g + t + 1)
                    TT(zt, zt, m_, ALU.subtract).then_inc(g_sub, 1)
                dve.wait_ge(g_ex, 2 * g + 2)
                z3 = zb[:, 1, 0:w].rearrange("p (h n) -> p h n", h=hn)
                TT(z3, z3, cnt[:, g // 2, 1, :].unsqueeze(1).broadcast_to([P, hn, N]), ALU.mult).then_inc(g_p1, 1)
                for t in range(NT):
                    dve.wait_ge(g_o, 2 * g + t + 1)
                    if c == F:
                        rd = small[:, 52 + t:53 + t]
                        ch.step(dve.tensor_scalar(rd, ps[:, 2 * t + 1, FH:FH + 1], 1e-16, None, ALU.add))
                        ch.step(dve.reciprocal(rd, rd))
                        dve.scalar_tensor_tensor(out=halves(X[:, t, :]), in0=two_banks(t), scalar=rd,
                                                 in1=halves(X[:, t, :]), op0=ALU.mult, op1=ALU.add).then_inc(s_fin, 1)
                        continue
                    per = max(1, hn // 2)
                    nbk = 1 if hn == 1 else 2
                    pv = ps[:, 2 * t:2 * t + nbk, 0:per * (c + 1)].rearrange("p b (h c) -> p b h c", h=per)
                    r_ = small[:, 52:52 + hn].rearrange("p (b h) -> p b h", b=nbk)
                    ch.step(dve.tensor_scalar(r_, pv[:, :, :, c], 1e-16, None, ALU.add))
                    ch.step(dve.reciprocal(r_, r_))
                    ch.step(TT(gout[:, t, 0:hc].rearrange("p (b h c) -> p b h c", b=nbk, h=per), pv[:, :, :, 0:c],
                               r_.unsqueeze(3).broadcast_to([P, nbk, per, c]), ALU.mult))
                    ch.step(TT(gout[:, t, 0:hc], gout[:, t, 0:hc], gb[:, o_b:o_b + hc], ALU.add))

            def relu_to_h(hc):
                for t in range(NT):
                    dve.tensor_scalar(H[:, t, 0:hc], gout[:, t, 0:hc], 0.0, None, ALU.max).then_inc(p_H, 1)

            proj_lo(0)
            ch.step(dve.tensor_scalar(MR[:], ident[0:64, 0:1].broadcast_to([64, N]), 0.0, None, ALU.mult))
            gat(0)
            relu_to_h(256)
            proj_lo(1)
            for t in range(NT):
                ins = TT(X[:, t, :], X[:, t, :], gb[:, GB_M2:GB_M2 + F], ALU.add)
            ch.step(ins)
            gat(1)
            relu_to_h(256)
            proj_lo(2)
            for t in range(NT):
                dve.wait_ge(p_out, 4 + t + 1)
                ch.step(TT(gout[:, t, 0:256], ps[:, 2 * t, 0:256], gb[:, GB_M1:GB_M1 + 256], ALU.add))
            relu_to_h(256)
            proj_lo(3)
            for t in range(NT):
                dve.wait_ge(p_out, 6 + t + 1)
                ins = TT(halves(X[:, t, :]), halves(X[:, t, :]), two_banks(t), ALU.add)
            ch.step(ins)
            norm_stats(X)
            norm_apply(X, 3)
            proj_lo(4)
            gat(2)
            dve.tensor_scalar(elu_t[:], gout[:], 0.0, None, ALU.min).then_inc(g_el, 2)
            ch.step(dve.tensor_scalar(H[:], gout[:], 0.0, None, ALU.max))
            dve.wait_ge(g_ex2, 1)
            for t in range(NT):
                dve.scalar_tensor_tensor(out=H[:, t, :], in0=elu_t[:, t, :], scalar=-1.0, in1=H[:, t, :],
                                         op0=ALU.add, op1=ALU.add).then_inc(p_H, 1)
            proj_lo(5)
            o_b = GAT[3][4]
            for t in range(NT):
                ins = TT(X[:, t, :], X[:, t, :], gb[:, o_b:o_b + F], ALU.add)
            ch.step(ins)
            gat(3)


def kernel(**inputs):
    import numpy as np
    import concourse.bacc as bacc
    from concourse.bass_utils import run_bass_kernel_spmd

    a = {k: np.asarray(v) for k, v in inputs.items()}

    def unit(w):
        return w.reshape(KC, P, F).transpose(1, 0, 2).reshape(P, 3, 2 * F)

    wg, wq = a["L0_gnn_Wg"], a["L0_gnn_Wq"]
    units = [unit(wg[:, F:].T)]
    for n in "12":
        units.append(unit(a["L0_gnn_W_root" + n]))
        units += [unit(w) for w in a["L0_gnn_W_rel" + n]]
        units += [unit(wg[:, :F].T), unit(wq[:, :F].T), unit(wq[:, F:].T)]
    for n in "123":
        units.append(unit(a["L1_gnn_root" + n]))
        units += [unit(w) for w in a["L1_gnn_W" + n]]
    small_w = [a["L2_gnn_" + n] for n in ("W1", "W2", "Wm1", "Wm2")]
    small_w = [w.reshape(-1, P, w.shape[1]).transpose(1, 0, 2).reshape(P, -1) for w in small_w]
    used = sum(w.shape[1] for w in small_w)
    small_w.append(np.zeros((P, KC * F - used), np.float32))
    units.append(np.concatenate(small_w, axis=1).reshape(P, 3, 2 * F))
    units += [unit(a["L3_gnn_W1"]), unit(a["L3_gnn_W2"])]

    consts = np.zeros((P, C_ALL), np.float32)
    consts[:, C_IOTA:C_IOTA + N] = np.arange(N)
    for col, m in ((C_P, P), (C_P64, 64), (C_P32, 32)):
        consts[:, col] = np.arange(P) % m

    arrays = {
        "x": a["x"],
        "edges": np.stack([a["src"], a["dst"], a["edge_type_3"], a["edge_type_4"]]).reshape(4, EC, P).transpose(2, 0, 1),
        "queries": a["L0_gnn_query_embs"].reshape(B * L, F).T.reshape(KC, P, B * L).transpose(1, 0, 2),
        "consts": consts,
        "biases": np.stack([np.concatenate([a[m], a[n]]) for m, n in (
            ("L0_gnn_b1", "L0_gnn_b2"), ("L0_gnn_bq", "L0_gnn_bq"), ("L1_gnn_b1", "L1_gnn_b2"), ("L1_gnn_b3", "L0_gnn_bg"))]),
        "gat_biases": np.concatenate([a[n] for n in ("L2_gnn_b1", "L2_gnn_b2", "L2_gnn_bm1", "L3_gnn_b1", "L3_gnn_b2",
                                                     "L2_gnn_bm2")]),
        "gat_vectors": np.concatenate([a[n].reshape(-1) for n in (
            "L2_gnn_a_src1", "L2_gnn_a_dst1", "L2_gnn_a_src2", "L2_gnn_a_dst2",
            "L3_gnn_a_src1", "L3_gnn_a_dst1", "L3_gnn_a_src2", "L3_gnn_a_dst2")]),
        "weights": np.stack(units),
    }
    nc = bacc.Bacc("TRN2", target_bir_lowering=False, num_devices=1)
    arrays = {n: np.ascontiguousarray(v) for n, v in arrays.items()}
    args = [nc.dram_tensor(n, v.shape, mybir.dt.from_np(v.dtype), kind="ExternalInput").ap() for n, v in arrays.items()]
    result = nc.dram_tensor("result", (N, F), F32, kind="ExternalOutput").ap()
    build(nc, *args, result)
    r = run_bass_kernel_spmd(nc, [arrays], core_ids=[0])
    return r.results[0]["result"]
```

```python
from contextlib import ExitStack

import concourse.bass as bass
from concourse import mybir

P = 128
N = 256
NT = N // P
F = 768
KC = F // P
FH = F // 2
E = 4352
EC = E // P
B, L = 8, 64
NB = N // B
LH = L // 2
R3, R4 = 3, 4
PACK = 4608.0
MID = 2048.0
ROUND = 1.5 * 2.0 ** 23
ZU = 2
FOLDED = [s % 5 in (1, 3) and s < KC * B - 2 for s in range(KC * B)]
STEPS = KC * B
NU = 33
NEG = -1.0e30
EPS = 1e-5
SLOPE = 0.2

F32, F32R, BF16 = mybir.dt.float32, mybir.dt.float32r, mybir.dt.bfloat16
I32, I16 = mybir.dt.int32, mybir.dt.int16
ALU, ACT, AX = mybir.AluOpType, mybir.ActivationFunctionType, mybir.AxisListType

C_IOTA, C_P, C_P64, C_P32 = 0, N, N + 1, N + 2
C_ALL = N + 3
SLOTS = 8
PSLOTS = 3
SELK = 8
BIAS_ROWS = 4
GAT = [(4, 64, 0, 256, 0), (1, 256, 512, 768, 256), (8, 96, 1024, 1792, 768), (1, 768, 2560, 3328, 1536)]
GB_M1, GB_M2 = 512, 2304
PIECES = [[(t, h0, min(hn, 4)) for t in range(NT) for h0 in range(0, hn, 4)] for hn, *_ in GAT]
PBASE = [sum(len(p) for p in PIECES[:g]) for g in range(len(GAT))]
PROJ = [(6, 256, 0, 30), (2, 256, 1536, 30), (2, 256, 2048, 30), (2, 768, 2560, 30), (6, 768, 0, 31), (6, 768, 0, 32)]
PTILE = [0, 3, 4, 5, 6, 9, 12]


class Chain:

    def __init__(self, eng, sem):
        self.eng, self.sem, self.n = eng, sem, 0

    def step(self, ins):
        self.n += 1
        ins.then_inc(self.sem, 1)
        self.eng.wait_ge(self.sem, self.n)


def build(nc, x, ei, qT, consts, brows, gbias, gavec, W, out):
    ctx = ExitStack()
    with ctx:
        at = [nc.sbuf_base]

        def place(size):
            o = (at[0] + 31) // 32 * 32
            at[0] = o + size
            return o

        def sb(name, shape, dt, off=None):
            size = 1
            for s in shape[1:]:
                size *= s
            size *= {F32: 4, F32R: 4, I32: 4, BF16: 2, I16: 2}[dt]
            o = place(size) if off is None else off
            return nc.alloc_sbuf_tensor_at(name, shape, dt, offset=o)

        def sem(name):
            return ctx.enter_context(nc.semaphore(name))

        ps = ctx.enter_context(nc.psum_tensor("ps", [P, 8, 512], F32))

        Wr = sb("w_raw", [P, 3, 2 * F], F32)
        Wh = sb("w_hi", [P, 3, 2 * F], F32R)
        Wl = sb("w_lo", [P, 3, 2 * F], F32R)
        y_off = place(12288)
        YTh = sb("yt_hi", [P, 2, KC, N], F32R, y_off)
        YTl = sb("yt_lo", [P, 2, KC, N], F32R)
        H = sb("h", [P, NT, F], F32)
        t_off = place(6144)
        qiT = sb("qi_t", [P, KC, N], F32, t_off)
        A3 = sb("a3", [P, NT, R3, N], F32R)
        A4i = sb("a4_i", [P, NT, R4, N], I16)
        deg3 = sb("deg3", [P, R3, N], I16)
        deg4 = sb("deg4", [P, R4, N], I16)
        rinv = sb("rinv", [P, N], F32, t_off)
        X = sb("x", [P, NT, F], F32)
        ident = sb("ident", [P, P], F32)
        ones = sb("ones", [P, P], F32R)
        identb = sb("ident_b", [P, P], BF16)
        SELn = sb("sel_node", [P, 2, 1024], F32R)
        SELl = sb("sel_query", [P, 2, 512], F32R)
        selb = sb("sel_row", [P, SELK, P], F32R)
        Bias = sb("bias", [P, 2 * F], F32R)
        q_off = place(12288)
        qTf = sb("q_t", [P, KC, B * L], F32, q_off)
        z_off = place(36864)
        HG = sb("hg", [P, B // 2, F], F32R, z_off)
        QG = sb("qg", [P, B, F], F32R, z_off + 4 * F * B // 2)
        g_off = place(24576)
        small = sb("small", [P, 128], F32)
        mhalf = sb("mhalf", [P, NT], F32)
        bias_in = sb("bias_in", [BIAS_ROWS, 2 * F], F32, z_off + 12288)
        edge_i = sb("edge_i", [P, 4, EC], I32, t_off)
        edge_f = sb("edge_f", [P, 5, EC], F32, t_off + 16 * EC)
        oh_off = (t_off + 36 * EC + 31) // 32 * 32
        iota = sb("iota", [P, N], BF16, oh_off)
        const_in = sb("const_in", [P, C_ALL], F32, oh_off + 1536)
        OH = sb("onehot_src", [P, SLOTS, N], BF16, g_off)
        V = sb("onehot_dst", [P, SLOTS, 3 * N], BF16, g_off + 2 * SLOTS * N)
        A4t = sb("a4_setup", [P, NT, R4, N], F32R, g_off + 8 * SLOTS * N)
        off_l = sb("offset_l", [P, P], BF16, oh_off + 512)
        off_r = sb("offset_r", [P, FH], BF16, oh_off + 768)
        other = sb("other_count", [P, NT, 3 * N], F32, z_off)
        rest = sb("rest_count", [P, NT, N], F32, z_off + 6144)
        Hh = sb("h_hi", [P, NT, F], F32R, g_off)
        Hl = sb("h_lo", [P, NT, F], F32R, g_off + 6144)
        PR = sb("prod", [P, PSLOTS, 2048], F32, g_off)
        alpha = sb("alpha", [P, NT, F], F32, g_off + 12288)
        tq = sb("tanh_q", [P, NT, F], F32, g_off + 18432)
        A4 = sb("a4", [P, NT, R4, N], F32R, z_off)
        hau = sb("h_aug", [P, 1568], F32, z_off)
        MR = sb("max_rows", [64, N], F32R, z_off + 6400)
        av = sb("a_vec", [P, 4096], F32, z_off + 8192)
        cnt = sb("count", [P, 2, NT, N], F32, z_off + 24576)
        noedge_d = sb("no_edge_dst", [P, 2, NT, N], BF16, z_off + 28672)
        noedge_s = sb("no_edge_src", [P, 2, NT, N], BF16, z_off + 30720)
        looped = sb("looped", [P, NT, N], F32, z_off + 32768)
        AR = sb("logit_rows", [64, 2, N], F32R, z_off + 34816)
        gb = sb("g_bias", [P, 3072], F32, q_off)
        zb = sb("attn", [P, 2, 2048], F32, g_off)
        gtmp = sb("gat_tmp", [P, 2048], F32, g_off + 16384)
        gout = sb("g_out", [P, NT, F], F32, y_off + 6144)
        elu_t = sb("elu_t", [P, NT, F], F32, g_off)

        w_landed = [sem(f"w_landed{j}") for j in range(3)]
        vector_step = sem("vector_step")
        consts_in = sem("consts_in")
        edges_in = sem("edges_in")
        x_in = sem("x_in")
        queries_in = sem("queries_in")
        biases_in = sem("biases_in")
        vectors_in = sem("vectors_in")
        offsets_set = sem("offsets_set")
        selectors_set = sem("selectors_set")
        bias_hi_set = sem("bias_hi_set")
        bias_rows_set = sem("bias_rows_set")
        onehots_ready = sem("onehots_ready")
        onehots_used = sem("onehots_used")
        counts_ready = sem("counts_ready")
        setup_counts_copied = sem("setup_counts_copied")
        degrees_ready = sem("degrees_ready")
        degrees_read = sem("degrees_read")
        query_hi = sem("query_hi")
        query_lo = sem("query_lo")
        qg_hi_ready = sem("qg_hi_ready")
        qg_lo_ready = sem("qg_lo_ready")
        w_hi_ready = sem("w_hi_ready")
        w_lo_ready = sem("w_lo_ready")
        w_used = sem("w_used")
        variance_ready = sem("variance_ready")
        rstd_ready = sem("rstd_ready")
        norm_ready = sem("norm_ready")
        h_ready = sem("h_ready")
        h_hi_ready = sem("h_hi_ready")
        h_lo_ready = sem("h_lo_ready")
        sums_ready = sem("sums_ready")
        sums_scaled = sem("sums_scaled")
        rinv_ready = sem("rinv_ready")
        yt_hi_ready = sem("yt_hi_ready")
        yt_lo_ready = sem("yt_lo_ready")
        out_ready = sem("out_ready")
        a4_ready = sem("a4_ready")
        residual_added = sem("residual_added")
        hg_hi_ready = sem("hg_hi_ready")
        hg_lo_ready = sem("hg_lo_ready")
        gate_args_ready = sem("gate_args_ready")
        sigmoid_ready = sem("sigmoid_ready")
        products_ready = sem("products_ready")
        halves_added = sem("halves_added")
        partial_sums_ready = sem("partial_sums_ready")
        qi_ready = sem("qi_ready")
        qi_hi_ready = sem("qi_hi_ready")
        qi_lo_ready = sem("qi_lo_ready")
        qi_transposed = sem("qi_transposed")
        tanh_ready = sem("tanh_ready")
        alpha_ready = sem("alpha_ready")
        diff_ready = sem("diff_ready")
        alpha_diff_ready = sem("alpha_diff_ready")
        count_matrix_ready = sem("count_matrix_ready")
        count_matrix_transposed = sem("count_matrix_transposed")
        p_h_ready = sem("p_h_ready")
        p_tile_ready = sem("p_tile_ready")
        p_hi_ready = sem("p_hi_ready")
        p_lo_ready = sem("p_lo_ready")
        p_out_ready = sem("p_out_ready")
        g_h_copied = sem("g_h_copied")
        g_dst_products = sem("g_dst_products")
        g_parts_ready = sem("g_parts_ready")
        g_parts_transposed = sem("g_parts_transposed")
        g_part_rows_ready = sem("g_part_rows_ready")
        g_masked_ready = sem("g_masked_ready")
        g_masked_read = sem("g_masked_read")
        g_max_ready = sem("g_max_ready")
        g_max_transposed = sem("g_max_transposed")
        g_max_rows_ready = sem("g_max_rows_ready")
        g_logits_ready = sem("g_logits_ready")
        g_maxima_ready = sem("g_maxima_ready")
        g_leak_ready = sem("g_leak_ready")
        g_leaky_ready = sem("g_leaky_ready")
        g_shifted_ready = sem("g_shifted_ready")
        g_exp_ready = sem("g_exp_ready")
        g_weights_pool = sem("g_weights_pool")
        g_weights_vector = sem("g_weights_vector")
        g_sums_ready = sem("g_sums_ready")
        elu_min_ready = sem("elu_min_ready")
        elu_exp_ready = sem("elu_exp_ready")
        result_ready = sem("result_ready")
        stored = sem("stored")

        block = ctx.enter_context(nc.Block())

        def nodes(ap):
            return ap.rearrange("(t p) f -> p t f", p=P)

        def two_banks(nt):
            return ps[:, 2 * nt:2 * nt + 2, 0:FH]

        def halves(ap):
            return ap.rearrange("p (h f) -> p h f", h=2)

        def tile3(j):
            return ps[:, 4 + j, :].rearrange("p (k n) -> p k n", k=2)

        def head_views(g):
            hn, c = GAT[g][:2]
            w = hn * N
            hv = hau[:, 0:NT * hn * (c + 1)].rearrange("p (t h c) -> p t h c", t=NT, h=hn)
            return hn, c, w, (w + 511) // 512, hv

        def piece_views(g, u):
            t, h0, n = PIECES[g][u]
            w = n * N
            nb = (w + 511) // 512
            zt = zb[:, t, h0 * N:h0 * N + w].rearrange("p (b n) -> p b n", b=nb)
            return zt, ps[:, 4 + 2 * (u % 2):4 + 2 * (u % 2) + nb, 0:min(512, w)], ps[:, 2 * (u % 2):2 * (u % 2) + nb, 0:min(512, w)]

        def masked_bank(g, t):
            return 4 * (1 - t) if GAT[g][0] * N > 1024 else 2 * t

        def piece_counts(g, u):
            t, h0, n = PIECES[g][u]
            return (zb[:, t, h0 * N:(h0 + n) * N].rearrange("p (h n) -> p h n", h=n),
                    cnt[:, g // 2, t, :].unsqueeze(1).broadcast_to([P, n, N]))

        def wait_out(eng, group, t, U):
            if t == 0:
                eng.wait_ge(out_ready, group + 1)
            else:
                eng.wait_ge(w_used, 3 * U + 3)

        @block.sync
        def _(sp):
            def load_slab(U, j):
                sp.dma_start(Wr[:, j, :], W[U, :, j, :] if isinstance(U, int)
                             else W[bass.DynSlice(U, 1), :, j, :].rearrange("o p f -> p (o f)")).then_inc(w_landed[j], 16)

            sp.dma_start(const_in[:], consts).then_inc(consts_in, 16)
            sp.dma_start(bias_in[:], brows).then_inc(biases_in, 16)
            for j in range(3):
                load_slab(0, j)
            with sp.Fori(1, NU) as U:
                for j in range(3):
                    sp.wait_ge(w_lo_ready, 3 * U + (j - 2))
                    load_slab(U, j)
            for t in range(NT):
                sp.wait_ge(result_ready, t + 1)
                sp.dma_start(nodes(out)[:, t, :], X[:, t, :]).then_inc(stored, 16)
            sp.wait_ge(stored, 16 * NT)

        @block.gpsimd
        def _(pool):
            def w_lo(U):
                for j in range(3):
                    w_lo_slab(U, j)

            def w_lo_slab(U, j):
                pool.wait_ge(w_hi_ready, 3 * U + (j + 1))
                pool.tensor_tensor(Wl[:, j, :], Wr[:, j, :], Wh[:, j, :], ALU.subtract).then_inc(w_lo_ready, 1)

            def w_lo_half(U, j, n):
                pool.wait_ge(w_hi_ready, 3 * U + (j + 1))
                c = slice(n * F, (n + 1) * F)
                ins = pool.tensor_tensor(Wl[:, j, c], Wr[:, j, c], Wh[:, j, c], ALU.subtract)
                if n == 1:
                    ins.then_inc(w_lo_ready, 1)

            def rstd(n):
                pool.wait_ge(variance_ready, n + 1)
                pool.tensor_tensor(small[:, 48:50], small[:, 44:46], mhalf[:], ALU.pow).then_inc(rstd_ready, 1)

            pool.memset(off_l[:], MID / P)
            pool.memset(off_r[:], -PACK)
            pool.memset(mhalf[:], -0.5).then_inc(offsets_set, 1)
            pool.wait_ge(consts_in, 16)

            def equal(out_, count, rest_, col):
                return pool.tensor_scalar(out_, count.broadcast_to(rest_), const_in[:, col:col + 1], None, ALU.is_equal)

            num = const_in[:, C_IOTA:C_IOTA + P]
            pool.tensor_scalar(ones[:], num, 0.0, 1.0, ALU.mult, ALU.add)
            pool.tensor_scalar(Bias[:], num[:, 0:1].broadcast_to([P, 2 * F]), 0.0, None, ALU.mult)
            equal(selb[:], num[:, 0:SELK].unsqueeze(2), [P, SELK, P], C_P32)
            pool.tensor_scalar(ident[:], num, const_in[:, C_P:C_P + 1], None, ALU.is_equal).then_inc(selectors_set, 1)
            pool.wait_ge(bias_hi_set, 1)
            pool.tensor_tensor(Bias[32:32 + BIAS_ROWS, :], bias_in[:], Bias[0:BIAS_ROWS, :],
                               ALU.subtract).then_inc(bias_rows_set, 1)
            pool.wait_ge(bias_rows_set, 1)
            w_lo(0)
            for b in range(2):
                equal(SELn[:, b, :].rearrange("p (n l) -> p n l", l=LH), num[:, b * NB:(b + 1) * NB].unsqueeze(2),
                      [P, NB, LH], C_P64)
            for h in range(2):
                ins = equal(SELl[:, h, :].rearrange("p (n l) -> p n l", l=LH),
                            num[:, h * LH:(h + 1) * LH].unsqueeze(1), [P, NB // 2, LH], C_P64)
            ins.then_inc(selectors_set, 1)
            rstd(0)
            w_lo(1)
            with pool.Fori(0, 2) as i:
                for v in range(1, 6):
                    w_lo(7 * i + (1 + v))
                for f in range(KC):
                    for b in range(B):
                        st = f * B + b
                        if f > 0 and b in (2, 3):
                            if f < 4:
                                w_lo_half(7 * i + 7, f - 1, b - 2)
                            else:
                                w_lo_half(7 * i + 8, f - 4, b - 2)
                        if st == STEPS - 1:
                            continue
                        pool.wait_ge(products_ready, ZU * (STEPS * i + (st + 1)))
                        sums = PR[:, st % PSLOTS, 0:1024]
                        ins = pool.tensor_tensor(sums, sums, PR[:, st % PSLOTS, 1024:2048], ALU.add)
                        if FOLDED[st]:
                            ins.then_inc(halves_added, 1)
                            pool.wait_ge(halves_added, sum(FOLDED) * i + sum(FOLDED[:st + 1]))
                            s3 = sums.rearrange("p (n l) -> p n l", l=LH)
                            ins = pool.tensor_tensor(s3[:, :, 0:LH // 2], s3[:, :, 0:LH // 2], s3[:, :, LH // 2:LH], ALU.add)
                        ins.then_inc(partial_sums_ready, 1)
                w_lo_slab(7 * i + 8, 2)
            rstd(1)
            with pool.Fori(0, 3) as i:
                for v in range(5):
                    w_lo(5 * i + (16 + v))
            rstd(2)

            def attention(g):
                hn, c, w, _, hv = head_views(g)
                o_d = GAT[g][3]
                pool.wait_ge(g_h_copied, 2 * g + 2)
                if g > 0:
                    pool.wait_ge(g_sums_ready, 2 * g)
                pool.tensor_tensor(zb[:, 0, 0:NT * hn * c].rearrange("p (t h c) -> p t h c", t=NT, h=hn), hv[:, :, :, 0:c],
                                   av[:, o_d:o_d + hn * c].rearrange("p (h c) -> p h c", h=hn).unsqueeze(1).broadcast_to(
                                       [P, NT, hn, c]), ALU.mult).then_inc(g_dst_products, 1)
                for u in range(len(PIECES[g]) // 2):
                    pool.wait_ge(g_exp_ready, PBASE[g] + u + 1)
                    z3, c3 = piece_counts(g, u)
                    pool.tensor_tensor(z3, z3, c3, ALU.mult).then_inc(g_weights_pool, 1)

            pool.wait_ge(vectors_in, 32)
            attention(0)
            attention(1)
            w_lo_slab(31, 0)
            rstd(3)
            w_lo_slab(31, 1)
            w_lo_slab(31, 2)
            attention(2)
            w_lo(32)
            attention(3)

        @block.scalar
        def _(act):
            def copy(o, i):
                return act.activation(o, i, ACT.Copy)

            def w_hi_slab(U, j, first=False):
                act.wait_ge(w_landed[j], 16 * U + 16)
                if not first:
                    act.wait_ge(w_used, 3 * U + (j - 2))
                copy(Wh[:, j, :], Wr[:, j, :]).then_inc(w_hi_ready, 1)

            def w_hi_piece(U, j, n):
                if n == 0:
                    act.wait_ge(w_landed[j], 16 * U + 16)
                    act.wait_ge(w_used, 3 * U + (j - 2))
                c = slice(n * FH, (n + 1) * FH)
                ins = copy(Wh[:, j, c], Wr[:, j, c])
                if n == 3:
                    ins.then_inc(w_hi_ready, 1)

            def w_hi(U, first=False):
                for j in range(3):
                    w_hi_slab(U, j, first)

            def yt_hi(T, slot, scaled=None):
                for j in range(3):
                    if scaled is None:
                        act.wait_ge(sums_ready, T + (j + 1))
                    else:
                        act.wait_ge(sums_scaled, scaled + (j + 1))
                    copy(YTh[:, slot, 2 * j:2 * j + 2, :], tile3(j)).then_inc(yt_hi_ready, 1)

            def relu_norm(n, h_sem):
                act.wait_ge(norm_ready, n + 1)
                for t in range(NT):
                    act.activation(H[:, t, :], X[:, t, :], ACT.Relu, scale=small[:, 48 + t:49 + t],
                                   bias=small[:, 40 + t:41 + t]).then_inc(h_sem, 1)

            def h_hi(n):
                act.wait_ge(h_ready, n)
                for t in range(NT):
                    copy(Hh[:, t, :], H[:, t, :]).then_inc(h_hi_ready, 1)

            act.dma_start(edge_i[:], ei).then_inc(edges_in, 16)
            act.dma_start(qTf[:], qT).then_inc(queries_in, 16)
            act.dma_start(X[:], nodes(x)).then_inc(x_in, 16)

            act.wait_ge(queries_in, 16)
            for t in range(2):
                copy(YTh[:, t, :, :], qTf[:, :, t * N:(t + 1) * N]).then_inc(query_hi, 1)
            act.wait_ge(biases_in, 16)
            act.wait_ge(selectors_set, 1)
            copy(Bias[0:BIAS_ROWS, :], bias_in[:]).then_inc(bias_hi_set, 1)
            w_hi(0, first=True)

            for t in range(2):
                for u in range(NT):
                    if t == 0:
                        act.wait_ge(out_ready, u + 1)
                    else:
                        wait_out(act, 2, u, 0)
                    for g in range(2):
                        copy(halves(QG[0:64, 4 * t + 2 * u + g, :]), ps[64 * g:64 * g + 64, 2 * u:2 * u + 2, 0:FH]
                             ).then_inc(qg_hi_ready, 1)
                if t == 0:
                    act.wait_ge(counts_ready, 1)
                    copy(A4t[:], A4i[:]).then_inc(setup_counts_copied, 1)
                    w_hi_slab(1, 0)
                    w_hi_slab(1, 1)
                    relu_norm(0, h_ready)
                    w_hi_slab(1, 2)

            with act.Fori(0, 2) as i:
                yt_hi(15 * i, 0)
                h_hi(4 * i + 2)
                for v in range(4):
                    if v < 3:
                        yt_hi(None, (v + 1) % 2, 9 * i + 3 * v)
                    w_hi(7 * i + (2 + v))
                for t in range(NT):
                    wait_out(act, 3 * i + 3, t, 7 * i + 4)
                    act.activation(halves(H[:, t, :]), two_banks(t), ACT.Relu).then_inc(h_ready, 1)
                yt_hi(15 * i + 12, 0)
                w_hi(7 * i + 6)

                def hg_hi(pair):
                    if pair % 2 == 0:
                        wait_out(act, 3 * i + 4, pair // 2, 7 * i + 5)
                    r = 64 * (pair % 2)
                    copy(halves(HG[0:64, pair, :]), ps[r:r + 64, 2 * (pair // 2):2 * (pair // 2) + 2, 0:FH]
                         ).then_inc(hg_hi_ready, 1)

                hg_hi(0)
                hg_hi(1)
                for f in range(KC):
                    for b in range(B):
                        st = f * B + b
                        if st in (1, 3):
                            hg_hi(2 + st // 2)
                        for k in range(2 * ZU):
                            act.wait_ge(gate_args_ready, 2 * ZU * STEPS * i + (2 * ZU * st + k + 1))
                            act.activation(ps[:, 4 + k, :], ps[:, 4 + k, :], ACT.Sigmoid).then_inc(sigmoid_ready, 1)
                            if f > 0 and b < 2 and k % 2 == 1:
                                if f < 4:
                                    w_hi_piece(7 * i + 7, f - 1, 2 * b + k // 2)
                                else:
                                    w_hi_piece(7 * i + 8, f - 4, 2 * b + k // 2)
                        if f > 0 and b == 2:
                            act.wait_ge(qi_ready, STEPS * i + B * f)
                            copy(YTh[:, 1, f - 1, :], qiT[:, f - 1, :]).then_inc(qi_hi_ready, 1)
                act.wait_ge(qi_ready, STEPS * i + STEPS)
                copy(YTh[:, 1, KC - 1, :], qiT[:, KC - 1, :]).then_inc(qi_hi_ready, 1)
                act.wait_ge(qi_transposed, i + 1)
                tflat = ps[:, 4:7, :].rearrange("p b n -> p (b n)")
                for t in range(NT):
                    act.activation(tq[:, t, :], tflat[:, t * F:(t + 1) * F], ACT.Tanh).then_inc(tanh_ready, 1)
                for t in range(NT):
                    wait_out(act, 3 * i + 5, t, 7 * i + 7)
                    act.activation(halves(alpha[:, t, :]), two_banks(t), ACT.Sigmoid).then_inc(alpha_ready, 1)
                w_hi_slab(7 * i + 8, 2)

            act.wait_ge(alpha_diff_ready, 4)
            act.dma_start(av[:], gavec.partition_broadcast(P)).then_inc(vectors_in, 16)
            act.dma_start(gb[:], gbias.partition_broadcast(P)).then_inc(vectors_in, 16)
            copy(A4[:], A4i[:]).then_inc(a4_ready, 1)
            relu_norm(1, h_ready)
            with act.Fori(0, 2) as i:
                yt_hi(15 * i + 30, 0)
                h_hi(2 * i + 12)
                for v in range(5):
                    if v < 4:
                        yt_hi(None, (v + 1) % 2, 12 * i + (18 + 3 * v))
                    w_hi(5 * i + (16 + v))
                for t in range(NT):
                    wait_out(act, i + 9, t, 5 * i + 19)
                    act.activation(halves(H[:, t, :]), two_banks(t), ACT.Relu).then_inc(h_ready, 1)
            yt_hi(60, 0)
            h_hi(16)
            for v in range(5):
                if v < 4:
                    yt_hi(None, (v + 1) % 2, 42 + 3 * v)
                w_hi(26 + v)
            relu_norm(2, p_h_ready)

            def proj_hi(q):
                for j in range(PTILE[q + 1] - PTILE[q]):
                    act.wait_ge(p_tile_ready, PTILE[q] + j + 1)
                    copy(YTh[:, 0, 2 * j:2 * j + 2, :], tile3(j)).then_inc(p_hi_ready, 1)

            def gat(g, q):
                hn, c, _, _, _ = GAT[g]
                hv = hau[:, 0:NT * hn * (c + 1)].rearrange("p (t h c) -> p t h c", t=NT, h=hn)
                for t in range(NT):
                    act.wait_ge(p_out_ready, 2 * q + t + 1)
                    if hn * c == F:
                        src = two_banks(t)
                        if hn == 1:
                            dst = halves(hv[:, t, 0, 0:c])
                            copy(dst, src).then_inc(g_h_copied, 1)
                        else:
                            for u in range(2):
                                ins = copy(hv[:, t, 4 * u:4 * u + 4, 0:c],
                                           ps[:, 2 * t + u, 0:FH].rearrange("p (h c) -> p h c", c=c))
                            ins.then_inc(g_h_copied, 1)
                    else:
                        copy(hv[:, t, :, 0:c], ps[:, 2 * t, 0:hn * c].rearrange("p (h c) -> p h c", c=c)).then_inc(g_h_copied, 1)
                def exponentials(u):
                    act.wait_ge(g_shifted_ready, PBASE[g] + u + 1)
                    z3, _ = piece_counts(g, u)
                    act.activation(z3, z3, ACT.Exp).then_inc(g_exp_ready, 1)

                n = len(PIECES[g])
                for u in range(n):
                    zt, z_, _ = piece_views(g, u)
                    act.wait_ge(g_logits_ready, PBASE[g] + u + 1)
                    act.activation(zt, z_, ACT.Copy, scale=SLOPE).then_inc(g_leak_ready, 1)
                    if u > 1:
                        exponentials(u - 2)
                for u in range(n - 2, n):
                    exponentials(u)

            proj_hi(0)
            gat(0, 0)
            proj_hi(1)
            gat(1, 1)
            proj_hi(2)
            proj_hi(3)
            act.wait_ge(p_out_ready, 8)
            w_hi(31, first=True)
            relu_norm(3, p_h_ready)
            proj_hi(4)
            gat(2, 4)
            w_hi(32, first=True)
            act.wait_ge(elu_min_ready, 2)
            act.activation(elu_t[:], elu_t[:], ACT.Exp).then_inc(elu_exp_ready, 1)
            proj_hi(5)
            gat(3, 5)

        @block.tensor
        def _(pe):
            def parts(slot, k, t, Wk, cols=((0, 0, FH), (1, FH, FH))):
                out_ = []
                for Y, Wx in ((YTh, Wh), (YTh, Wl), (YTl, Wh)):
                    for bank, c0, w in cols:
                        out_.append((ps[:, 2 * t + bank, 0:w], Y[:, slot, k, t * P:(t + 1) * P], Wk(Wx, c0, w)))
                return out_

            def slab_chunk(k):
                return lambda Wx, c0, w: Wx[:, k // 2, (k % 2) * F + c0:(k % 2) * F + c0 + w]

            def bias_mm(row, slot):
                for t in range(NT):
                    for h in range(2):
                        if isinstance(slot, int):
                            rhs = Bias[:, slot * F + h * FH:slot * F + (h + 1) * FH]
                        else:
                            rhs = Bias[:, bass.DynSlice(slot * F + h * FH, FH)]
                        pe.matmul(ps[:, 2 * t + h, 0:FH], selb[:, row, :], rhs, start=True, stop=False)

            def product(U, slot, ready, bias, last=False, release=True, fresh=False, between=None):
                if bias is not None:
                    bias_mm(*bias)
                def chunks(j, t, end):
                    for k in (2 * j, 2 * j + 1):
                        for n, (o, a, b_) in enumerate(parts(slot, k, t, slab_chunk(k))):
                            mm = pe.matmul(o, a, b_, start=(fresh and k == 0 and n < 2),
                                           stop=(end and k == KC - 1 and n >= 4))
                    return mm

                for j in range(3):
                    if between is not None and j == 2:
                        between()
                    pe.wait_ge(w_lo_ready, 3 * U + (j + 1))
                    if ready is not None:
                        pe.wait_ge(yt_lo_ready, ready + (j + 1))
                    for t in range(NT):
                        mm = chunks(j, t, last)
                        if last and j == 2 and (t == 0 or not release):
                            mm.then_inc(out_ready, 1)
                    if release:
                        mm.then_inc(w_used, 1)

            def transposed(src, sem_, src_ready, count, chunks=KC):
                for t in range(NT):
                    pe.wait_ge(src_ready, count - (1 - t))
                    for j in range(chunks // 2):
                        for kk in range(2):
                            k = 2 * j + kk
                            ins = pe.transpose(ps[:, 4 + j, kk * N + t * P:kk * N + (t + 1) * P],
                                               src[:, t, k * P:(k + 1) * P], ident[:])
                        if t == NT - 1:
                            ins.then_inc(sem_, 1)

            def aggregate(A, r, prev):
                for j in range(3):
                    pe.wait_ge(yt_lo_ready, prev + (j + 1))
                    for kk in range(2):
                        k = 2 * j + kk
                        n = 0
                        for t in range(NT):
                            for Hx in (Hh, Hl):
                                ins = pe.matmul(ps[:, 4 + j, kk * N:(kk + 1) * N], Hx[:, t, k * P:(k + 1) * P],
                                                A[:, t, r, :], start=(n == 0), stop=(n == 3))
                                n += 1
                    ins.then_inc(sums_ready, 1)

            def count_chunk(slot, last, ready):
                pe.wait_ge(onehots_ready, ready)
                for t in range(NT):
                    for u in range(2):
                        ins = pe.matmul(ps[:, 4 + 2 * t + u, 0:FH], OH[:, slot, t * P:(t + 1) * P],
                                        V[:, slot, u * FH:(u + 1) * FH], start=False, stop=last)
                ins.then_inc(onehots_used, 1)

            pe.wait_ge(offsets_set, 1)
            for k in range(4):
                pe.matmul(ps[:, 4 + k, 0:FH], off_l[:], off_r[:], start=True, stop=False)

            def count_group(i):
                for u in range(SLOTS):
                    count_chunk(u, False, SLOTS * i + (u + 1))

            with pe.Fori(0, 2) as i:
                count_group(i)
            pe.wait_ge(bias_rows_set, 1)
            pe.wait_ge(query_lo, 1)
            product(0, 0, None, (3, 1), last=True, release=False)
            with pe.Fori(2, EC // SLOTS) as i:
                count_group(i)
            for c in range(EC // SLOTS * SLOTS, EC):
                count_chunk(c % SLOTS, c == EC - 1, c + 1)
            pe.wait_ge(query_lo, 2)
            pe.wait_ge(qg_lo_ready, 4)
            product(0, 1, None, (3, 1), last=True)
            pe.wait_ge(counts_ready, 1)
            for r, bank, c in ((0, 4, 0), (1, 4, N), (2, 5, 0)):
                for t in range(NT):
                    ins = pe.matmul(ps[:, bank, c:c + N], ones[:], A3[:, t, r, :], start=(t == 0), stop=(t == 1))
            pe.wait_ge(setup_counts_copied, 1)
            for r in range(R4):
                for t in range(NT):
                    ins = pe.matmul(ps[:, 6 + r // 2, (r % 2) * N:(r % 2 + 1) * N], ones[:], A4t[:, t, r, :],
                                    start=(t == 0), stop=(t == 1))
            ins.then_inc(degrees_ready, 1)
            pe.wait_ge(degrees_read, 1)
            pe.wait_ge(selectors_set, 2)

            with pe.Fori(0, 2) as i:
                T = 15 * i
                U = 7 * i + 1
                transposed(H, sums_ready, h_ready, 4 * i + 2)

                def first_sums():
                    pe.wait_ge(h_lo_ready, 2 * i + 2)
                    aggregate(A3, 0, T)

                pe.wait_ge(qg_lo_ready, 8)
                for v in range(4):
                    product(U + v, v % 2, T + 3 * v, (0, i) if v == 0 else None, last=v == 3,
                            between=first_sums if v == 0 else None)
                    if v < 2:
                        aggregate(A3, v + 1, T + 3 * (v + 1))
                transposed(H, sums_ready, h_ready, 4 * i + 4)
                product(U + 4, 0, T + 12, None, last=True, fresh=True)

                def gate_arguments(f, b, u):
                    k = ZU * (f * B + b) + u
                    if k >= ZU:
                        pe.wait_ge(products_ready, ZU * STEPS * i + (k - 1))
                    for h in range(2):
                        pe.matmul(ps[:, 4 + 2 * u + h, :], HG[:, b // 2, f * P:(f + 1) * P],
                                  SELn[:, b % 2, h * 512:(h + 1) * 512], start=True, stop=False)
                        pe.matmul(ps[:, 4 + 2 * u + h, :], QG[:, b, f * P:(f + 1) * P], SELl[:, u, :],
                                  start=False, stop=True).then_inc(gate_args_ready, 1)

                for f in range(KC):
                    hq = [m for kk in range(2) for t in range(NT) for m in parts(0, 2 * f + kk, t, slab_chunk(2 * f + kk))] \
                        if f < 3 else []
                    qq = [m for t in range(NT) for m in parts(1, f - 1, t, slab_chunk(f - 1))] if f > 0 else []
                    for b in range(B):
                        st = f * B + b
                        if f == 0:
                            pe.wait_ge(hg_lo_ready, 4 * i + (b // 2 + 1))
                        gate_arguments(f, b, 0)
                        if f < 3 and (f > 0 or b >= 4):
                            if b == (4 if f == 0 else 0):
                                pe.wait_ge(w_lo_ready, 3 * (U + 5) + (f + 1))
                            if (f, b) == (0, 4):
                                pe.wait_ge(hg_lo_ready, 4 * i + 4)
                                bias_mm(1, i)
                            for o, a, b_ in hq[3 * b:3 * b + 3] if f > 0 else hq[6 * (b - 4):6 * (b - 4) + 6]:
                                mm = pe.matmul(o, a, b_, start=False, stop=False)
                            if b == B - 1:
                                mm.then_inc(w_used, 1)
                        if f > 0 and b >= 5:
                            if b == 5:
                                pe.wait_ge(w_lo_ready, 3 * (U + 6) + ((f - 1) // 2 + 1))
                                pe.wait_ge(qi_lo_ready, 6 * i + f)
                            for o, a, b_ in qq[4 * (b - 5):4 * (b - 5) + 4]:
                                mm = pe.matmul(o, a, b_, start=False, stop=False)
                            if b == B - 1 and f in (2, 4):
                                mm.then_inc(w_used, 1)
                        gate_arguments(f, b, 1)
                pe.wait_ge(products_ready, ZU * STEPS * i + ZU * STEPS)
                pe.wait_ge(qi_ready, STEPS * i + STEPS)
                tflat = ps[:, 4:7, :].rearrange("p b n -> p (b n)")
                for t in range(NT):
                    for f in range(KC):
                        ins = pe.transpose(tflat[:, t * F + f * P:t * F + (f + 1) * P],
                                           qiT[:, f, t * P:(t + 1) * P], ident[:])
                ins.then_inc(qi_transposed, 1)
                pe.wait_ge(w_lo_ready, 3 * (U + 6) + 3)
                pe.wait_ge(qi_lo_ready, 6 * i + 6)
                for t in range(NT):
                    for n, (o, a, b_) in enumerate(parts(1, KC - 1, t, slab_chunk(KC - 1))):
                        mm = pe.matmul(o, a, b_, start=False, stop=(n >= 4))
                    mm.then_inc(out_ready if t == 0 else w_used, 1)

            def layer1(i, last):
                T = 15 * i + 30
                U = 5 * i + 15
                transposed(H, sums_ready, h_ready, 2 * i + 12)
                def first_sums():
                    if not last:
                        pe.wait_ge(a4_ready, 1)
                    pe.wait_ge(h_lo_ready, 2 * i + 6)
                    aggregate(A4, 0, T)

                for v in range(5):
                    product(U + v, v % 2, T + 3 * v, ((3, 0) if last else (2, i)) if v == 0 else None,
                            last=v == 4, between=first_sums if v == 0 else None)
                    if v < 3:
                        aggregate(A4, v + 1, T + 3 * (v + 1))
                    if last and v == 1:
                        pe.wait_ge(count_matrix_ready, 1)
                        for t in range(NT):
                            for u in range(NT):
                                ins = pe.transpose(ps[:, 7, t * N + u * P:t * N + (u + 1) * P],
                                                   cnt[:, 1, u, t * P:(t + 1) * P], ident[:])
                        ins.then_inc(count_matrix_transposed, 1)

            with pe.Fori(0, 2) as i:
                layer1(i, False)
            layer1(2, True)

            def project(q):
                chunks, w, off, unit = PROJ[q]
                if q > 0:
                    pe.wait_ge(p_lo_ready, PTILE[q])
                transposed(H, p_tile_ready, p_h_ready, 2 * q + 2, chunks)
                cols = ((0, 0, w),) if w <= 512 else ((0, 0, FH), (1, FH, FH))
                pe.wait_ge(w_lo_ready, 3 * unit + 3)
                for k in range(chunks):
                    if k % 2 == 0:
                        pe.wait_ge(p_lo_ready, PTILE[q] + k // 2 + 1)
                    for t in range(NT):
                        ms = parts(0, k, t, lambda Wx, c0, n: Wx[:].rearrange("p j f -> p (j f)")[:, off + k * w + c0:off + k * w + c0 + n], cols)
                        for n, (o, a, b_) in enumerate(ms):
                            mm = pe.matmul(o, a, b_, start=(k == 0 and n < len(cols)), 
                                           stop=(k == chunks - 1 and n >= 2 * len(cols)))
                        if k == chunks - 1:
                            mm.then_inc(p_out_ready, 1)

            def gat(g):
                hn, c, w, _, hv = head_views(g)
                loop = g // 2
                heads = range(hn)

                def bank_of(base, h):
                    return ps[:, base + h // 2, (h % 2) * N:(h % 2 + 1) * N]

                pe.wait_ge(g_parts_ready, g + 1)
                for k in range(2):
                    for t in range(NT):
                        ins = pe.transpose(ps[0:hn, 4, k * N + t * P:k * N + (t + 1) * P],
                                           small[:, 64 + 16 * k + hn * t:64 + 16 * k + hn * (t + 1)], ident[:])
                ins.then_inc(g_parts_transposed, 1)
                pe.wait_ge(g_part_rows_ready, g + 1)
                pe.wait_ge(g_h_copied, 2 * g + 2)
                for t, h0, n in PIECES[g]:
                    for h in range(h0, h0 + n):
                        o = bank_of(masked_bank(g, t), h)
                        pe.matmul(o, selb[0:64, h, :], AR[:, 0, :], start=True, stop=False)
                        ins = pe.matmul(o, identb[:], noedge_d[:, loop, t, :], start=False, stop=True)
                    ins.then_inc(g_masked_ready, 1)
                def logits(u):
                    t, h0, n = PIECES[g][u]
                    bank = 4 + 2 * (u % 2)
                    for h in range(0, n, 2):
                        m = min(2, n - h)
                        pe.matmul(ps[:, bank + h // 2, 0:m * N].rearrange("p (h n) -> p h n", h=m),
                                  AR[:, 0, t * P:(t + 1) * P], selb[0:64, h0 + h:h0 + h + m, 0:1].broadcast_to([64, m, N]),
                                  start=True, stop=False)
                        for k in range(h, h + m):
                            ins = pe.matmul(bank_of(bank, k), selb[0:64, h0 + k, :], AR[:, 1, :], start=False,
                                            stop=(k == h + m - 1))
                    ins.then_inc(g_logits_ready, 1)

                def maxima(u):
                    t, h0, n = PIECES[g][u]
                    for k in range(n):
                        o = bank_of(2 * (u % 2), k)
                        pe.matmul(o, selb[0:64, h0 + k, :], MR[:], start=True, stop=False)
                        ins = pe.matmul(o, identb[:], noedge_s[:, loop, t, :], start=False, stop=True)
                    ins.then_inc(g_maxima_ready, 1)

                if w > 1024:
                    pe.wait_ge(g_masked_read, PBASE[g] + 2)
                for u in range(2):
                    logits(u)
                pe.wait_ge(g_max_ready, g + 1)
                for t in range(NT):
                    ins = pe.transpose(ps[0:hn, 0, t * P:(t + 1) * P], small[:, 96 + hn * t:96 + hn * (t + 1)], ident[:])
                ins.then_inc(g_max_transposed, 1)
                pe.wait_ge(g_max_rows_ready, g + 1)
                for u in range(len(PIECES[g])):
                    if u >= 2:
                        pe.wait_ge(g_leaky_ready, PBASE[g] + u - 1)
                        logits(u)
                        pe.wait_ge(g_shifted_ready, PBASE[g] + u - 1)
                    maxima(u)
                done = (PBASE[g] + len(PIECES[g])) // 2
                pe.wait_ge(g_weights_pool, done)
                pe.wait_ge(g_weights_vector, done)
                for d in range(NT):
                    if c == F:
                        todo = [(ps[:, 2 * d + u, 0:FH + u], 0, u * FH, (u + 1) * FH + u) for u in range(2)]
                    else:
                        per = max(1, hn // 2)
                        todo = [(ps[:, 2 * d + h // per, (h % per) * (c + 1):(h % per + 1) * (c + 1)], h, 0, c + 1)
                                for h in heads]
                    for o, h, c0, c1 in todo:
                        for t in range(NT):
                            ins = pe.matmul(o, zb[:, t, h * N + d * P:h * N + (d + 1) * P], hv[:, t, h, c0:c1],
                                            start=(t == 0), stop=(t == 1))
                    ins.then_inc(g_sums_ready, 1)

            project(0)
            gat(0)
            project(1)
            gat(1)
            project(2)
            project(3)
            project(4)
            gat(2)
            project(5)
            gat(3)

        @block.vector
        def _(dve):
            ch = Chain(dve, vector_step)
            TT = dve.tensor_tensor

            def norm_stats(src):
                for t in range(NT):
                    for h in range(2):
                        ins = dve.bn_stats(small[:, 12 * t + 6 * h:12 * t + 6 * h + 6], src[:, t, h * FH:(h + 1) * FH])
                ch.step(ins)
                for t in range(NT):
                    ins = dve.bn_aggr(small[:, 24 + 2 * t:26 + 2 * t],
                                      small[:, 12 * t:12 * t + 12])
                ch.step(ins)
                mv = small[:, 24:28].rearrange("p (t s) -> p t s", t=NT)
                dve.tensor_scalar(small[:, 44:46], mv[:, :, 1], EPS, None, ALU.add).then_inc(variance_ready, 1)

            def norm_shift(n):
                dve.wait_ge(rstd_ready, n + 1)
                mean = small[:, 24:28].rearrange("p (t s) -> p t s", t=NT)[:, :, 0]
                dve.scalar_tensor_tensor(out=small[:, 40:42], in0=mean, scalar=-1.0, in1=small[:, 48:50], op0=ALU.mult,
                                         op1=ALU.mult).then_inc(norm_ready, 1)

            def h_lo(n):
                for t in range(NT):
                    dve.wait_ge(h_hi_ready, n + (t + 1))
                    TT(Hl[:, t, :], H[:, t, :], Hh[:, t, :], ALU.subtract).then_inc(h_lo_ready, 1)

            def yt_lo_tile(T, slot, j):
                dve.wait_ge(yt_hi_ready, T + (j + 1))
                TT(YTl[:, slot, 2 * j:2 * j + 2, :], tile3(j), YTh[:, slot, 2 * j:2 * j + 2, :],
                   ALU.subtract).then_inc(yt_lo_ready, 1)

            def yt_root(T):
                for j in range(3):
                    yt_lo_tile(T, 0, j)

            def yt_relation(T, slot, deg, r, nth):
                dve.reciprocal(rinv[:], deg[:, r, :]).then_inc(rinv_ready, 1)
                dve.wait_ge(rinv_ready, nth)
                for j in range(4):
                    if j < 3:
                        dve.wait_ge(sums_ready, T + (j + 1))
                        TT(tile3(j), tile3(j), rinv[:].unsqueeze(1).broadcast_to([P, 2, N]),
                           ALU.mult).then_inc(sums_scaled, 1)
                    if j > 0:
                        yt_lo_tile(T, slot, j - 1)

            dve.wait_ge(consts_in, 16)
            dve.tensor_copy(iota[:], const_in[:, C_IOTA:C_IOTA + N])
            dve.wait_ge(edges_in, 16)
            ef = lambda k: edge_f[:, k, :]
            dve.tensor_copy(ef(0), edge_i[:, 0, :])
            ch.step(dve.tensor_copy(ef(1), edge_i[:, 1, :]))
            tmp = small[:, 64:64 + EC]
            for k, col, t0 in ((2, 2, 0), (3, 3, 0), (4, 3, 2)):
                ch.step(dve.tensor_scalar(tmp, edge_i[:, col, :], float(t0 + 1), PACK, ALU.is_equal, ALU.mult))
                ch.step(dve.scalar_tensor_tensor(out=ef(k), in0=edge_i[:, col, :], scalar=float(t0), in1=tmp,
                                                 op0=ALU.is_equal, op1=ALU.add))

            def onehots(c, slot, wait):
                if wait is not None:
                    dve.wait_ge(onehots_used, wait)
                col = lambda k: (edge_f[:, k, c:c + 1] if isinstance(c, int) else edge_f[:, k, bass.DynSlice(c, 1)])
                dve.tensor_scalar(OH[:, slot, :], iota[:], col(0), None, ALU.is_equal)
                for k in range(3):
                    ins = dve.tensor_scalar(V[:, slot, k * N:(k + 1) * N], iota[:], col(1), col(2 + k),
                                            ALU.is_equal, ALU.mult)
                ins.then_inc(onehots_ready, 1)

            for u in range(SLOTS):
                onehots(u, u, None)
            for t in range(2):
                dve.wait_ge(query_hi, t + 1)
                TT(YTl[:, t, :, :], qTf[:, :, t * N:(t + 1) * N], YTh[:, t, :, :], ALU.subtract).then_inc(query_lo, 1)
            with dve.Fori(1, EC // SLOTS) as i:
                for u in range(SLOTS):
                    onehots(SLOTS * i + u, u, SLOTS * (i - 1) + (u + 1))
            def qg_lo(t):
                for k in range(4 * t, 4 * t + 4):
                    u, g = k % 4 // 2, k % 2
                    dve.wait_ge(qg_hi_ready, k + 1)
                    TT(halves(QG[64:128, k, :]), ps[64 * g:64 * g + 64, 2 * u:2 * u + 2, 0:FH], halves(QG[0:64, k, :]),
                       ALU.subtract).then_inc(qg_lo_ready, 1)

            for c in range(EC // SLOTS * SLOTS, EC):
                onehots(c, c % SLOTS, c - SLOTS + 1)
            qg_lo(0)

            dve.wait_ge(onehots_used, EC)
            for t in range(NT):
                dve.tensor_scalar(halves(other[:, t, :]), ps[:, 4 + 2 * t:6 + 2 * t, 0:FH], 1.0 / PACK, -E / PACK / 2,
                                  ALU.mult, ALU.add).then_inc(vector_step, 1)
            ch.n += NT
            dve.wait_ge(vector_step, ch.n)
            ch.step(dve.tensor_scalar(other[:], other[:], ROUND, -ROUND, ALU.add, ALU.add))
            dve.tensor_scalar(A3[:, :, 1, :], other[:, :, 0:N], MID, None, ALU.add)
            for k in range(2):
                dve.tensor_scalar(A4i[:, :, 2 * k + 1, :], other[:, :, (k + 1) * N:(k + 2) * N], MID, None, ALU.add)
            for t in range(NT):
                for k in range(3):
                    lo = k * N
                    while lo < (k + 1) * N:
                        hi = min((k + 1) * N, (lo // FH + 1) * FH)
                        dst = A3[:, t, 0, lo - k * N:hi - k * N] if k == 0 else A4i[:, t, 2 * (k - 1), lo - k * N:hi - k * N]
                        ins = dve.scalar_tensor_tensor(out=dst, in0=other[:, t, lo:hi], scalar=-PACK,
                                                       in1=ps[:, 4 + 2 * t + lo // FH, lo % FH:lo % FH + hi - lo],
                                                       op0=ALU.mult, op1=ALU.add)
                        lo = hi
            ch.step(ins)
            ch.step(TT(rest[:], A4i[:, :, 0, :], A4i[:, :, 1, :], ALU.add))
            for a_, op in ((A4i[:, :, 2, :], ALU.add), (A4i[:, :, 3, :], ALU.add), (A3[:, :, 0, :], ALU.subtract)):
                ch.step(TT(rest[:], rest[:], a_, op))
            TT(A3[:, :, 2, :], rest[:], A3[:, :, 1, :], ALU.subtract).then_inc(counts_ready, 1)
            dve.wait_ge(x_in, 16)
            norm_stats(X)
            norm_shift(0)

            dve.wait_ge(degrees_ready, 1)
            ch.step(dve.tensor_scalar(deg3[:, 0:2, :], ps[:, 4, :].rearrange("p (r n) -> p r n", r=2), 1.0, None, ALU.max))
            ch.step(dve.tensor_scalar(deg3[:, 2, :], ps[:, 5, 0:N], 1.0, None, ALU.max))
            dve.tensor_scalar(deg4[:].rearrange("p (b r) n -> p b (r n)", b=2), ps[:, 6:8, :], 1.0, None,
                              ALU.max).then_inc(degrees_read, 1)
            dve.wait_ge(degrees_read, 1)
            qg_lo(1)

            with dve.Fori(0, 2) as i:
                T = 15 * i
                yt_root(T)
                h_lo(2 * i)
                for v in range(1, 4):
                    yt_relation(T + 3 * v, v % 2, deg3, v - 1, R3 * i + v)
                yt_root(T + 12)

                def hg_lo(pair):
                    dve.wait_ge(hg_hi_ready, 4 * i + (pair + 1))
                    r = 64 * (pair % 2)
                    TT(halves(HG[64:128, pair, :]), ps[r:r + 64, 2 * (pair // 2):2 * (pair // 2) + 2, 0:FH],
                       halves(HG[0:64, pair, :]), ALU.subtract).then_inc(hg_lo_ready, 1)

                hg_lo(0)
                hg_lo(1)

                def reduce(st):
                    f, b = st // B, st % B
                    dve.wait_ge(partial_sums_ready, (STEPS - 1) * i + (st + 1))
                    dve.tensor_reduce(qiT[:, f, b * NB:(b + 1) * NB], PR[:, st % PSLOTS, 0:1024].rearrange(
                        "p (n l) -> p n l", l=LH)[:, :, 0:LH // 2 if FOLDED[st] else LH],
                                      AX.X, ALU.add).then_inc(qi_ready, 1)

                def qi_lo(f):
                    dve.wait_ge(qi_hi_ready, 6 * i + (f + 1))
                    TT(YTl[:, 1, f, :], qiT[:, f, :], YTh[:, 1, f, :], ALU.subtract).then_inc(qi_lo_ready, 1)

                for st in range(STEPS):
                    f, b = st // B, st % B
                    if st in (1, 3):
                        hg_lo(2 + st // 2)
                    if st >= PSLOTS:
                        dve.wait_ge(qi_ready, STEPS * i + (st - PSLOTS + 1))
                    for u in range(ZU):
                        if u == 1 and st >= 2:
                            reduce(st - 2)
                        dve.wait_ge(sigmoid_ready, 2 * (ZU * STEPS * i + (ZU * st + u + 1)))
                        l0 = b * L + u * LH
                        TT(PR[:, st % PSLOTS, u * 1024:(u + 1) * 1024].rearrange("p (n l) -> p n l", l=LH),
                           ps[:, 4 + 2 * u:6 + 2 * u, :].rearrange("p b (n l) -> p (b n) l", l=LH),
                           qTf[:, f, l0:l0 + LH].unsqueeze(1).broadcast_to([P, NB, LH]), ALU.mult).then_inc(products_ready, 1)
                    if f > 0 and b == 3:
                        qi_lo(f - 1)
                dve.wait_ge(products_ready, ZU * STEPS * (i + 1))
                dve.tensor_reduce(qiT[:, KC - 1, (B - 1) * NB:B * NB], PR[:, (STEPS - 1) % PSLOTS, :].rearrange(
                    "p (u n l) -> p n u l", u=ZU, l=LH), AX.XY, ALU.add).then_inc(qi_ready, 1)
                reduce(STEPS - 2)
                qi_lo(KC - 1)
                for t in range(NT):
                    dve.wait_ge(tanh_ready, 2 * i + (t + 1))
                    TT(tq[:, t, :], tq[:, t, :], H[:, t, :], ALU.subtract).then_inc(diff_ready, 1)
                for t in range(NT):
                    dve.wait_ge(diff_ready, 2 * i + (t + 1))
                    dve.wait_ge(alpha_ready, 2 * i + (t + 1))
                    TT(tq[:, t, :], tq[:, t, :], alpha[:, t, :], ALU.mult).then_inc(alpha_diff_ready, 1)
                for t in range(NT):
                    dve.wait_ge(alpha_diff_ready, 2 * i + (t + 1))
                    TT(H[:, t, :], H[:, t, :], tq[:, t, :], ALU.add).then_inc(h_ready, 1)

            dve.wait_ge(h_ready, 10)
            ch.step(TT(X[:], X[:], H[:], ALU.add))
            norm_stats(X)
            norm_shift(1)

            def layer1(i):
                T = 15 * i + 30
                yt_root(T)
                h_lo(2 * i + 4)
                for v in range(1, 5):
                    if isinstance(i, int) and v == 2:
                        counts_of_all()
                    if isinstance(i, int) and v == 4:
                        attention_counts()
                    yt_relation(T + 3 * v, v % 2, deg4, v - 1, 2 * R3 + (R4 * i + v))

            def counts_of_all():
                ch.step(TT(cnt[:, 1, :, :], A4i[:, :, 0, :], A4i[:, :, 1, :], ALU.add))
                ch.step(TT(cnt[:, 1, :, :], cnt[:, 1, :, :], A4i[:, :, 2, :], ALU.add))
                ch.step(TT(cnt[:, 1, :, :], cnt[:, 1, :, :], A4i[:, :, 3, :], ALU.add))
                ch.step(dve.tensor_copy(cnt[:, 0, :, :], cnt[:, 1, :, :]))
                for t in range(NT):
                    ins = TT(cnt[:, 0, t, t * P:(t + 1) * P], cnt[:, 0, t, t * P:(t + 1) * P], ident[:], ALU.add)
                ins.then_inc(count_matrix_ready, 1)
                dve.wait_ge(count_matrix_ready, 1)

            def attention_counts():
                dve.wait_ge(count_matrix_transposed, 1)
                cT = ps[:, 7, :].rearrange("p (t n) -> p t n", t=NT)
                dve.tensor_scalar(noedge_d[:, 1, :, :], cT, 0.0, NEG, ALU.is_equal, ALU.mult)
                dve.tensor_scalar(noedge_s[:, 1, :, :], cnt[:, 1, :, :], 0.0, -NEG, ALU.is_equal, ALU.mult)
                dve.tensor_scalar(noedge_s[:, 0, :, :], cnt[:, 0, :, :], 0.0, -NEG, ALU.is_equal, ALU.mult)
                dve.tensor_copy(identb[:], ident[:])
                dve.tensor_scalar(AR[:], ident[0:64, 0:1].unsqueeze(2).broadcast_to([64, 2, N]), 0.0, None, ALU.mult)
                ch.step(dve.tensor_copy(looped[:], cT))
                for t in range(NT):
                    ins = TT(looped[:, t, t * P:(t + 1) * P], looped[:, t, t * P:(t + 1) * P], ident[:], ALU.add)
                ch.step(ins)
                ch.step(dve.tensor_scalar(noedge_d[:, 0, :, :], looped[:], 0.0, NEG, ALU.is_equal, ALU.mult))

            with dve.Fori(0, 2) as i:
                layer1(i)
            layer1(2)
            for t in range(NT):
                wait_out(dve, 11, t, 29)
                TT(halves(X[:, t, :]), halves(X[:, t, :]), two_banks(t), ALU.add).then_inc(residual_added, 1)
            dve.wait_ge(residual_added, 2)
            norm_stats(X)
            norm_shift(2)
            dve.wait_ge(vectors_in, 32)

            def proj_lo(q):
                for j in range(PTILE[q + 1] - PTILE[q]):
                    dve.wait_ge(p_hi_ready, PTILE[q] + j + 1)
                    TT(YTl[:, 0, 2 * j:2 * j + 2, :], tile3(j), YTh[:, 0, 2 * j:2 * j + 2, :],
                       ALU.subtract).then_inc(p_lo_ready, 1)

            def rows_hi_lo(rows, src, hn, done):
                ch.step(dve.tensor_copy(rows[0:hn], src))
                TT(rows[32:32 + hn], src, rows[0:hn], ALU.subtract).then_inc(done, 1)

            def gat(g, last=False):
                hn, c, w, nb, hv = head_views(g)
                o_s, o_b = GAT[g][2], GAT[g][4]
                hc = hn * c
                ch.step(dve.memset(hv[:, :, :, c:c + 1], 1.0))
                dve.wait_ge(g_h_copied, 2 * g + 2)
                tv = gtmp[:, 0:NT * hc].rearrange("p (t h c) -> p t h c", t=NT, h=hn)
                ch.step(TT(tv, hv[:, :, :, 0:c], av[:, o_s:o_s + hc].rearrange("p (h c) -> p h c", h=hn).unsqueeze(
                    1).broadcast_to([P, NT, hn, c]), ALU.mult))
                dve.tensor_reduce(small[:, 64:64 + NT * hn], gtmp[:, 0:NT * hc].rearrange("p (h c) -> p h c", c=c),
                                  AX.X, ALU.add)
                dve.wait_ge(g_dst_products, g + 1)
                dve.tensor_reduce(small[:, 80:80 + NT * hn], zb[:, 0, 0:NT * hc].rearrange("p (h c) -> p h c", c=c),
                                  AX.X, ALU.add).then_inc(g_parts_ready, 1)
                dve.wait_ge(g_parts_transposed, g + 1)
                rows_hi_lo(AR, ps[0:hn, 4, :].rearrange("p (k n) -> p k n", k=2), hn, g_part_rows_ready)
                for u, (t, h0, n) in enumerate(PIECES[g]):
                    dve.wait_ge(g_masked_ready, PBASE[g] + u + 1)
                    bank = masked_bank(g, t) + h0 // 2
                    srcs = ps[:, bank:bank + (n + 1) // 2, 0:min(512, n * N)]
                    if n > 1:
                        srcs = srcs.rearrange("p b (h n) -> p (b h) n", n=N)
                    dve.tensor_reduce(small[:, 96 + hn * t + h0:96 + hn * t + h0 + n], srcs, AX.X,
                                      ALU.max).then_inc(g_masked_read, 1)
                dve.wait_ge(g_masked_read, PBASE[g] + len(PIECES[g]))
                mx, ald = small[:, 96:96 + NT * hn], small[:, 80:80 + NT * hn]
                ch.step(TT(mx, mx, ald, ALU.add))
                dve.scalar_tensor_tensor(out=mx, in0=mx, scalar=SLOPE, in1=mx, op0=ALU.mult, op1=ALU.max).then_inc(g_max_ready, 1)
                pieces = range(len(PIECES[g]))

                def leaky(u):
                    zt, z_, _ = piece_views(g, u)
                    dve.wait_ge(g_leak_ready, PBASE[g] + u + 1)
                    TT(zt, zt, z_, ALU.max).then_inc(g_leaky_ready, 1)

                leaky(0)
                dve.wait_ge(g_max_transposed, g + 1)
                rows_hi_lo(MR, ps[0:hn, 0, 0:N], hn, g_max_rows_ready)
                leaky(1)
                for u in pieces:
                    if u >= 2:
                        leaky(u)
                    zt, _, m_ = piece_views(g, u)
                    dve.wait_ge(g_leaky_ready, PBASE[g] + u + 1)
                    dve.wait_ge(g_maxima_ready, PBASE[g] + u + 1)
                    TT(zt, zt, m_, ALU.subtract).then_inc(g_shifted_ready, 1)
                for u in pieces[len(pieces) // 2:]:
                    dve.wait_ge(g_exp_ready, PBASE[g] + u + 1)
                    z3, c3 = piece_counts(g, u)
                    TT(z3, z3, c3, ALU.mult).then_inc(g_weights_vector, 1)
                for t in range(NT):
                    dve.wait_ge(g_sums_ready, 2 * g + t + 1)
                    if c == F:
                        rd = small[:, 52 + t:53 + t]
                        ch.step(dve.tensor_scalar(rd, ps[:, 2 * t + 1, FH:FH + 1], 1e-16, None, ALU.add))
                        ch.step(dve.reciprocal(rd, rd))
                        dve.scalar_tensor_tensor(out=halves(X[:, t, :]), in0=two_banks(t), scalar=rd,
                                                 in1=halves(X[:, t, :]), op0=ALU.mult, op1=ALU.add).then_inc(result_ready, 1)
                        continue
                    per = max(1, hn // 2)
                    nbk = 1 if hn == 1 else 2
                    pv = ps[:, 2 * t:2 * t + nbk, 0:per * (c + 1)].rearrange("p b (h c) -> p b h c", h=per)
                    r_ = small[:, 52:52 + hn].rearrange("p (b h) -> p b h", b=nbk)
                    ch.step(dve.tensor_scalar(r_, pv[:, :, :, c], 1e-16, None, ALU.add))
                    ch.step(dve.reciprocal(r_, r_))
                    ch.step(TT(gout[:, t, 0:hc].rearrange("p (b h c) -> p b h c", b=nbk, h=per), pv[:, :, :, 0:c],
                               r_.unsqueeze(3).broadcast_to([P, nbk, per, c]), ALU.mult))
                    ch.step(TT(gout[:, t, 0:hc], gout[:, t, 0:hc], gb[:, o_b:o_b + hc], ALU.add))

            def relu_to_h(hc):
                for t in range(NT):
                    dve.tensor_scalar(H[:, t, 0:hc], gout[:, t, 0:hc], 0.0, None, ALU.max).then_inc(p_h_ready, 1)

            proj_lo(0)
            ch.step(dve.tensor_scalar(MR[:], ident[0:64, 0:1].broadcast_to([64, N]), 0.0, None, ALU.mult))
            gat(0)
            relu_to_h(256)
            proj_lo(1)
            for t in range(NT):
                ins = TT(X[:, t, :], X[:, t, :], gb[:, GB_M2:GB_M2 + F], ALU.add)
            ch.step(ins)
            gat(1)
            relu_to_h(256)
            proj_lo(2)
            for t in range(NT):
                dve.wait_ge(p_out_ready, 4 + t + 1)
                ch.step(TT(gout[:, t, 0:256], ps[:, 2 * t, 0:256], gb[:, GB_M1:GB_M1 + 256], ALU.add))
            relu_to_h(256)
            proj_lo(3)
            for t in range(NT):
                dve.wait_ge(p_out_ready, 6 + t + 1)
                ins = TT(halves(X[:, t, :]), halves(X[:, t, :]), two_banks(t), ALU.add)
            ch.step(ins)
            norm_stats(X)
            norm_shift(3)
            proj_lo(4)
            gat(2)
            dve.tensor_scalar(elu_t[:], gout[:], 0.0, None, ALU.min).then_inc(elu_min_ready, 2)
            ch.step(dve.tensor_scalar(H[:], gout[:], 0.0, None, ALU.max))
            dve.wait_ge(elu_exp_ready, 1)
            for t in range(NT):
                dve.scalar_tensor_tensor(out=H[:, t, :], in0=elu_t[:, t, :], scalar=-1.0, in1=H[:, t, :],
                                         op0=ALU.add, op1=ALU.add).then_inc(p_h_ready, 1)
            proj_lo(5)
            o_b = GAT[3][4]
            for t in range(NT):
                ins = TT(X[:, t, :], X[:, t, :], gb[:, o_b:o_b + F], ALU.add)
            ch.step(ins)
            gat(3)


def kernel(**inputs):
    import numpy as np
    import concourse.bacc as bacc
    from concourse.bass_utils import run_bass_kernel_spmd

    a = {k: np.asarray(v) for k, v in inputs.items()}

    def unit(w):
        return w.reshape(KC, P, F).transpose(1, 0, 2).reshape(P, 3, 2 * F)

    wg, wq = a["L0_gnn_Wg"], a["L0_gnn_Wq"]
    units = [unit(wg[:, F:].T)]
    for n in "12":
        units.append(unit(a["L0_gnn_W_root" + n]))
        units += [unit(w) for w in a["L0_gnn_W_rel" + n]]
        units += [unit(wg[:, :F].T), unit(wq[:, :F].T), unit(wq[:, F:].T)]
    for n in "123":
        units.append(unit(a["L1_gnn_root" + n]))
        units += [unit(w) for w in a["L1_gnn_W" + n]]
    small_w = [a["L2_gnn_" + n] for n in ("W1", "W2", "Wm1", "Wm2")]
    small_w = [w.reshape(-1, P, w.shape[1]).transpose(1, 0, 2).reshape(P, -1) for w in small_w]
    used = sum(w.shape[1] for w in small_w)
    small_w.append(np.zeros((P, KC * F - used), np.float32))
    units.append(np.concatenate(small_w, axis=1).reshape(P, 3, 2 * F))
    units += [unit(a["L3_gnn_W1"]), unit(a["L3_gnn_W2"])]

    consts = np.zeros((P, C_ALL), np.float32)
    consts[:, C_IOTA:C_IOTA + N] = np.arange(N)
    for col, m in ((C_P, P), (C_P64, 64), (C_P32, 32)):
        consts[:, col] = np.arange(P) % m

    arrays = {
        "x": a["x"],
        "edges": np.stack([a["src"], a["dst"], a["edge_type_3"], a["edge_type_4"]]).reshape(4, EC, P).transpose(2, 0, 1),
        "queries": a["L0_gnn_query_embs"].reshape(B * L, F).T.reshape(KC, P, B * L).transpose(1, 0, 2),
        "consts": consts,
        "biases": np.stack([np.concatenate([a[m], a[n]]) for m, n in (
            ("L0_gnn_b1", "L0_gnn_b2"), ("L0_gnn_bq", "L0_gnn_bq"), ("L1_gnn_b1", "L1_gnn_b2"), ("L1_gnn_b3", "L0_gnn_bg"))]),
        "gat_biases": np.concatenate([a[n] for n in ("L2_gnn_b1", "L2_gnn_b2", "L2_gnn_bm1", "L3_gnn_b1", "L3_gnn_b2",
                                                     "L2_gnn_bm2")]),
        "gat_vectors": np.concatenate([a[n].reshape(-1) for n in (
            "L2_gnn_a_src1", "L2_gnn_a_dst1", "L2_gnn_a_src2", "L2_gnn_a_dst2",
            "L3_gnn_a_src1", "L3_gnn_a_dst1", "L3_gnn_a_src2", "L3_gnn_a_dst2")]),
        "weights": np.stack(units),
    }
    nc = bacc.Bacc("TRN2", target_bir_lowering=False, num_devices=1)
    arrays = {n: np.ascontiguousarray(v) for n, v in arrays.items()}
    args = [nc.dram_tensor(n, v.shape, mybir.dt.from_np(v.dtype), kind="ExternalInput").ap() for n, v in arrays.items()]
    result = nc.dram_tensor("result", (N, F), F32, kind="ExternalOutput").ap()
    build(nc, *args, result)
    r = run_bass_kernel_spmd(nc, [arrays], core_ids=[0])
    return r.results[0]["result"]
```
